# Optimizing a Trainium2 kernel written in Bass

```python
import numpy as np
import jax
import jax.numpy as jnp

def _softmax(x, axis=-1):
    return jax.nn.softmax(x, axis=axis)

def _gelu(x):
    return jax.nn.gelu(x, approximate=True)

def _silu(x):
    return jax.nn.silu(x)

def _sigmoid(x):
    return jax.nn.sigmoid(x)

def _layernorm(x, axis=-1, eps=1e-05):
    m = jnp.mean(x, axis=axis, keepdims=True)
    v = jnp.var(x, axis=axis, keepdims=True)
    return (x - m) / jnp.sqrt(v + eps)

def _scatter_add(tgt, idx, src, axis=0):
    return tgt.at[idx].add(src)

def _segment_sum(src, seg, n):
    return jax.ops.segment_sum(src, seg, n)
kernel_name = 'mk_lm_tower_d1_tok_ids1024_r4_519e41'

def setup_inputs(seed: int=0):
    np.random.seed(seed)
    _w = jnp.asarray

    def _rec_inputs():
        import jax
        import jax.numpy as jnp
        _rk = jax.random.key(seed)
        x = jax.random.randint(jax.random.fold_in(_rk, 1), (8, 1024), 0, 64, jnp.int32)
        return x
    x = _rec_inputs()

    def _L0_tok_setup():
        import jax, jax.numpy as jnp
        import numpy as np
        N_FFT = 64
        HOP = 64
        NUM_FREQ = N_FFT // 2 + 1

        def _stft_mag(sig, window):
            L = sig.shape[1]
            pad = N_FFT // 2
            x = jnp.pad(sig, ((0, 0), (pad, pad)), mode='reflect')
            n_frames = 1 + L // HOP
            idx = jnp.arange(n_frames)[:, None] * HOP + jnp.arange(N_FFT)[None, :]
            frames = x[:, idx] * window
            spec = jnp.fft.rfft(frames, axis=-1)
            r, im = (spec.real, spec.imag)
            m2 = r * r + im * im
            mag = jnp.where(m2 == 0, 0.0, jnp.sqrt(jnp.where(m2 == 0, 1.0, m2)))
            return (mag, n_frames)

        def _linear_interp_last(feat, out_len):
            in_len = feat.shape[-1]
            coord = jnp.clip((jnp.arange(out_len) + 0.5) * (in_len / out_len) - 0.5, 0.0, in_len - 1.0)
            i0 = jnp.floor(coord).astype(jnp.int32)
            i1 = jnp.minimum(i0 + 1, in_len - 1)
            w = (coord - i0).astype(feat.dtype)
            return feat[..., i0] * (1.0 - w) + feat[..., i1] * w
        key = jax.random.key(seed)
        k0, k1, k2 = jax.random.split(key, 3)
        B, L, V, d_model = (2, 256, 64, 256)
        d_emb = int(d_model * 0.7)
        d_stft = d_model - d_emb
        input_ids = jax.random.randint(k0, (B, L), 0, V)
        emb_table = jax.random.normal(k1, (V, d_emb), jnp.float32) * 0.02
        proj_w = jax.random.normal(k2, (d_stft, V * NUM_FREQ), jnp.float32) * 0.02
        proj_b = jnp.zeros((d_stft,), jnp.float32)
        n = jnp.arange(N_FFT, dtype=jnp.float32)
        window = 0.5 * (1.0 - jnp.cos(2.0 * jnp.pi * n / N_FFT))
        return {'input_ids': input_ids, 'emb_table': emb_table, 'proj_w': proj_w, 'proj_b': proj_b, 'window': window}
    _L0_tok_all = _L0_tok_setup()
    _L0_tok_in = {k: v for k, v in _L0_tok_all.items() if k in ('emb_table', 'proj_w', 'proj_b', 'window')}
    del _L0_tok_all

    def _L0_attn_setup():
        import jax, jax.numpy as jnp
        import numpy as np
        import math
        N_HEADS = 16
        ROPE_BASE = 10000.0

        def build_rope_cache(seq_len, head_dim):
            theta = ROPE_BASE ** (-jnp.arange(0, head_dim, 2, dtype=jnp.float32) / head_dim)
            seq = jnp.arange(seq_len, dtype=jnp.float32)
            freqs = jnp.einsum('i,j->ij', seq, theta)
            return (jnp.sin(freqs), jnp.cos(freqs))

        def apply_rope(x, sin, cos):
            sin = sin[None, :, None, :]
            cos = cos[None, :, None, :]
            x1, x2 = (x[..., ::2], x[..., 1::2])
            return jnp.concatenate([x1 * cos - x2 * sin, x1 * sin + x2 * cos], axis=-1)
        key = jax.random.key(seed)
        ks = jax.random.split(key, 6)
        B, T, C = (2, 512, 256)
        s = 1.0 / math.sqrt(C)
        return {'x': jax.random.normal(ks[0], (B, T, C), dtype=jnp.float32), 'Wq': jax.random.normal(ks[1], (C, C), dtype=jnp.float32) * s, 'bq': jnp.zeros((C,), dtype=jnp.float32), 'Wk': jax.random.normal(ks[2], (C, C), dtype=jnp.float32) * s, 'bk': jnp.zeros((C,), dtype=jnp.float32), 'Wv': jax.random.normal(ks[3], (C, C), dtype=jnp.float32) * s, 'bv': jnp.zeros((C,), dtype=jnp.float32), 'Wo': jax.random.normal(ks[4], (C, C), dtype=jnp.float32) * s, 'bo': jnp.zeros((C,), dtype=jnp.float32)}
    _L0_attn_all = _L0_attn_setup()
    _L0_attn_in = {k: v for k, v in _L0_attn_all.items() if k in ('Wq', 'bq', 'Wk', 'bk', 'Wv', 'bv', 'Wo', 'bo')}
    del _L0_attn_all

    def _L0_ffn_setup():
        import math
        import jax, jax.numpy as jnp
        import numpy as np
        D_MODEL = 256
        D_HIDDEN = 512
        N_EXPERTS = 8
        TOP_K = 2
        CAPACITY_FACTOR = 1.25

        def _moe_forward(x, w_router, w_gate, w_down):
            B, T, D = x.shape
            N = B * T
            xf = x.reshape(N, D)
            logits = xf.astype(jnp.float32) @ w_router.T
            gates = jax.nn.softmax(logits, axis=-1)
            topk_gates, topk_idx = jax.lax.top_k(gates, TOP_K)
            expert_mask = jax.nn.one_hot(topk_idx, N_EXPERTS, dtype=jnp.int32).sum(axis=1)
            capacity = math.ceil(N / N_EXPERTS * CAPACITY_FACTOR)
            position_in_expert = jnp.cumsum(expert_mask, axis=0) - 1
            expert_mask = expert_mask * (position_in_expert < capacity)
            keep = jnp.take_along_axis(expert_mask, topk_idx, axis=1) > 0
            topk_gates = topk_gates * keep
            topk_gates = topk_gates / (topk_gates.sum(axis=-1, keepdims=True) + 1e-06)
            hidden = jax.nn.silu(xf @ w_gate.T)
            combine = (topk_gates[:, :, None] * jax.nn.one_hot(topk_idx, N_EXPERTS, dtype=topk_gates.dtype)).sum(axis=1)
            y = jnp.zeros((N, D), dtype=x.dtype)
            for e in range(N_EXPERTS):
                y = y + combine[:, e:e + 1] * (hidden @ w_down[e].T)
            return y.reshape(B, T, D)
        key = jax.random.key(seed)
        k0, k1, k2, k3 = jax.random.split(key, 4)
        B, T = (2, 512)
        x = jax.random.normal(k0, (B, T, D_MODEL), dtype=jnp.float32)
        w_router = jax.random.normal(k1, (N_EXPERTS, D_MODEL), dtype=jnp.float32) * 0.02
        w_gate = jax.random.normal(k2, (D_HIDDEN, D_MODEL), dtype=jnp.float32) * 0.02
        w_down = jax.random.normal(k3, (N_EXPERTS, D_MODEL, D_HIDDEN), dtype=jnp.float32) * 0.02
        return {'x': x, 'w_router': w_router, 'w_gate': w_gate, 'w_down': w_down}
    _L0_ffn_all = _L0_ffn_setup()
    _L0_ffn_in = {k: v for k, v in _L0_ffn_all.items() if k in ('w_router', 'w_gate', 'w_down')}
    del _L0_ffn_all
    return {'x': x, 'L0_tok_emb_table': _L0_tok_in['emb_table'], 'L0_tok_proj_w': _L0_tok_in['proj_w'], 'L0_tok_proj_b': _L0_tok_in['proj_b'], 'L0_tok_window': _L0_tok_in['window'], 'L0_attn_Wq': _L0_attn_in['Wq'], 'L0_attn_bq': _L0_attn_in['bq'], 'L0_attn_Wk': _L0_attn_in['Wk'], 'L0_attn_bk': _L0_attn_in['bk'], 'L0_attn_Wv': _L0_attn_in['Wv'], 'L0_attn_bv': _L0_attn_in['bv'], 'L0_attn_Wo': _L0_attn_in['Wo'], 'L0_attn_bo': _L0_attn_in['bo'], 'L0_ffn_w_router': _L0_ffn_in['w_router'], 'L0_ffn_w_gate': _L0_ffn_in['w_gate'], 'L0_ffn_w_down': _L0_ffn_in['w_down']}

def reference(x, L0_tok_emb_table, L0_tok_proj_w, L0_tok_proj_b, L0_tok_window, L0_attn_Wq, L0_attn_bq, L0_attn_Wk, L0_attn_bk, L0_attn_Wv, L0_attn_bv, L0_attn_Wo, L0_attn_bo, L0_ffn_w_router, L0_ffn_w_gate, L0_ffn_w_down):
    import jax
    import jax.numpy as jnp

    def _L0_tok_ref(input_ids, emb_table, proj_w, proj_b, window):
        import jax, jax.numpy as jnp
        import numpy as np
        N_FFT = 64
        HOP = 64
        NUM_FREQ = N_FFT // 2 + 1

        def _stft_mag(sig, window):
            L = sig.shape[1]
            pad = N_FFT // 2
            x = jnp.pad(sig, ((0, 0), (pad, pad)), mode='reflect')
            n_frames = 1 + L // HOP
            idx = jnp.arange(n_frames)[:, None] * HOP + jnp.arange(N_FFT)[None, :]
            frames = x[:, idx] * window
            spec = jnp.fft.rfft(frames, axis=-1)
            r, im = (spec.real, spec.imag)
            m2 = r * r + im * im
            mag = jnp.where(m2 == 0, 0.0, jnp.sqrt(jnp.where(m2 == 0, 1.0, m2)))
            return (mag, n_frames)

        def _linear_interp_last(feat, out_len):
            in_len = feat.shape[-1]
            coord = jnp.clip((jnp.arange(out_len) + 0.5) * (in_len / out_len) - 0.5, 0.0, in_len - 1.0)
            i0 = jnp.floor(coord).astype(jnp.int32)
            i1 = jnp.minimum(i0 + 1, in_len - 1)
            w = (coord - i0).astype(feat.dtype)
            return feat[..., i0] * (1.0 - w) + feat[..., i1] * w
        B, L = input_ids.shape
        V = emb_table.shape[0]
        word_embeds = emb_table[input_ids]
        sig = jax.nn.one_hot(input_ids, V, dtype=jnp.float32)
        sig = jnp.transpose(sig, (0, 2, 1)).reshape(B * V, L)
        mag, T = _stft_mag(sig, window)
        feat = mag.reshape(B, V, T, NUM_FREQ).transpose(0, 3, 1, 2)
        feat = feat.reshape(B, NUM_FREQ * V, T)
        up = _linear_interp_last(feat, L)
        stft_feat = jnp.transpose(up, (0, 2, 1))
        stft_enc = stft_feat @ proj_w.T + proj_b
        return jnp.concatenate([word_embeds, stft_enc], axis=-1)

    def _L0_attn_ref(x, Wq, bq, Wk, bk, Wv, bv, Wo, bo):
        import jax, jax.numpy as jnp
        import numpy as np
        import math
        N_HEADS = 16
        ROPE_BASE = 10000.0

        def build_rope_cache(seq_len, head_dim):
            theta = ROPE_BASE ** (-jnp.arange(0, head_dim, 2, dtype=jnp.float32) / head_dim)
            seq = jnp.arange(seq_len, dtype=jnp.float32)
            freqs = jnp.einsum('i,j->ij', seq, theta)
            return (jnp.sin(freqs), jnp.cos(freqs))

        def apply_rope(x, sin, cos):
            sin = sin[None, :, None, :]
            cos = cos[None, :, None, :]
            x1, x2 = (x[..., ::2], x[..., 1::2])
            return jnp.concatenate([x1 * cos - x2 * sin, x1 * sin + x2 * cos], axis=-1)
        B, T, C = x.shape
        H = N_HEADS
        D = C // H
        q = (x @ Wq.T + bq).reshape(B, T, H, D)
        k = (x @ Wk.T + bk).reshape(B, T, H, D)
        v = (x @ Wv.T + bv).reshape(B, T, H, D)
        sin, cos = build_rope_cache(T, D)
        q = apply_rope(q, sin, cos)
        k = apply_rope(k, sin, cos)
        scores = jnp.einsum('bqhd,bkhd->bhqk', q, k) / math.sqrt(D)
        causal = jnp.tril(jnp.ones((T, T), dtype=bool))
        scores = jnp.where(causal[None, None], scores, -jnp.inf)
        probs = jax.nn.softmax(scores, axis=-1)
        out = jnp.einsum('bhqk,bkhd->bqhd', probs, v).reshape(B, T, C)
        return out @ Wo.T + bo

    def _L0_ffn_ref(x, w_router, w_gate, w_down):
        import math
        import jax, jax.numpy as jnp
        import numpy as np
        D_MODEL = 256
        D_HIDDEN = 512
        N_EXPERTS = 8
        TOP_K = 2
        CAPACITY_FACTOR = 1.25

        def _moe_forward(x, w_router, w_gate, w_down):
            B, T, D = x.shape
            N = B * T
            xf = x.reshape(N, D)
            logits = xf.astype(jnp.float32) @ w_router.T
            gates = jax.nn.softmax(logits, axis=-1)
            topk_gates, topk_idx = jax.lax.top_k(gates, TOP_K)
            expert_mask = jax.nn.one_hot(topk_idx, N_EXPERTS, dtype=jnp.int32).sum(axis=1)
            capacity = math.ceil(N / N_EXPERTS * CAPACITY_FACTOR)
            position_in_expert = jnp.cumsum(expert_mask, axis=0) - 1
            expert_mask = expert_mask * (position_in_expert < capacity)
            keep = jnp.take_along_axis(expert_mask, topk_idx, axis=1) > 0
            topk_gates = topk_gates * keep
            topk_gates = topk_gates / (topk_gates.sum(axis=-1, keepdims=True) + 1e-06)
            hidden = jax.nn.silu(xf @ w_gate.T)
            combine = (topk_gates[:, :, None] * jax.nn.one_hot(topk_idx, N_EXPERTS, dtype=topk_gates.dtype)).sum(axis=1)
            y = jnp.zeros((N, D), dtype=x.dtype)
            for e in range(N_EXPERTS):
                y = y + combine[:, e:e + 1] * (hidden @ w_down[e].T)
            return y.reshape(B, T, D)
        return _moe_forward(x, w_router, w_gate, w_down)
    h = _L0_tok_ref(x, L0_tok_emb_table, L0_tok_proj_w, L0_tok_proj_b, L0_tok_window)
    h = h + _L0_attn_ref(_layernorm(h, axis=-1), L0_attn_Wq, L0_attn_bq, L0_attn_Wk, L0_attn_bk, L0_attn_Wv, L0_attn_bv, L0_attn_Wo, L0_attn_bo)
    h = h + _L0_ffn_ref(_layernorm(h, axis=-1), L0_ffn_w_router, L0_ffn_w_gate, L0_ffn_w_down)
    return h

_drawn_inputs = setup_inputs


def setup_inputs(seed=0):
    import zlib

    import numpy as np

    out = dict(_drawn_inputs(seed))
    spreads = {'L0_tok_proj_b': (0.0, 0.1),
     'L0_attn_bq': (0.0, 0.39),
     'L0_attn_bk': (0.0, 0.584),
     'L0_attn_bv': (0.0, 0.1),
     'L0_attn_bo': (0.0, 0.1)}
    factors = {}
    for name, (base, spread) in spreads.items():
        noise = np.random.default_rng([zlib.crc32(name.encode()), seed]).standard_normal(out[name].shape)
        drawn = base * np.exp(spread * noise) if base else spread * noise
        out[name] = jnp.asarray(drawn.astype(out[name].dtype))
    for name, factor in factors.items():
        out[name] = (out[name] * factor).astype(out[name].dtype)
    return out
```

```python
import concourse.bass as bass
from concourse import mybir
from contextlib import ExitStack

F32 = mybir.dt.float32
BF16 = mybir.dt.bfloat16
I32 = mybir.dt.int32
U32 = mybir.dt.uint32
ALU = mybir.AluOpType
ACT = mybir.ActivationFunctionType
AX = mybir.AxisListType

B, T, V, D = 8, 1024, 64, 256
P = 128
NT = T // P
NFFT, NFRAME, NFREQ = 64, 17, 33
DEMB = 179
DST = D - DEMB
BF = B * NFRAME
NH, HD, HALF = 16, 16, 8
GH, NG = 4, 4
NE, HID, CAP = 8, 512, 1280
NTOK = B * T
NTILE = NTOK // P
NSLOT = NE * CAP
SCALE = HD ** -0.5
EPS = 1e-5
STACK = 6 * HD
VW = 32


def piece_range(half, j):
    start = max(512 * half, P * j)
    return start, 512 * (half + 1) - start


HEAD_TILES = [
    [(0, 0, 0), (0, 1, 512), (0, 3, 896)],
    [(0, 2, 0), (1, 6, 256), (1, 0, 512)],
    [(1, 1, 0), (1, 2, 512)],
    [(1, 3, 0), (1, 4, 512)],
    [(1, 5, 0), (1, 7, 384)],
]
PV_ORDER = [
    [[(0, 0, 0), (0, 1, 512), (0, 3, 896)], []],
    [[(0, 2, 0)], [(1, 0, 512), (1, 6, 256)]],
    [[], [(1, 1, 0), (1, 2, 512)]],
    [[], [(1, 3, 0), (1, 4, 512)]],
    [[], [(1, 5, 0), (1, 7, 384)]],
]
NSTEP = len(HEAD_TILES)
STEPS = NG * NSTEP
TILES_OF_STEP = [4, 4, 4, 4, 2]
TILES_OF_GROUP = sum(TILES_OF_STEP)


def max_banks():
    out = []
    for i in range(NT):
        w = min(512, P * (i + 1))
        per = min(GH, 512 // w)
        for h in range(0, GH, per):
            out.append((i, 0, w, list(range(h, h + per)), 0))
    for i in range(4, NT):
        w = P * (i + 1) - 512
        per = min(GH, 512 // w)
        for h in range(0, GH, per):
            out.append((i, 512, w, list(range(h, h + per)), 1))
    return out


MAXB = max_banks()


def max_quota(tile_no):
    if tile_no < 3:
        return 0
    return min(len(MAXB), -(-(tile_no - 2) * len(MAXB) // 11))


def ring_order():
    r = [("emb", k) for k in range(4)] + [("xT", k) for k in range(4)]
    r += [("qk", k) for k in range(8)] + [("v", k) for k in range(4)]
    r += [("max", 0, m) for m in range(len(MAXB))] + [("mT", 0)]
    n = 0
    for s in range(STEPS + 2):
        g, t = divmod(s, NSTEP)
        if s < STEPS:
            if t == 0:
                n = 0
            for _ in range(TILES_OF_STEP[t]):
                if g + 1 < NG:
                    r += [("max", g + 1, m) for m in range(max_quota(n - 1) if n else 0, max_quota(n))]
                n += 1
            if t == NSTEP - 2 and g + 1 < NG:
                r.append(("mT", g + 1))
        for half in range(2):
            if turn_step(s, half) is not None:
                r.append(("turn", turn_step(s, half), half))
    r += [("aT", k) for k in range(4)] + [("wo", k) for k in range(4)]
    r += [("x2T", k) for k in range(4)] + [("logit", 0)]
    return r


def turn_step(s, half):
    s0 = s - (3 if half == 0 else 6)
    if s0 >= 0 and s0 % NSTEP == 0 and s0 // NSTEP < NG:
        return s0 // NSTEP
    return None


RING = ring_order()
RING_AT = {u: n for n, u in enumerate(RING)}
ACT_USES = ("emb", "xT", "qk", "aT", "x2T")


def by_act(u):
    return u[0] in ACT_USES


N_RING = len(RING)
N_RING_ACT = sum(by_act(u) for u in RING)
N_RING_DVE = N_RING - N_RING_ACT
NB = 3


def freed_before(n):
    a = sum(by_act(u) for u in RING[:n])
    return a, n - a


def build(nc, ins, out):
    (x_frames, x_tok, emb, pw, pb, window, wq, bq, wk, bk, wv, bv, wo, bo, wr, wg, wd,
     c_dft, c_interp, c_rope, c_ident, c_mask, c_iota) = ins
    top = ExitStack()
    with top:
        def dram(name, shape, dt):
            return nc.dram_tensor(name, shape, dt, kind="Internal").ap()

        scratch = {
            "parts": dram("parts", [2, 3, NH, HD, T], BF16),
            "h2": dram("h2", [NTOK, D], F32),
            "xn2": dram("xn2", [NTOK, D], F32),
            "yslot": dram("yslot", [NSLOT + P, D], F32),
        }
        keep = {}
        for name, shape, dt in (("zcat", [P, B, DST], F32), ("logits", [P, NTILE, NE], F32),
                                ("ident", [P, P], F32), ("b16", [P, 5, P], BF16),
                                ("iota", [P, V + 2 + NE + P], F32)):
            keep[name] = top.enter_context(nc.sbuf_tensor(name, shape, dt))
        features(nc, scratch, keep, x_frames, pw, window, c_dft, c_ident, c_mask, c_iota)
        attention(nc, scratch, keep, x_tok, emb, pb, wq, bq, wk, bk, wv, bv, wo, bo, wr, c_interp, c_rope, c_iota)
        experts(nc, scratch, keep, wg, wd, c_iota, out)


def wait_for(eng, sem, value):
    if not isinstance(value, int) or value > 0:
        eng.wait_ge(sem, value)


def features(nc, scratch, keep, x_frames, pw, window, c_dft, c_ident, c_mask, c_iota):
    ctx = ExitStack()
    with ctx:
        def sb(name, shape, dt=F32):
            return ctx.enter_context(nc.sbuf_tensor(name, shape, dt))

        def sem(name):
            return ctx.enter_context(nc.semaphore(name))

        PER = 7
        groups = [(a, min(PER, BF - a)) for a in range(0, BF, PER)]
        W = 2 * NFREQ
        xf_i = sb("xf_i", [NFFT, BF], I32)
        xf = sb("xf", [NFFT, BF])
        iota = keep["iota"][:, 0:V]
        win = sb("win", [NFFT, 1])
        dft = sb("dft", [NFFT, W])
        dftw = sb("dftw", [NFFT, W])
        onehot = sb("onehot", [NFFT, 2, PER, V])
        square = sb("square", [V, 2, PER, W])
        power = sb("power", [V, BF, NFREQ])
        mag = sb("mag", [V, BF, NFREQ])
        pw_sb = sb("pw_sb", [V, NFREQ, DST])
        zT = sb("zT", [DST, BF])
        zero = sb("zero", [P, D])
        masks = sb("masks", [P, 5, P])
        bank = [ctx.enter_context(nc.psum_tensor(f"f_bank{i}", [P, 512], F32)) for i in range(2)]
        zbank = ctx.enter_context(nc.psum_tensor("zbank", [P, 512], F32))
        tbank = [ctx.enter_context(nc.psum_tensor(f"tbank{i}", [P, 512], F32)) for i in range(2)]
        loaded, consts_in, masks_kept = sem("loaded"), sem("consts_in"), sem("masks_kept")
        zero_set, zero_out = sem("zero_set"), sem("zero_out")
        ids_float, window_on = sem("ids_float"), sem("window_on")
        onehot_made, spectrum_done = sem("onehot_made"), sem("spectrum_done")
        squared, powered, mag_done = sem("squared"), sem("powered"), sem("mag_done")
        z_done, z_copied, z_turned, z_kept = sem("z_done"), sem("z_copied"), sem("z_turned"), sem("z_kept")

        with nc.Block() as block:
            @block.sync
            def _(sp):
                for dst, src in ((xf_i[:], x_frames), (keep["iota"][:], c_iota), (win[:], window),
                                 (dft[:], c_dft), (keep["ident"][:], c_ident)):
                    sp.dma_start(dst, src).then_inc(loaded, 16)
                sp.dma_start(masks[:], c_mask).then_inc(consts_in, 16)
                sp.dma_start(pw_sb[:], pw).then_inc(consts_in, 16)
                sp.wait_ge(zero_set, 1)
                sp.dma_start(scratch["yslot"][NSLOT:NSLOT + P, :], zero[:]).then_inc(zero_out, 16)
                sp.wait_ge(zero_out, 16)
                sp.wait_ge(consts_in, 32)

            @block.vector
            def _(dve):
                nc.vector.memset(zero[:], 0.0).then_inc(zero_set, 1)
                dve.wait_ge(loaded, 80)
                nc.vector.tensor_copy(xf[:], xf_i[:]).then_inc(ids_float, 1)
                nc.vector.tensor_scalar(dftw[:], dft[:], win[:, 0:1], None, ALU.mult).then_inc(window_on, 1)
                dve.wait_ge(ids_float, 1)
                for n in range(len(groups) + 1):
                    if n < len(groups):
                        a, k = groups[n]
                        if n >= 2:
                            dve.wait_ge(spectrum_done, n - 1)
                        nc.vector.tensor_tensor(
                            onehot[:, n % 2, 0:k, :],
                            xf[:, a:a + k].unsqueeze(2).to_broadcast([NFFT, k, V]),
                            iota[0:NFFT].unsqueeze(1).to_broadcast([NFFT, k, V]),
                            ALU.is_equal).then_inc(onehot_made, 1)
                    if n >= 1:
                        a, k = groups[n - 1]
                        dve.wait_ge(squared, n)
                        nc.vector.tensor_tensor(power[:, a:a + k, :], square[:, (n - 1) % 2, 0:k, 0:NFREQ],
                                                square[:, (n - 1) % 2, 0:k, NFREQ:W], ALU.add).then_inc(powered, 1)
                dve.wait_ge(consts_in, 32)
                nc.vector.tensor_copy(keep["b16"][:], masks[:]).then_inc(masks_kept, 1)
                dve.wait_ge(z_done, 1)
                nc.vector.tensor_copy(zT[:], zbank[0:DST, 0:BF]).then_inc(z_copied, 1)
                for b in range(B):
                    dve.wait_ge(z_turned, b + 1)
                    nc.vector.tensor_copy(keep["zcat"][V:V + NFRAME, b, :],
                                          tbank[b % 2][0:NFRAME, 0:DST]).then_inc(z_kept, 1)

            @block.scalar
            def _(act):
                for n, (a, k) in enumerate(groups):
                    act.wait_ge(spectrum_done, n + 1)
                    if n >= 2:
                        act.wait_ge(powered, n - 1)
                    nc.scalar.activation(square[:, n % 2, 0:k, :],
                                         bank[n % 2][0:V, 0:k * W].rearrange("p (k w) -> p k w", w=W),
                                         ACT.Square).then_inc(squared, 1)
                act.wait_ge(powered, len(groups))
                nc.scalar.activation(mag[:], power[:], ACT.Sqrt).then_inc(mag_done, 1)

            @block.tensor
            def _(pe):
                pe.wait_ge(window_on, 1)
                for n, (a, k) in enumerate(groups):
                    pe.wait_ge(onehot_made, n + 1)
                    if n >= 2:
                        pe.wait_ge(squared, n - 1)
                    for i in range(k):
                        mm = nc.tensor.matmul(bank[n % 2][0:V, i * W:(i + 1) * W], onehot[:, n % 2, i, :],
                                              dftw[:], start=True, stop=True)
                    mm.then_inc(spectrum_done, 1)
                pe.wait_ge(mag_done, 1)
                pe.wait_ge(consts_in, 32)
                for f in range(NFREQ):
                    mm = nc.tensor.matmul(zbank[0:DST, 0:BF], pw_sb[:, f, :], mag[:, :, f],
                                          start=(f == 0), stop=(f == NFREQ - 1))
                mm.then_inc(z_done, 1)
                pe.wait_ge(z_copied, 1)
                for b in range(B):
                    if b >= 2:
                        pe.wait_ge(z_kept, b - 1)
                    nc.tensor.transpose(tbank[b % 2][0:NFRAME, 0:DST], zT[:, b * NFRAME:(b + 1) * NFRAME],
                                        keep["ident"][0:DST, 0:DST]).then_inc(z_turned, 1)


def attention(nc, scratch, keep, x_tok, emb, pb, wq, bq, wk, bk, wv, bv, wo, bo, wr, c_interp, c_rope, c_iota):
    ctx = ExitStack()
    with ctx:
        def sb(name, shape, dt=F32):
            return ctx.enter_context(nc.sbuf_tensor(name, shape, dt))

        def sem(name):
            return ctx.enter_context(nc.semaphore(name))

        def psum(name, shape):
            return ctx.enter_context(nc.psum_tensor(name, shape, F32))

        ident = keep["ident"]
        identb, mask_q, mask_k = keep["b16"][:, 0, :], keep["b16"][:, 1, :], keep["b16"][:, 2, :]
        KE = V + NFRAME + 1
        ids = sb("ids", [V, T], I32)
        e_lhs = sb("e_lhs", [KE, T])
        e_rhs = sb("e_rhs", [KE, D])
        iota_p = keep["iota"][:, V:V + 1]
        rope = sb("rope", [P, 2, T])
        wq_sb, wk_sb, wv_sb, wo_sb = (sb(n, [P, 2, D]) for n in ("wq_sb", "wk_sb", "wv_sb", "wo_sb"))
        wr_sb = sb("wr_sb", [P, 2, NE])
        qk_bias = sb("qk_bias", [P, 2, 2])
        bv_sb, bo_sb = sb("bv_sb", [P, D]), sb("bo_sb", [P, D])
        h = sb("h", [P, NT, D])
        hb = sb("hb", [P, NT, D])
        xn = sb("xn", [P, NT, D])
        stats = sb("stats", [P, NT, 6])
        mv = sb("mv", [P, NT, 2])
        var, logv, guess, newton, rstd = (sb(n, [P, NT]) for n in ("var", "logv", "guess", "newton", "rstd"))
        xnT = sb("xnT", [P, 2, T])
        qk = sb("qk", [P, 2, 2, T])
        rot = sb("rot", [P, 2, 2, T // 2])
        turned = sb("turned", [P, 2, 2, T // 2])
        parts = sb("parts_sb", [P, 2, 3, 2, T // 2], BF16)
        qs = sb("qs", [P, 2, GH, T], BF16)
        ks = sb("ks", [P, 2, GH, T], BF16)
        vals = sb("vals", [P, NT, NH, VW])
        probs = sb("probs", [P, 2, GH, T])
        mx = sb("mx", [P, NT, GH])
        mx2 = sb("mx2", [P, NT // 2, GH])
        mparts = sb("mparts", [P, 2, GH, NT], BF16)
        mrest = sb("mrest", [P, NT, GH])
        mT = sb("mT", [2 * GH * NT, P], BF16)
        sums = sb("sums", [P, 2, 512])
        rec = sb("rec", [P, 4, GH, 1])
        attn = sb("attn", [P, NT, D])
        ring = [psum(f"ring{i}", [P, 512]) for i in range(NB)]
        st = [psum(f"st{i}", [P, T]) for i in range(2)]
        pv = psum("pv", [P, 512])

        weights_in, ids_in, set_once = sem("weights_in"), sem("ids_in"), sem("set_once")
        e_ready = sem("e_ready")
        ring_filled, ring_freed_act, ring_freed_dve = sem("ring_filled"), sem("ring_freed_act"), sem("ring_freed_dve")
        stats_done, aggr_done, rstd_done, normed = sem("stats_done"), sem("aggr_done"), sem("rstd_done"), sem("normed")
        hb_done, var_done, guess_done = sem("hb_done"), sem("var_done"), sem("guess_done")
        rot_q, rot_k = sem("rot_q"), sem("rot_k")
        parts_out = sem("parts_out")
        stack_in = sem("stack_in")
        st_done, exp_done, pv_done, pv_half, pv_freed = (sem("st_done"), sem("exp_done"), sem("pv_done"),
                                                         sem("pv_half"), sem("pv_freed"))
        max_joined, m_hi, m_diff, m_parts, m_rows = (
            sem("max_joined"), sem("m_hi"), sem("m_diff"), sem("m_parts"), sem("m_rows"))
        rec_done, rows_out = sem("rec_done"), sem("rows_out")

        ROT = 10
        LOADS = 12
        block = ctx.enter_context(nc.Block())

        def take(pe, b, use):
            n = RING_AT[use]
            if n >= NB:
                last = RING[n - NB]
                a, v = freed_before(n - NB + 1)
                if by_act(last):
                    wait_for(pe, ring_freed_act, b * N_RING_ACT + a)
                else:
                    wait_for(pe, ring_freed_dve, b * N_RING_DVE + v)
            elif n == 0:
                wait_for(pe, ring_freed_act, b * N_RING_ACT)
                wait_for(pe, ring_freed_dve, b * N_RING_DVE)
            return ring[n % NB]

        def filled(eng, b, use):
            n = RING_AT[use]
            eng.wait_ge(ring_filled, b * N_RING + n + 1)
            return ring[n % NB]

        def rotary(eng, ops, b, i, rot_sem):
            for c in range(2):
                cols = slice(c * 512, (c + 1) * 512)
                a, _ = freed_before(RING_AT[("qk", 4 * i + 2 * c + 1)] + 1)
                wait_for(eng, ring_freed_act, b * N_RING_ACT + a)
                x1, x2 = qk[:, i, 0, cols], qk[:, i, 1, cols]
                cos, sin = rope[:, 0, cols], rope[:, 1, cols]
                t1, t2 = rot[:, i, 0, :], rot[:, i, 1, :]
                n = [2 * ROT * b + ROT * c]

                def chain(ins):
                    n[0] += 1
                    ins.then_inc(rot_sem, 1)
                    return n[0]
                for o, (ca, cb, op) in enumerate(((cos, sin, ALU.subtract), (sin, cos, ALU.add))):
                    if o:
                        eng.wait_ge(rot_sem, at)
                    chain(ops.tensor_tensor(t1, x1, ca, ALU.mult))
                    at = chain(ops.tensor_tensor(t2, x2, cb, ALU.mult))
                    eng.wait_ge(rot_sem, at)
                    at = chain(ops.tensor_tensor(turned[:, i, o, :], t1, t2, op))
                eng.wait_ge(rot_sem, at)
                if c == 0:
                    wait_for(eng, parts_out, 16 * 24 * b)
                else:
                    eng.wait_ge(parts_out, 16 * (24 * b + 12))
                eng.nop(nofuse=True)
                at = chain(ops.tensor_copy(parts[:, i, 0], turned[:, i]))
                eng.wait_ge(rot_sem, at)
                at = chain(ops.tensor_tensor(rot[:, i], turned[:, i], parts[:, i, 0], ALU.subtract))
                eng.wait_ge(rot_sem, at)
                eng.nop(nofuse=True)
                at = chain(ops.tensor_copy(parts[:, i, 1], rot[:, i]))
                eng.wait_ge(rot_sem, at)
                at = chain(ops.tensor_tensor(parts[:, i, 2], rot[:, i], parts[:, i, 1], ALU.subtract))
                eng.wait_ge(rot_sem, at)

        @block.sync
        def _(sp):
            w_rows = [(w_sb[:], w) for w_sb, w in ((wq_sb, wq), (wk_sb, wk), (wv_sb, wv), (wo_sb, wo), (wr_sb, wr))]
            w_rows += [(qk_bias[:, 0, :], bq), (qk_bias[:, 1, :], bk), (rope[:], c_rope),
                       (bv_sb[:], bv.to_broadcast([P, D])), (bo_sb[:], bo.to_broadcast([P, D])),
                       (e_lhs[V:KE, :], c_interp), (e_rhs[0:V, 0:DEMB], emb),
                       (e_rhs[KE - 1:KE, DEMB:D], pb)]
            sp.wait_ge(set_once, 1)
            for dst, src in w_rows:
                sp.dma_start(dst, src).then_inc(weights_in, 16)
            def sequence(b):
                wait_for(sp, e_ready, 2 * b)
                sp.dma_start(ids[:], x_tok[bass.ds(b, 1), :].to_broadcast([V, T])).then_inc(ids_in, 16)
                for c in range(2):
                    for i, made in ((0, rot_q), (1, rot_k)):
                        sp.wait_ge(made, 2 * ROT * b + ROT * (c + 1))
                        for term in range(3):
                            for half in range(2):
                                dst = scratch["parts"][i, term, :, half * HALF:(half + 1) * HALF, c * 512:(c + 1) * 512]
                                sp.dma_start(dst, parts[:, i, term, half, :]).then_inc(parts_out, 16)
                    sp.wait_ge(parts_out, 16 * (24 * b + 12 * (c + 1)))
                    sp.nop(nofuse=True)

                def stacks(g):
                    for i, (buf, order) in enumerate(((qs, (0, 0, 1, 1, 0, 2)), (ks, (0, 1, 0, 1, 2, 0)))):
                        for k, term in enumerate(order):
                            src = scratch["parts"][i, term, g * GH:(g + 1) * GH, :, :].rearrange("h d t -> d h t")
                            sp.dma_start(buf[k * HD:(k + 1) * HD, g % 2, :, :], src).then_inc(stack_in, 16)

                def shift_rows(g):
                    sp.wait_ge(ring_freed_dve, b * N_RING_DVE + freed_before(RING_AT[("mT", g)] + 1)[1])
                    for s in range(2):
                        sp.dma_start(qs[STACK + s:STACK + s + 1, g % 2, :, :],
                                     mT[s * 32:(s + 1) * 32, :]).then_inc(m_rows, 16)
                stacks(0)
                stacks(1)
                shift_rows(0)
                for g in range(NG):
                    if g + 1 < NG:
                        shift_rows(g + 1)
                    if g + 2 < NG:
                        sp.wait_ge(st_done, b * NG * TILES_OF_GROUP + (g + 1) * TILES_OF_GROUP)
                        stacks(g + 2)
                sp.wait_ge(ring_freed_dve, b * N_RING_DVE + freed_before(RING_AT[("wo", 3)] + 1)[1])
                sp.dma_start(scratch["h2"][bass.ds(b * T, T), :].rearrange("(t p) d -> p t d", p=P),
                             h[:]).then_inc(rows_out, 16)
                sp.wait_ge(normed, 2 * NT * (b + 1))
                sp.dma_start(scratch["xn2"][bass.ds(b * T, T), :].rearrange("(t p) d -> p t d", p=P),
                             xn[:]).then_inc(rows_out, 16)

            sequence(0)
            with sp.Fori(1, B) as b:
                sequence(b)
            sp.wait_ge(rows_out, 32 * B)
            sp.wait_ge(m_rows, 32 * NG * B)
            sp.wait_ge(stack_in, 16 * LOADS * NG * B)

        @block.gpsimd
        def _(pool):
            def sequence(b):
                pool.wait_ge(weights_in, 16 * 13)
                pool.wait_ge(ring_freed_act, b * N_RING_ACT + 4)
                nc.gpsimd.tensor_tensor(hb[:], h[:], bo_sb[:].unsqueeze(1).to_broadcast([P, NT, D]),
                                        ALU.add).then_inc(hb_done, 1)
                rotary(pool, nc.gpsimd, b, 1, rot_k)

            sequence(0)
            with pool.Fori(1, B) as b:
                sequence(b)

        @block.scalar
        def _(act):
            def evac(b, use, dst, func=ACT.Copy, view=None, **kw):
                src = filled(act, b, use)[:]
                nc.scalar.activation(dst, view(src) if view else src, func, **kw).then_inc(ring_freed_act, 1)

            def turn_view(src):
                return src.rearrange("p (c t) -> p c t", c=2)

            def deviation(b, first):
                at = 2 * b + first
                act.wait_ge(var_done, at + 1)
                nc.scalar.activation(logv[:], var[:], ACT.Ln).then_inc(guess_done, 1)
                act.wait_ge(guess_done, 2 * at + 1)
                nc.scalar.activation(guess[:], logv[:], ACT.Exp, scale=-0.5).then_inc(guess_done, 1)

            act.wait_ge(weights_in, 16 * 13)
            def sequence(b):
                wait_for(act, rows_out, 32 * b)
                for k in range(4):
                    evac(b, ("emb", k), h[:, 2 * k:2 * k + 2, :].rearrange("p t d -> p (t d)"))
                deviation(b, 0)
                for k in range(4):
                    evac(b, ("xT", k), xnT[:, :, 256 * k:256 * (k + 1)], view=turn_view)
                for k in range(8):
                    i, c, half = k // 4, k // 2 % 2, k % 2
                    evac(b, ("qk", k), qk[:, i, half, c * 512:(c + 1) * 512], ACT.Identity,
                         bias=qk_bias[:, i, half:half + 1])
                n = b * (NG * TILES_OF_GROUP)
                done = 0
                for s in range(STEPS + 1):
                    g, t = divmod(s, NSTEP)
                    tiles = TILES_OF_STEP[t] if s < STEPS else 0
                    for k in range(max(tiles, 2)):
                        if k < tiles:
                            act.wait_ge(st_done, n + done + 1)
                            if k == 0:
                                if s >= 2:
                                    wait_for(act, pv_done, b * STEPS + s - 1)
                                else:
                                    wait_for(act, pv_done, b * STEPS)
                            dst = probs[:, s % 2, k, :] if t < NSTEP - 1 else \
                                probs[:, s % 2, 2 * k:2 * k + 2, 0:512]
                            src = st[done % 2][:] if t < NSTEP - 1 else \
                                st[done % 2][:].rearrange("p (h q) -> p h q", h=2)
                            nc.scalar.activation(dst, src, ACT.Exp, scale=SCALE).then_inc(exp_done, 1)
                            done += 1
                        if k == 1:
                            for half in range(2):
                                if turn_step(s + 1, half) is not None:
                                    gh = turn_step(s + 1, half)
                                    if half == 0:
                                        act.wait_ge(pv_half, b * NG + gh + 1)
                                    else:
                                        act.wait_ge(pv_done, b * STEPS + (gh + 1) * NSTEP)
                                    if gh >= 1:
                                        act.wait_ge(ring_filled, b * N_RING + RING_AT[("turn", gh - 1, half)] + 1)
                                    nc.scalar.activation(sums[:, half, :], pv[:], ACT.Copy).then_inc(pv_freed, 1)
                for k in range(4):
                    evac(b, ("aT", k), xnT[:, :, 256 * k:256 * (k + 1)], view=turn_view)
                deviation(b, 1)
                for k in range(4):
                    if k == 0:
                        act.wait_ge(ring_filled, b * N_RING + RING_AT[("wo", 3)] + 1)
                    evac(b, ("x2T", k), xnT[:, :, 256 * k:256 * (k + 1)], view=turn_view)

            sequence(0)
            with act.Fori(1, B) as b:
                sequence(b)

        @block.vector
        def _(dve):
            nc.vector.memset(e_rhs[:], 0.0).then_inc(set_once, 1)
            nc.vector.memset(ks[STACK:STACK + 32, :, :, :], -1.0).then_inc(set_once, 1)
            nc.vector.memset(vals[:], 0.0).then_inc(set_once, 1)
            dve.wait_ge(set_once, 3)
            nc.vector.memset(vals[:, :, :, HD:HD + 1], 1.0).then_inc(set_once, 1)
            dve.wait_ge(weights_in, 16 * 13)

            def norm(b, first, ready):
                base = 2 * NT * b + NT * first
                for t in range(NT):
                    ready(t)
                    nc.vector.bn_stats(stats[:, t, :], h[:, t, :]).then_inc(stats_done, 1)
                dve.wait_ge(stats_done, base + NT)
                wait_for(dve, normed, base)
                dve.nop(nofuse=True)
                for t in range(NT):
                    nc.vector.bn_aggr(mv[:, t, :], stats[:, t, :]).then_inc(aggr_done, 1)
                dve.wait_ge(aggr_done, base + NT)
                at = 2 * b + first
                nc.vector.tensor_scalar(var[:], mv[:, :, 1], EPS, None, ALU.add).then_inc(var_done, 1)
                dve.wait_ge(guess_done, 2 * at + 2)
                nc.vector.tensor_tensor(newton[:], guess[:], guess[:], ALU.mult).then_inc(rstd_done, 1)
                dve.wait_ge(rstd_done, 4 * at + 1)
                nc.vector.tensor_tensor(newton[:], newton[:], var[:], ALU.mult).then_inc(rstd_done, 1)
                dve.wait_ge(rstd_done, 4 * at + 2)
                nc.vector.tensor_scalar(newton[:], newton[:], -0.5, 1.5, ALU.mult, ALU.add).then_inc(rstd_done, 1)
                dve.wait_ge(rstd_done, 4 * at + 3)
                nc.vector.tensor_tensor(rstd[:], newton[:], guess[:], ALU.mult).then_inc(rstd_done, 1)
                dve.wait_ge(rstd_done, 4 * at + 4)
                for t in range(NT):
                    nc.vector.tensor_scalar(xn[:, t, :], h[:, t, :], mv[:, t, 0:1], rstd[:, t:t + 1],
                                            ALU.subtract, ALU.mult).then_inc(normed, 1)

            def maxima(b, g, m):
                i, k0, w, heads, part = MAXB[m]
                src = filled(dve, b, ("max", g, m))[:, 0:w * len(heads)].rearrange("p (h k) -> p h k", k=w)
                dst = mx[:, i, heads[0]:heads[-1] + 1] if part == 0 else mx2[:, i - 4, heads[0]:heads[-1] + 1]
                nc.vector.tensor_reduce(dst, src, AX.X, ALU.max).then_inc(ring_freed_dve, 1)

            def shift(b, g):
                at = NG * b + g + 1
                _, v = freed_before(RING_AT[("max", g, len(MAXB) - 1)] + 1)
                wait_for(dve, ring_freed_dve, b * N_RING_DVE + v)
                nc.vector.tensor_tensor(mx[:, 4:8, :], mx[:, 4:8, :], mx2[:], ALU.max).then_inc(max_joined, 1)
                dve.wait_ge(max_joined, at)
                nc.vector.tensor_copy(mparts[:, 0].rearrange("p h i -> p i h"), mx[:]).then_inc(m_hi, 1)
                dve.wait_ge(m_hi, at)
                nc.vector.tensor_tensor(mrest[:], mx[:], mparts[:, 0].rearrange("p h i -> p i h"),
                                        ALU.subtract).then_inc(m_diff, 1)
                dve.wait_ge(m_diff, at)
                nc.vector.tensor_copy(mparts[:, 1].rearrange("p h i -> p i h"), mrest[:]).then_inc(m_parts, 1)
                bank = filled(dve, b, ("mT", g))
                wait_for(dve, m_rows, 32 * (NG * b + g))
                nc.vector.tensor_copy(mT[:], bank[0:64, 0:64].bitcast(BF16)).then_inc(ring_freed_dve, 1)

            def scale_half(b, g, half):
                src = filled(dve, b, ("turn", g, half))[:].rearrange("p (t h v) -> p t h v", t=4, h=GH)
                wait_for(dve, ring_freed_dve, b * N_RING_DVE + freed_before(RING_AT[("turn", g, half)])[1])
                nc.vector.reciprocal(rec[:], src[:, :, :, HD:HD + 1]).then_inc(rec_done, 1)
                dve.wait_ge(rec_done, 2 * NG * b + 2 * g + half + 1)
                dst = attn[:, 4 * half:4 * half + 4, g * GH * HD:(g + 1) * GH * HD]
                nc.vector.tensor_tensor(dst.rearrange("p t (h v) -> p t h v", h=GH), src[:, :, :, 0:HD],
                                        rec[:].to_broadcast([P, 4, GH, HD]), ALU.mult).then_inc(ring_freed_dve, 1)

            def sequence(b):
                dve.wait_ge(ids_in, 16 * (b + 1))
                nc.vector.tensor_scalar(e_lhs[0:V, :], ids[:], iota_p[0:V], None,
                                        ALU.is_equal).then_inc(e_ready, 1)
                nc.vector.tensor_copy(e_rhs[V:V + NFRAME, DEMB:D],
                                      keep["zcat"][V:V + NFRAME, bass.ds(b, 1), :].rearrange("p b d -> p (b d)")
                                      ).then_inc(e_ready, 1)
                wait_for(dve, rows_out, 32 * b)

                def h_there(t):
                    if t % 2 == 0:
                        dve.wait_ge(ring_freed_act, b * N_RING_ACT + t // 2 + 1)
                norm(b, 0, h_there)
                for k in range(4):
                    bank = filled(dve, b, ("v", k))[:].rearrange("p (t h v) -> p t h v", t=2, h=NH)
                    nc.vector.tensor_tensor(vals[:, 2 * k:2 * k + 2, :, 0:HD], bank,
                                            bv_sb[:].rearrange("p (h v) -> p h v", h=NH).unsqueeze(1)
                                            .to_broadcast([P, 2, NH, HD]), ALU.add).then_inc(ring_freed_dve, 1)
                rotary(dve, nc.vector, b, 0, rot_q)
                for m in range(len(MAXB)):
                    maxima(b, 0, m)
                shift(b, 0)
                n = 0
                for s in range(STEPS + 2):
                    g, t = divmod(s, NSTEP)
                    if s < STEPS:
                        if t == 0:
                            n = 0
                        for _ in range(TILES_OF_STEP[t]):
                            if g + 1 < NG:
                                for m in range(max_quota(n - 1) if n else 0, max_quota(n)):
                                    maxima(b, g + 1, m)
                            n += 1
                        if t == NSTEP - 2 and g + 1 < NG:
                            shift(b, g + 1)
                    for half in range(2):
                        if turn_step(s, half) is not None:
                            scale_half(b, turn_step(s, half), half)
                dve.wait_ge(hb_done, b + 1)
                for k in range(4):
                    bank = filled(dve, b, ("wo", k))[:].rearrange("p (t d) -> p t d", t=2)
                    nc.vector.tensor_tensor(h[:, 2 * k:2 * k + 2, :], bank, hb[:, 2 * k:2 * k + 2, :],
                                            ALU.add).then_inc(ring_freed_dve, 1)

                def h2_there(t):
                    if t % 2 == 0:
                        _, v = freed_before(RING_AT[("wo", t // 2)] + 1)
                        wait_for(dve, ring_freed_dve, b * N_RING_DVE + v)
                norm(b, 1, h2_there)
                bank = filled(dve, b, ("logit", 0))[:, 0:NT * NE]
                nc.vector.tensor_copy(keep["logits"][:, bass.ds(b * NT, NT), :].rearrange("p t e -> p (t e)"),
                                      bank).then_inc(ring_freed_dve, 1)

            sequence(0)
            with dve.Fori(1, B) as b:
                sequence(b)

        @block.tensor
        def _(pe):
            pe.wait_ge(weights_in, 16 * 13)
            pe.wait_ge(set_once, 4)

            def turns(b, name, src, waits=None):
                for k in range(4):
                    bank = take(pe, b, (name, k))
                    if waits:
                        waits(k)
                    for c in range(2):
                        for u in range(2):
                            mm = nc.tensor.transpose(bank[:, (2 * c + u) * P:(2 * c + u + 1) * P],
                                                     src[:, 2 * k + u, c * P:(c + 1) * P], ident[:])
                    mm.then_inc(ring_filled, 1)

            def rows_product(b, name, w_sb, waits=None):
                for k in range(4):
                    bank = take(pe, b, (name, k))
                    if waits:
                        waits(k)
                    for u in range(2):
                        t = 2 * k + u
                        for c in range(2):
                            mm = nc.tensor.matmul(bank[:, u * D:(u + 1) * D], xnT[:, c, t * P:(t + 1) * P],
                                                  w_sb[:, c, :], start=(c == 0), stop=(c == 1))
                    mm.then_inc(ring_filled, 1)

            def max_bank(b, g, m):
                i, k0, w, heads, part = MAXB[m]
                bank = take(pe, b, ("max", g, m))
                diag = P * i if P * i >= k0 and P * (i + 1) <= k0 + w else None
                for n, h_ in enumerate(heads):
                    mm = nc.tensor.matmul(bank[:, n * w:(n + 1) * w], qs[0:STACK, g % 2, h_, P * i:P * (i + 1)],
                                          ks[0:STACK, g % 2, h_, k0:k0 + w], start=True, stop=(diag is None))
                    if diag is not None:
                        o = n * w + diag - k0
                        mm = nc.tensor.matmul(bank[:, o:o + P], identb, mask_q, start=False, stop=True)
                mm.then_inc(ring_filled, 1)

            def max_turn(b, g):
                bank = take(pe, b, ("mT", g))
                pe.wait_ge(m_parts, NG * b + g + 1)
                pe.nop(nofuse=True)
                nc.tensor.transpose(bank[0:64, 0:64].bitcast(BF16), mparts[:].rearrange("p s h i -> p (s h i)"),
                                    identb).then_inc(ring_filled, 1)

            def score_piece(g, tile, h_, half, j, col):
                q0, w = piece_range(half, j)
                diag = j // 4 == half
                mm = nc.tensor.matmul(tile[:, col:col + w], ks[0:STACK + 2, g % 2, h_, P * j:P * (j + 1)],
                                      qs[0:STACK + 2, g % 2, h_, q0:q0 + w], start=True, stop=not diag)
                if diag:
                    mm = nc.tensor.matmul(tile[:, col:col + P], identb, mask_k, start=False, stop=True)
                return mm

            def sum_pieces(b, s, half):
                g, t = divmod(s, NSTEP)
                mm = None
                for (hf, j, col) in PV_ORDER[t][half]:
                    q0, w = piece_range(hf, j)
                    q0 -= 512 * hf
                    first, last = (j == 0), (j == (2 if hf == 0 else 7))
                    for h_ in range(GH):
                        mm = nc.tensor.matmul(pv[32 * h_:32 * h_ + VW, q0:q0 + w],
                                              vals[:, j, g * GH + h_, :], probs[:, s % 2, h_, col:col + w],
                                              start=first, stop=last)
                return mm

            def sum_step(b, s, part):
                g, t = divmod(s, NSTEP)
                mm = None
                if part == 0:
                    pe.wait_ge(exp_done, b * NG * TILES_OF_GROUP + TILES_OF_GROUP * g + sum(TILES_OF_STEP[:t + 1]))
                    if t == 0:
                        wait_for(pe, pv_freed, 2 * NG * b + 2 * g)
                    if PV_ORDER[t][0]:
                        mm = sum_pieces(b, s, 0)
                        if t == 1:
                            mm.then_inc(pv_half, 1)
                        else:
                            mm.then_inc(pv_done, 1)
                else:
                    if PV_ORDER[t][1]:
                        if t == 1:
                            pe.wait_ge(pv_freed, 2 * NG * b + 2 * g + 1)
                        mm = sum_pieces(b, s, 1)
                        mm.then_inc(pv_done, 1)

            def turn_half(b, g, half):
                bank = take(pe, b, ("turn", g, half))
                pe.wait_ge(pv_freed, 2 * NG * b + 2 * g + half + 1)
                for t in range(4):
                    mm = nc.tensor.transpose(bank[:, t * P:(t + 1) * P], sums[:, half, t * P:(t + 1) * P], ident[:])
                mm.then_inc(ring_filled, 1)

            def sequence(b):
                for k in range(4):
                    bank = take(pe, b, ("emb", k))
                    if k == 0:
                        pe.wait_ge(e_ready, 2 * (b + 1))
                    for u in range(2):
                        t = 2 * k + u
                        mm = nc.tensor.matmul(bank[:, u * D:(u + 1) * D], e_lhs[:, t * P:(t + 1) * P], e_rhs[:],
                                              start=True, stop=True)
                    mm.then_inc(ring_filled, 1)
                turns(b, "xT", xn, lambda k: pe.wait_ge(normed, 2 * NT * b + 2 * k + 2))
                pe.wait_ge(ring_freed_act, b * N_RING_ACT + 8)
                for k in range(8):
                    i, c, half = k // 4, k // 2 % 2, k % 2
                    bank = take(pe, b, ("qk", k))
                    w_sb = (wq_sb, wk_sb)[i]
                    for ch in range(2):
                        mm = nc.tensor.matmul(bank[:], w_sb[:, ch, half * P:(half + 1) * P],
                                              xnT[:, ch, c * 512:(c + 1) * 512], start=(ch == 0), stop=(ch == 1))
                    mm.then_inc(ring_filled, 1)
                rows_product(b, "v", wv_sb)
                pe.wait_ge(stack_in, 16 * LOADS * (NG * b + 2))
                for m in range(len(MAXB)):
                    max_bank(b, 0, m)
                max_turn(b, 0)
                n = 0
                done = 0
                base = b * (NG * TILES_OF_GROUP)
                for s in range(STEPS + 2):
                    g, t = divmod(s, NSTEP)
                    tiles = TILES_OF_STEP[t] if s < STEPS else 0
                    if tiles and t == 0:
                        n = 0
                        pe.wait_ge(m_rows, 32 * (NG * b + g + 1))
                        if g == 0:
                            _, v = freed_before(RING_AT[("v", 3)] + 1)
                            wait_for(pe, ring_freed_dve, b * N_RING_DVE + v)
                    for k in range(max(tiles, 3 if s <= STEPS else 0)):
                        if k < tiles:
                            tile = st[done % 2]
                            if done >= 2:
                                wait_for(pe, exp_done, base + done - 1)
                            else:
                                wait_for(pe, exp_done, base)
                            for h_ in ([k] if t < NSTEP - 1 else [2 * k, 2 * k + 1]):
                                o = 0 if t < NSTEP - 1 else 512 * (h_ % 2)
                                for (half, j, col) in HEAD_TILES[t]:
                                    mm = score_piece(g, tile, h_, half, j, o + col)
                            mm.then_inc(st_done, 1)
                            done += 1
                            if g + 1 < NG:
                                if n == 3 and g >= 1:
                                    pe.wait_ge(stack_in, 16 * LOADS * (NG * b + g + 2))
                                for m in range(max_quota(n - 1) if n else 0, max_quota(n)):
                                    max_bank(b, g + 1, m)
                            n += 1
                        if 1 <= s <= STEPS and k == 1:
                            sum_step(b, s - 1, 0)
                        if 1 <= s <= STEPS and k == (2 if tiles != 2 else 1):
                            sum_step(b, s - 1, 1)
                    if tiles and t == NSTEP - 2 and g + 1 < NG:
                        max_turn(b, g + 1)
                    for half in range(2):
                        if turn_step(s, half) is not None:
                            turn_half(b, turn_step(s, half), half)
                _, v = freed_before(RING_AT[("turn", NG - 1, 1)] + 1)
                wait_for(pe, ring_freed_dve, b * N_RING_DVE + v)
                turns(b, "aT", attn)
                a, _ = freed_before(RING_AT[("aT", 3)] + 1)
                wait_for(pe, ring_freed_act, b * N_RING_ACT + a)
                rows_product(b, "wo", wo_sb)
                turns(b, "x2T", xn, lambda k: pe.wait_ge(normed, 2 * NT * b + NT + 2 * k + 2))
                a, _ = freed_before(RING_AT[("x2T", 3)] + 1)
                wait_for(pe, ring_freed_act, b * N_RING_ACT + a)
                bank = take(pe, b, ("logit", 0))
                for t in range(NT):
                    for c in range(2):
                        mm = nc.tensor.matmul(bank[:, t * NE:(t + 1) * NE], xnT[:, c, t * P:(t + 1) * P],
                                              wr_sb[:, c, :], start=(c == 0), stop=(c == 1))
                mm.then_inc(ring_filled, 1)

            sequence(0)
            with pe.Fori(1, B) as b:
                sequence(b)


def experts(nc, scratch, keep, wg, wd, c_iota, out):
    ctx = ExitStack()
    with ctx:
        def sb(name, shape, dt=F32):
            return ctx.enter_context(nc.sbuf_tensor(name, shape, dt))

        def sem(name):
            return ctx.enter_context(nc.semaphore(name))

        def psum(name):
            return ctx.enter_context(nc.psum_tensor(name, [P, 512], F32))

        N = NTILE
        logits = keep["logits"]
        route = {n: sb("r_" + n, [P, N, NE]) for n in
                 ("l", "g", "t", "eq", "sel", "pre", "pos", "ex", "ex2", "first", "second", "e")}
        one = {n: sb("o_" + n, [P, N]) for n in ("mx", "sum", "rs", "n0", "v2", "need", "va", "vb", "wden")}
        slot_f = sb("slot_f", [P, N, 2])
        slot = sb("slot", [P, N, 2], I32)
        weight = sb("weight", [P, N, 2])
        selb = sb("selb", [P, N, NE], BF16)
        spare = keep["iota"][:, V + 1:V + 2]
        ecap = keep["iota"][:, V + 2:V + 2 + NE]
        NC = NSLOT // P
        TG = 8
        slot_hl = sb("slot_hl", [P, 2, N, 2], I32)
        slot_hlf = sb("slot_hlf", [P, 2, N, 2])
        place_hot = sb("place_hot", [P, 2, TG, 2, P], BF16)
        tile_hot = sb("tile_hot", [P, 2, TG, 2, 3, NC], BF16)
        token_f = sb("token_f", [P, 2, NC])
        token = sb("token", [P, NC], I32)
        c_rows = keep["iota"][:, V + 2 + NE:V + 2 + NE + P]
        NX = 4
        idx = sb("idx", [P, NX, 2], I32)
        NXS = 5
        xidx = sb("xidx", [P, NXS, 2], I32)
        wg_sb = sb("wg_sb", [P, 2, HID])
        wd_sb = sb("wd_sb", [P, 2, 4, D])
        UN = 2
        NU = CAP // (UN * P)
        xs = sb("xs", [P, NXS, UN, D])
        xT = sb("xT", [P, 2, 2, UN * P])
        eneg = sb("eneg", [P, 2, 2, 512])
        hT = sb("hT", [P, 2, 4, UN * P])
        ys = sb("ys", [P, 2, UN * D])
        ya = sb("ya", [P, NX, D])
        yb = sb("yb", [P, NX, D])
        hh = sb("hh", [P, NX, D])
        oo = sb("oo", [P, NX, D])
        wcol = sb("wcol", [P, NX, 2])
        tb = [psum(f"tb{i}") for i in range(2)]
        hbk = [psum(f"hbk{i}") for i in range(4)]
        yb_ = [psum(f"ybk{i}") for i in range(2)]

        w_in, tri_done, route_step = sem("w_in"), sem("tri_done"), sem("route_step")
        exp_out = sem("exp_out")
        hot_made, hot_used = sem("hot_made"), sem("hot_used")
        idx_set = sem("idx_set")
        wd_in = [sem(f"wd_in{i}") for i in range(2)]
        xs_in = [sem(f"xs_in{i}") for i in range(NXS)]
        x_turned, xT_made, hid_done, e_done, r_done, h_made = (sem("x_turned"), sem("xT_made"), sem("hid_done"),
                                                              sem("e_done"), sem("r_done"), sem("h_made"))
        d_done = sem("d_done")
        y_done, y_copied = sem("y_done"), sem("y_copied")
        y_out = [sem(f"y_out{i}") for i in range(2)]
        gidx_set = sem("gidx_set")
        ya_in = [sem(f"ya_in{i}") for i in range(NX)]
        hh_in = [sem(f"hh_in{i}") for i in range(NX)]
        mixed, half_mixed, wcol_set = sem("mixed"), sem("half_mixed"), sem("wcol_set")
        o_out = [sem(f"o_out{i}") for i in range(NX)]

        count = [0]
        marks = {}
        block = ctx.enter_context(nc.Block())
        n_units = NE * NU

        def copy_out(act, pair, m):
            n = pair * (2 * NU) + m
            act.wait_ge(y_done, n + 1)
            wait_for(act, y_out[m % 2], 16 * (pair * NU + m // 2))
            nc.scalar.activation(ys[:, m % 2, :], yb_[m % 2][:], ACT.Copy).then_inc(y_copied, 1)

        def store_y(sp, pair, m):
            n = pair * (2 * NU) + m
            wait_for(sp, y_copied, n + 1)
            sp.dma_start(scratch["yslot"][bass.ds(n * UN * P, UN * P), :].rearrange("(t p) d -> p t d", p=P),
                         ys[:, m % 2, :].rearrange("p (t d) -> p t d", t=UN)).then_inc(y_out[m % 2], 16)

        @block.vector
        def _(dve):
            def step(ins):
                count[0] += 1
                ins.then_inc(route_step, 1)
                dve.wait_ge(route_step, count[0])

            def wide(a):
                return a[:].unsqueeze(2).to_broadcast([P, N, NE])
            v = nc.vector
            r, o = route, one
            dve.wait_ge(w_in, 16)
            step(v.tensor_reduce(o["mx"][:], logits[:], AX.X, ALU.max))
            step(v.tensor_tensor(r["l"][:], logits[:], wide(o["mx"]), ALU.subtract))
            step(v.tensor_scalar(r["l"][:], r["l"][:], -87.33654, None, ALU.max))
            marks["logits"] = count[0]
            step(v.tensor_scalar(r["eq"][:], r["l"][:], 0.0, None, ALU.is_equal))
            step(v.tensor_reduce(o["n0"][:], r["eq"][:], AX.X, ALU.add))
            step(v.scalar_tensor_tensor(r["t"][:], r["eq"][:], -1e4, r["l"][:], ALU.mult, ALU.add))
            step(v.tensor_reduce(o["v2"][:], r["t"][:], AX.X, ALU.max))
            step(v.tensor_scalar(o["n0"][:], o["n0"][:], 1.5, None, ALU.is_lt))
            step(v.tensor_tensor(o["v2"][:], o["v2"][:], o["n0"][:], ALU.mult))
            step(v.tensor_tensor(r["t"][:], r["l"][:], wide(o["v2"]), ALU.is_gt))
            step(v.tensor_reduce(o["need"][:], r["t"][:], AX.X, ALU.add))
            step(v.tensor_scalar(o["need"][:], o["need"][:], -1.0, 2.0, ALU.mult, ALU.add))
            step(v.tensor_tensor(r["eq"][:], r["l"][:], wide(o["v2"]), ALU.is_equal))

            def before(dst, src):
                step(v.memset(dst[:, :, 0:1], 0.0))
                for e in range(1, NE):
                    step(v.tensor_tensor(dst[:, :, e:e + 1], dst[:, :, e - 1:e], src[:, :, e - 1:e], ALU.add))
            before(r["pre"], r["eq"])
            step(v.tensor_tensor(r["pre"][:], r["pre"][:], wide(o["need"]), ALU.is_lt))
            step(v.tensor_tensor(r["eq"][:], r["eq"][:], r["pre"][:], ALU.mult))
            step(v.tensor_tensor(r["sel"][:], r["eq"][:], r["t"][:], ALU.add))
            step(v.tensor_copy(selb[:], r["sel"][:]))
            marks["chosen"] = count[0]
            before(r["pre"], r["sel"])
            step(v.tensor_scalar(r["first"][:], r["pre"][:], 0.5, None, ALU.is_lt))
            step(v.tensor_tensor(r["first"][:], r["first"][:], r["sel"][:], ALU.mult))
            step(v.tensor_tensor(r["second"][:], r["sel"][:], r["first"][:], ALU.subtract))
            dve.wait_ge(exp_out, 1)
            step(v.tensor_reduce(o["sum"][:], r["e"][:], AX.X, ALU.add))
            step(v.reciprocal(o["rs"][:], o["sum"][:]))
            step(v.tensor_tensor(r["g"][:], r["e"][:], wide(o["rs"]), ALU.mult))
            dve.wait_ge(tri_done, 2)
            step(v.memset(r["ex"][:, 0:1, :], 0.0))
            step(v.tensor_copy(r["ex"][:, 1:N, :], tb[1][:].rearrange("p (t e) -> p t e", e=NE)[:, 0:N - 1, :]))
            a, c = r["ex"], r["ex2"]
            reach = 1
            while reach < N:
                step(v.tensor_copy(c[:, 0:reach, :], a[:, 0:reach, :]))
                step(v.tensor_tensor(c[:, reach:N, :], a[:, reach:N, :], a[:, 0:N - reach, :], ALU.add))
                a, c = c, a
                reach *= 2
            step(v.scalar_tensor_tensor(r["pos"][:], tb[0][:].rearrange("p (t e) -> p t e", e=NE), -1.0, a[:],
                                        ALU.add, ALU.add))
            keep_ = r["eq"]
            step(v.tensor_scalar(keep_[:], r["pos"][:], CAP - 0.5, None, ALU.is_lt))
            step(v.tensor_tensor(r["pos"][:], r["pos"][:], ecap.unsqueeze(1).to_broadcast([P, N, NE]), ALU.add))
            for k, (name, valid) in enumerate((("first", "va"), ("second", "vb"))):
                step(v.tensor_tensor(r["t"][:], r[name][:], keep_[:], ALU.mult))
                step(v.tensor_reduce(o[valid][:], r["t"][:], AX.X, ALU.add))
                step(v.tensor_tensor(r["e"][:], r["t"][:], r["pos"][:], ALU.mult))
                step(v.tensor_reduce(slot_f[:, :, k], r["e"][:], AX.X, ALU.add))
                step(v.tensor_scalar(o[valid][:], o[valid][:], -1.0, 1.0, ALU.mult, ALU.add))
                step(v.tensor_scalar(o[valid][:], o[valid][:], spare, None, ALU.mult))
                step(v.tensor_tensor(slot_f[:, :, k], slot_f[:, :, k], o[valid][:], ALU.add))
                step(v.tensor_tensor(r["e"][:], r["t"][:], r["g"][:], ALU.mult))
                step(v.tensor_reduce(weight[:, :, k], r["e"][:], AX.X, ALU.add))
            step(v.tensor_copy(slot[:], slot_f[:]))
            step(v.tensor_tensor(o["wden"][:], weight[:, :, 0], weight[:, :, 1], ALU.add))
            step(v.tensor_scalar(o["wden"][:], o["wden"][:], 1e-6, None, ALU.add))
            step(v.reciprocal(o["wden"][:], o["wden"][:]))
            step(v.tensor_tensor(weight[:], weight[:], o["wden"][:].unsqueeze(2).to_broadcast([P, N, 2]), ALU.mult))
            marks["slots"] = count[0]

            step(v.tensor_scalar(slot_hl[:, 0], slot[:], 7, None, ALU.arith_shift_right))
            step(v.tensor_scalar(slot_hl[:, 1], slot[:], P - 1, None, ALU.bitwise_and))
            step(v.tensor_copy(slot_hlf[:], slot_hl[:]))
            for gr in range(N // TG):
                ts = slice(gr * TG, (gr + 1) * TG)
                if gr >= 2:
                    dve.wait_ge(hot_used, gr - 1)
                v.tensor_tensor(place_hot[:, gr % 2], slot_hlf[:, 1, ts, :].unsqueeze(3).to_broadcast([P, TG, 2, P]),
                                c_rows.unsqueeze(1).unsqueeze(1).to_broadcast([P, TG, 2, P]),
                                ALU.is_equal).then_inc(hot_made, 1)
                hot = tile_hot[:, gr % 2]
                step(v.tensor_tensor(hot[:, :, :, 0, :], slot_hlf[:, 0, ts, :].unsqueeze(3).to_broadcast([P, TG, 2, NC]),
                                     c_rows[:, 0:NC].unsqueeze(1).unsqueeze(1).to_broadcast([P, TG, 2, NC]),
                                     ALU.is_equal))
                v.tensor_scalar(hot[:, :, :, 1, :], hot[:, :, :, 0, :], keep["iota"][:, V:V + 1], None,
                                ALU.mult).then_inc(hot_made, 1)
                v.tensor_tensor(hot[:, :, :, 2, :], hot[:, :, :, 0, :],
                                c_rows[:, ts].unsqueeze(2).unsqueeze(3).to_broadcast([P, TG, 2, NC]),
                                ALU.mult).then_inc(hot_made, 1)
            dve.wait_ge(hot_used, N // TG)
            sums = hbk[0][:, 0:2 * NC].rearrange("p (k c) -> p k c", k=2)
            step(v.tensor_scalar(token_f[:, 1, :], sums[:, 1, :], float(P), None, ALU.mult))
            step(v.tensor_tensor(token_f[:, 0, :], sums[:, 0, :], token_f[:, 1, :], ALU.add))
            step(v.tensor_copy(token[:], token_f[:, 0, :]))
            marks["tokens"] = count[0]

            def expert_pair(pair):
                for m in range(2 * NU):
                    n = pair * (2 * NU) + m
                    wait_for(dve, x_turned, n + 1)
                    if m >= 2:
                        wait_for(dve, hid_done, 2 * n - 2)
                    v.tensor_copy(xT[:, m % 2].rearrange("p c t -> p (c t)"), tb[m % 2][:]).then_inc(xT_made, 1)
                    for f in range(2):
                        e_, d_ = eneg[:, f, 0, :], eneg[:, f, 1, :]
                        dve.wait_ge(e_done, 2 * n + f + 1)
                        wait_for(dve, h_made, 2 * n + f - 1) if m else wait_for(dve, h_made, 2 * n)
                        v.tensor_scalar(d_, e_, 1.0, None, ALU.add).then_inc(d_done, 1)
                        dve.wait_ge(d_done, 2 * n + f + 1)
                        v.reciprocal(d_, d_).then_inc(r_done, 1)
                        wait_for(dve, r_done, 2 * n + f + 1)
                        if m >= 2:
                            wait_for(dve, y_done, n - 1)
                        v.tensor_tensor(hT[:, m % 2, 2 * f:2 * f + 2, :].rearrange("p f t -> p (f t)"),
                                        hbk[2 * (m % 2) + f][:], d_, ALU.mult).then_inc(h_made, 1)

            expert_pair(0)
            with dve.Fori(1, NE // 2) as pair:
                expert_pair(pair)

            def tile_group(q):
                for i in range(NX):
                    n = q * NX + i
                    dve.wait_ge(ya_in[i], 32 * (q + 1))
                    dve.wait_ge(hh_in[i], 16 * (q + 1))
                    wait_for(dve, o_out[i], 16 * q)
                    v.tensor_copy(wcol[:, i, :], weight[:, bass.ds(n, 1), :].rearrange("p t k -> p (t k)")
                                  ).then_inc(wcol_set, 1)
                    dve.wait_ge(wcol_set, n + 1)
                    v.scalar_tensor_tensor(hh[:, i, :], ya[:, i, :], wcol[:, i, 0:1], hh[:, i, :],
                                           ALU.mult, ALU.add).then_inc(half_mixed, 1)
                    dve.wait_ge(half_mixed, n + 1)
                    v.scalar_tensor_tensor(oo[:, i, :], yb[:, i, :], wcol[:, i, 1:2], hh[:, i, :],
                                           ALU.mult, ALU.add).then_inc(mixed, 1)

            tile_group(0)
            with dve.Fori(1, N // NX) as q:
                tile_group(q)

        @block.scalar
        def _(act):
            act.wait_ge(route_step, marks["logits"])
            nc.scalar.activation(route["e"][:], route["l"][:], ACT.Exp).then_inc(exp_out, 1)
            def expert_pair(pair):
                for m in range(2 * NU):
                    n = pair * (2 * NU) + m
                    for f in range(2):
                        act.wait_ge(hid_done, 2 * n + f + 1)
                        wait_for(act, r_done, 2 * n + f - 1) if m else wait_for(act, r_done, 2 * n)
                        nc.scalar.activation(eneg[:, f, 0, :], hbk[2 * (m % 2) + f][:], ACT.Exp,
                                             scale=-1.0).then_inc(e_done, 1)
                    if m >= 1:
                        copy_out(act, pair, m - 1)
                copy_out(act, pair, 2 * NU - 1)

            expert_pair(0)
            with act.Fori(1, NE // 2) as pair:
                expert_pair(pair)

        @block.tensor
        def _(pe):
            pe.wait_ge(route_step, marks["chosen"])
            for k in range(2):
                nc.tensor.matmul(tb[k][:], keep["b16"][:, 3 + k, :], selb[:].rearrange("p t e -> p (t e)"),
                                 start=True, stop=True).then_inc(tri_done, 1)
            pe.wait_ge(w_in, 16)
            for gr in range(N // TG):
                pe.wait_ge(hot_made, 3 * (gr + 1))
                for t in range(TG):
                    for k in range(2):
                        mm = nc.tensor.matmul(hbk[0][:, 0:2 * NC], place_hot[:, gr % 2, t, k, :],
                                              tile_hot[:, gr % 2, t, k, 1:3, :].rearrange("p a c -> p (a c)"),
                                              start=(gr == 0 and t == 0 and k == 0),
                                              stop=(gr == N // TG - 1 and t == TG - 1 and k == 1))
                mm.then_inc(hot_used, 1)
            pe.wait_ge(route_step, marks["tokens"])

            def out_rows(pair, m):
                n = pair * (2 * NU) + m
                wait_for(pe, h_made, 2 * n + 2)
                if m % NU == 0:
                    pe.wait_ge(wd_in[m // NU], 16 * (pair + 1))
                wait_for(pe, y_copied, n - 1) if m >= 2 else wait_for(pe, y_copied, pair * (2 * NU))
                for t in range(UN):
                    for f in range(4):
                        mm = nc.tensor.matmul(yb_[m % 2][:, t * D:(t + 1) * D], hT[:, m % 2, f, t * P:(t + 1) * P],
                                              wd_sb[:, m // NU, f, :], start=(f == 0), stop=(f == 3))
                mm.then_inc(y_done, 1)

            def expert_pair(pair):
                for m in range(2 * NU):
                    n = pair * (2 * NU) + m
                    pe.wait_ge(xs_in[m % NXS], 32 * (pair * 2 + m // NXS + 1))
                    wait_for(pe, xT_made, n - 1) if m >= 2 else wait_for(pe, xT_made, pair * (2 * NU))
                    for c in range(2):
                        for t in range(UN):
                            mm = nc.tensor.transpose(tb[m % 2][:, (c * UN + t) * P:(c * UN + t + 1) * P],
                                                     xs[:, m % NXS, t, c * P:(c + 1) * P], keep["ident"][:])
                    mm.then_inc(x_turned, 1)
                    pe.wait_ge(xT_made, n + 1)
                    wait_for(pe, h_made, 2 * n - 2) if m >= 2 else wait_for(pe, h_made, pair * (4 * NU))
                    for f in range(4):
                        for c in range(2):
                            mm = nc.tensor.matmul(hbk[2 * (m % 2) + f // 2][:, (f % 2) * 256:(f % 2) * 256 + 256],
                                                  wg_sb[:, c, f * P:(f + 1) * P], xT[:, m % 2, c, :],
                                                  start=(c == 0), stop=(c == 1))
                        if f % 2:
                            mm.then_inc(hid_done, 1)
                    if m >= 1:
                        out_rows(pair, m - 1)
                out_rows(pair, 2 * NU - 1)

            expert_pair(0)
            with pe.Fori(1, NE // 2) as pair:
                expert_pair(pair)

        @block.sync
        def _(sp):
            sp.dma_start(wg_sb[:], wg).then_inc(w_in, 16)
            def expert_pair(pair):
                for m in range(2 * NU):
                    n = pair * (2 * NU) + m
                    if m % NU == 0:
                        e = m // NU
                        wait_for(sp, y_done, pair * (2 * NU))
                        sp.dma_start(wd_sb[:, e], wd[bass.ds(pair * 2 + e, 1)].rearrange("o p f d -> (o p) f d")
                                     ).then_inc(wd_in[e], 16)
                    if m >= 3:
                        store_y(sp, pair, m - 3)
                for m in range(2 * NU - 3, 2 * NU):
                    store_y(sp, pair, m)

            expert_pair(0)
            with sp.Fori(1, NE // 2) as pair:
                expert_pair(pair)
            for i in range(2):
                sp.wait_ge(y_out[i], 16 * (n_units // 2))
            def tile_group(q):
                for i in range(NX):
                    n = q * NX + i
                    wait_for(sp, mixed, q * NX)
                    sp.dma_start(hh[:, i, :], scratch["h2"][bass.ds(n * P, P), :]).then_inc(hh_in[i], 16)
                for i in range(NX):
                    n = q * NX + i
                    sp.wait_ge(mixed, n + 1)
                    sp.dma_start(out[bass.ds(n * P, P), :], oo[:, i, :]).then_inc(o_out[i], 16)

            tile_group(0)
            with sp.Fori(1, N // NX) as q:
                tile_group(q)
            for i in range(NX):
                sp.wait_ge(o_out[i], 16 * (N // NX))

        @block.gpsimd
        def _(pool):
            pool.wait_ge(route_step, marks["tokens"])
            def expert_pair(pair):
                for m in range(2 * NU):
                    n = pair * (2 * NU) + m
                    wait_for(pool, x_turned, n - NXS + 1) if m >= NXS else wait_for(pool, x_turned, pair * (2 * NU))
                    pool.nop(nofuse=True)
                    nc.gpsimd.tensor_copy(xidx[:, m % NXS, :], token[:, bass.ds(n * UN, UN)]).then_inc(idx_set, 1)
                    pool.wait_ge(idx_set, n + 1)
                    pool.nop(nofuse=True)
                    for t in range(UN):
                        nc.gpsimd.indirect_dma_start(
                            xs[:, m % NXS, t, :], None, scratch["xn2"],
                            bass.IndirectOffsetOnAxis(xidx[:, m % NXS, t:t + 1].bitcast(U32), 0)
                            ).then_inc(xs_in[m % NXS], 16)

            expert_pair(0)
            with pool.Fori(1, NE // 2) as pair:
                expert_pair(pair)
            for i in range(2):
                pool.wait_ge(y_out[i], 16 * (n_units // 2))
            def tile_group(q):
                for i in range(NX):
                    n = q * NX + i
                    wait_for(pool, ya_in[i], 32 * q)
                    pool.nop(nofuse=True)
                    nc.gpsimd.tensor_copy(idx[:, i, :], slot[:, bass.ds(n, 1), :].rearrange("p t k -> p (t k)")
                                          ).then_inc(gidx_set, 1)
                for i in range(NX):
                    n = q * NX + i
                    pool.wait_ge(gidx_set, n + 1)
                    wait_for(pool, mixed, q * NX)
                    pool.nop(nofuse=True)
                    for k, dst in enumerate((ya, yb)):
                        nc.gpsimd.indirect_dma_start(
                            dst[:, i, :], None, scratch["yslot"],
                            bass.IndirectOffsetOnAxis(idx[:, i, k:k + 1].bitcast(U32), 0)).then_inc(ya_in[i], 16)

            tile_group(0)
            with pool.Fori(1, N // NX) as q:
                tile_group(q)


def constants(np):
    f32 = np.float32
    n, f = np.arange(NFFT)[:, None], np.arange(NFREQ)[None, :]
    angle = 2.0 * np.pi * ((n * f) % NFFT) / NFFT
    dft = np.concatenate([np.cos(angle), -np.sin(angle)], 1).astype(f32)
    coord = np.clip((np.arange(T, dtype=f32) + f32(0.5)) * f32(NFRAME / T) - f32(0.5), f32(0), f32(NFRAME - 1))
    i0 = np.floor(coord).astype(np.int32)
    i1 = np.minimum(i0 + 1, NFRAME - 1)
    w = (coord - i0).astype(f32)
    interp = np.zeros((NFRAME + 1, T), f32)
    interp[i0, np.arange(T)] += f32(1) - w
    interp[i1, np.arange(T)] += w
    interp[NFRAME] = 1
    theta = f32(10000.0) ** (-np.arange(0, HD, 2, dtype=f32) / f32(HD))
    freqs = (np.arange(T, dtype=f32)[:, None] * theta[None, :]).T.astype(np.float64)
    rope = np.stack([np.tile(np.cos(freqs), (NH, 1)), np.tile(np.sin(freqs), (NH, 1))], 1).astype(f32)
    ident = np.eye(P, dtype=f32)
    row, col = np.arange(P)[:, None], np.arange(P)[None, :]
    b16 = np.stack([ident, np.where(col <= row, 0, -1e30), np.where(col >= row, 0, -1e30),
                    (row <= col) * 1.0, np.ones((P, P))], 1).astype(f32)
    iota = np.zeros((P, V + 2 + NE + P), f32)
    iota[:, 0:V] = np.arange(V)
    iota[:, V] = np.arange(P)
    iota[:, V + 1] = NSLOT + np.arange(P)
    iota[:, V + 2:V + 2 + NE] = np.arange(NE) * CAP
    iota[:, V + 2 + NE:] = np.arange(P)
    return dict(c_dft=dft, c_interp=interp, c_rope=rope, c_ident=ident, c_mask=b16, c_iota=iota)


def kernel(**inputs):
    import numpy as np
    import concourse.bacc as bacc
    from concourse.bass_utils import run_bass_kernel_spmd

    i = {k: np.asarray(v) for k, v in inputs.items()}
    x = i["x"]
    c = np.ascontiguousarray
    padded = np.pad(x, ((0, 0), (NFFT // 2, NFFT // 2)), mode="reflect")
    frames = np.stack([padded[:, NFFT * t:NFFT * (t + 1)] for t in range(NFRAME)], 1)

    def cols(w):
        return c(w.T.reshape(2, P, -1).transpose(1, 0, 2))

    order = np.concatenate([np.arange(0, D, 2), np.arange(1, D, 2)])
    arrays = dict(
        x_frames=c(frames.reshape(BF, NFFT).T), x_tok=c(x), emb=c(i["L0_tok_emb_table"]),
        pw=c(i["L0_tok_proj_w"].reshape(DST, NFREQ, V).transpose(2, 1, 0)),
        pb=c(i["L0_tok_proj_b"][None]), window=c(i["L0_tok_window"][:, None]),
        wq=cols(i["L0_attn_Wq"][order]), bq=c(i["L0_attn_bq"][order].reshape(2, P).T),
        wk=cols(i["L0_attn_Wk"][order]), bk=c(i["L0_attn_bk"][order].reshape(2, P).T),
        wv=cols(i["L0_attn_Wv"]), bv=c(i["L0_attn_bv"][None]),
        wo=cols(i["L0_attn_Wo"]), bo=c(i["L0_attn_bo"][None]),
        wr=cols(i["L0_ffn_w_router"]), wg=cols(i["L0_ffn_w_gate"]),
        wd=c(i["L0_ffn_w_down"].transpose(0, 2, 1).reshape(NE, 4, P, D).transpose(0, 2, 1, 3)),
        **constants(np))
    nc = bacc.Bacc("TRN2", target_bir_lowering=False, num_devices=1)
    ins = [nc.dram_tensor(k, a.shape, mybir.dt.from_np(a.dtype), kind="ExternalInput").ap() for k, a in arrays.items()]
    out = nc.dram_tensor("out", (NTOK, D), F32, kind="ExternalOutput").ap()
    build(nc, ins, out)
    r = run_bass_kernel_spmd(nc, [arrays], core_ids=[0])
    return r.results[0]["out"].reshape(B, T, D)
```

```python
import concourse.bass as bass
from concourse import mybir
from contextlib import ExitStack

F32 = mybir.dt.float32
BF16 = mybir.dt.bfloat16
I32 = mybir.dt.int32
U32 = mybir.dt.uint32
ALU = mybir.AluOpType
ACT = mybir.ActivationFunctionType
AX = mybir.AxisListType

B, T, V, D = 8, 1024, 64, 256
P = 128
NT = T // P
NFFT, NFRAME, NFREQ = 64, 17, 33
DEMB = 179
DST = D - DEMB
BF = B * NFRAME
NH, HD, HALF = 16, 16, 8
GH, NG = 4, 4
NE, HID, CAP = 8, 512, 1280
NTOK = B * T
NTILE = NTOK // P
NSLOT = NE * CAP
SCALE = HD ** -0.5
EPS = 1e-5
STACK = 6 * HD
VW = 32


def piece_range(half, j):
    start = max(512 * half, P * j)
    return start, 512 * (half + 1) - start


HEAD_TILES = [
    [(0, 0, 0), (0, 1, 512), (0, 3, 896)],
    [(0, 2, 0), (1, 6, 256), (1, 0, 512)],
    [(1, 1, 0), (1, 2, 512)],
    [(1, 3, 0), (1, 4, 512)],
    [(1, 5, 0), (1, 7, 384)],
]
PV_ORDER = [
    [[(0, 0, 0), (0, 1, 512), (0, 3, 896)], []],
    [[(0, 2, 0)], [(1, 0, 512), (1, 6, 256)]],
    [[], [(1, 1, 0), (1, 2, 512)]],
    [[], [(1, 3, 0), (1, 4, 512)]],
    [[], [(1, 5, 0), (1, 7, 384)]],
]
NSTEP = len(HEAD_TILES)
STEPS = NG * NSTEP
TILES_OF_STEP = [4, 4, 4, 4, 2]
TILES_OF_GROUP = sum(TILES_OF_STEP)


def max_banks():
    out = []
    for i in range(NT):
        w = min(512, P * (i + 1))
        per = min(GH, 512 // w)
        for h in range(0, GH, per):
            out.append((i, 0, w, list(range(h, h + per)), 0))
    for i in range(4, NT):
        w = P * (i + 1) - 512
        per = min(GH, 512 // w)
        for h in range(0, GH, per):
            out.append((i, 512, w, list(range(h, h + per)), 1))
    return out


MAXB = max_banks()


def max_quota(tile_no):
    if tile_no < 3:
        return 0
    return min(len(MAXB), -(-(tile_no - 2) * len(MAXB) // 11))


POST_USES = {(2, k): [("aT", k)] for k in range(4)} | {(3, k): [("wo", k)] for k in range(4)} \
    | {(6, k): [("x2T", k)] for k in range(4)} | {(7, 0): [("logit", 0)]}
PRE_USES = {(1, k): [("emb", k)] for k in range(4)} | {(8, k): [("xT", k)] for k in range(4)} \
    | {(9, 0): [("qk", 4), ("qk", 5)], (9, 1): [("qk", 6), ("qk", 7)]} \
    | {(10, k): [("qk", k)] for k in range(4)} | {(11, k): [("v", k)] for k in range(4)}
QK_ORDER = (4, 5, 6, 7, 0, 1, 2, 3)


def extra_uses(s, k, pre, post):
    return (PRE_USES.get((s, k), []) if pre else []) + (POST_USES.get((s, k), []) if post else [])


def max_range(s, k, pre):
    g, t = divmod(s, NSTEP)
    if g + 1 == NG and not pre:
        return 0, range(0)
    n = sum(TILES_OF_STEP[:t]) + k
    return g + 1, range(max_quota(n - 1) if n else 0, max_quota(n))


def max_turned(s, pre):
    g, t = divmod(s, NSTEP)
    return g + 1 if t == NSTEP - 2 and (g + 1 < NG or pre) else None


def turns_of(s, post):
    g, t = divmod(s, NSTEP)
    out = []
    if t == 3 and s < STEPS:
        out.append((g, 0))
    if t == 1 and (g >= 1 or post):
        out.append((g - 1, 1))
    return out


def copied_in(s, post):
    return turns_of(s + 1, post)


def body_uses(pre, post):
    r = []
    for s in range(STEPS):
        for k in range(TILES_OF_STEP[s % NSTEP]):
            g, ms = max_range(s, k, pre)
            r += [("max", g, m) for m in ms] + extra_uses(s, k, pre, post)
        if max_turned(s, pre) is not None:
            r.append(("mT", max_turned(s, pre)))
        r += [("turn", g, half) for g, half in turns_of(s, post)]
    return r


SEGMENTS = {
    "pro": [("emb", k) for k in range(4)] + [("xT", k) for k in range(4)] + [("qk", k) for k in QK_ORDER]
    + [("v", k) for k in range(4)] + [("max", NG, m) for m in range(len(MAXB))] + [("mT", NG)],
    "first": body_uses(True, False),
    "mid": body_uses(True, True),
    "last": body_uses(False, True),
    "end": [("turn", -1, 1)] + [("aT", k) for k in range(4)] + [("wo", k) for k in range(4)]
    + [("x2T", k) for k in range(4)] + [("logit", 0)],
}
ACT_USES = ("emb", "xT", "qk", "aT", "x2T")
NB = 3


def by_act(u):
    return u[0] in ACT_USES


def counts(uses):
    a = sum(by_act(u) for u in uses)
    return len(uses), a, len(uses) - a


class Ring:

    def __init__(self, segment, b=0):
        self.uses = SEGMENTS[segment]
        self.at = {u: n for n, u in enumerate(self.uses)}
        pro, first, mid, last = (counts(SEGMENTS[x]) for x in ("pro", "first", "mid", "last"))
        if segment == "pro":
            self.start = (0, 0, 0)
        elif segment == "first":
            self.start = pro
        elif segment == "end":
            self.start = tuple(p + f + (B - 2) * m + e for p, f, m, e in zip(pro, first, mid, last))
        else:
            self.start = tuple(b * m + (p + f - m) for p, f, m in zip(pro, first, mid))

    def filled(self, use):
        return self.start[0] + self.at[use] + 1

    def freed(self, use):
        _, a, v = counts(self.uses[:self.at[use] + 1])
        return (True, self.start[1] + a) if by_act(use) else (False, self.start[2] + v)


def build(nc, ins, out):
    (x_frames, x_tok, emb, pw, pb, window, wq, bq, wk, bk, wv, bv, wo, bo, wr, wg, wd,
     c_dft, c_interp, c_rope, c_ident, c_mask, c_iota) = ins
    top = ExitStack()
    with top:
        def dram(name, shape, dt):
            return nc.dram_tensor(name, shape, dt, kind="Internal").ap()

        scratch = {
            "parts": dram("parts", [B, 2, 3, NH, HD, T], BF16),
            "h": dram("h_rows", [NTOK, D], F32),
            "h2": dram("h2", [NTOK, D], F32),
            "xn2": dram("xn2", [NTOK, D], F32),
            "yslot": dram("yslot", [NSLOT + P, D], F32),
        }
        keep = {}
        for name, shape, dt in (("zcat", [P, B, DST], F32), ("logits", [P, NTILE, NE], F32),
                                ("ident", [P, P], F32), ("b16", [P, 5, P], BF16),
                                ("iota", [P, V + 2 + NE + P], F32)):
            keep[name] = top.enter_context(nc.sbuf_tensor(name, shape, dt))
        features(nc, scratch, keep, x_frames, pw, window, c_dft, c_ident, c_mask, c_iota)
        attention(nc, scratch, keep, x_tok, emb, pb, wq, bq, wk, bk, wv, bv, wo, bo, wr, c_interp, c_rope)
        experts(nc, scratch, keep, wg, wd, out)


def wait_for(eng, sem, value):
    if not isinstance(value, int) or value > 0:
        eng.wait_ge(sem, value)


def features(nc, scratch, keep, x_frames, pw, window, c_dft, c_ident, c_mask, c_iota):
    ctx = ExitStack()
    with ctx:
        def sb(name, shape, dt=F32):
            return ctx.enter_context(nc.sbuf_tensor(name, shape, dt))

        def sem(name):
            return ctx.enter_context(nc.semaphore(name))

        PER = 7
        groups = [(a, min(PER, BF - a)) for a in range(0, BF, PER)]
        W = 2 * NFREQ
        xf_i = sb("xf_i", [NFFT, BF], I32)
        xf = sb("xf", [NFFT, BF])
        iota = keep["iota"][:, 0:V]
        win = sb("win", [NFFT, 1])
        dft = sb("dft", [NFFT, W])
        dftw = sb("dftw", [NFFT, W])
        onehot = sb("onehot", [NFFT, 2, PER, V])
        square = sb("square", [V, 2, PER, W])
        power = sb("power", [V, BF, NFREQ])
        mag = sb("mag", [V, BF, NFREQ])
        pw_sb = sb("pw_sb", [V, NFREQ, DST])
        zT = sb("zT", [DST, BF])
        zero = sb("zero", [P, D])
        masks = sb("masks", [P, 5, P])
        bank = [ctx.enter_context(nc.psum_tensor(f"f_bank{i}", [P, 512], F32)) for i in range(2)]
        zbank = ctx.enter_context(nc.psum_tensor("zbank", [P, 512], F32))
        tbank = [ctx.enter_context(nc.psum_tensor(f"tbank{i}", [P, 512], F32)) for i in range(2)]
        loaded, consts_in, masks_kept = sem("loaded"), sem("consts_in"), sem("masks_kept")
        zero_set, zero_out = sem("zero_set"), sem("zero_out")
        ids_float, window_on = sem("ids_float"), sem("window_on")
        onehot_made, spectrum_done = sem("onehot_made"), sem("spectrum_done")
        squared, powered, mag_done = sem("squared"), sem("powered"), sem("mag_done")
        z_done, z_copied, z_turned, z_kept = sem("z_done"), sem("z_copied"), sem("z_turned"), sem("z_kept")

        with nc.Block() as block:
            @block.sync
            def _(sp):
                for dst, src in ((xf_i[:], x_frames), (keep["iota"][:], c_iota), (win[:], window),
                                 (dft[:], c_dft), (keep["ident"][:], c_ident)):
                    sp.dma_start(dst, src).then_inc(loaded, 16)
                sp.dma_start(masks[:], c_mask).then_inc(consts_in, 16)
                sp.dma_start(pw_sb[:], pw).then_inc(consts_in, 16)
                sp.wait_ge(zero_set, 1)
                sp.dma_start(scratch["yslot"][NSLOT:NSLOT + P, :], zero[:]).then_inc(zero_out, 16)
                sp.wait_ge(zero_out, 16)
                sp.wait_ge(consts_in, 32)

            @block.vector
            def _(dve):
                nc.vector.memset(zero[:], 0.0).then_inc(zero_set, 1)
                dve.wait_ge(loaded, 80)
                nc.vector.tensor_copy(xf[:], xf_i[:]).then_inc(ids_float, 1)
                nc.vector.tensor_scalar(dftw[:], dft[:], win[:, 0:1], None, ALU.mult).then_inc(window_on, 1)
                dve.wait_ge(ids_float, 1)
                for n in range(len(groups) + 1):
                    if n < len(groups):
                        a, k = groups[n]
                        if n >= 2:
                            dve.wait_ge(spectrum_done, n - 1)
                        nc.vector.tensor_tensor(
                            onehot[:, n % 2, 0:k, :],
                            xf[:, a:a + k].unsqueeze(2).to_broadcast([NFFT, k, V]),
                            iota[0:NFFT].unsqueeze(1).to_broadcast([NFFT, k, V]),
                            ALU.is_equal).then_inc(onehot_made, 1)
                    if n >= 1:
                        a, k = groups[n - 1]
                        dve.wait_ge(squared, n)
                        nc.vector.tensor_tensor(power[:, a:a + k, :], square[:, (n - 1) % 2, 0:k, 0:NFREQ],
                                                square[:, (n - 1) % 2, 0:k, NFREQ:W], ALU.add).then_inc(powered, 1)
                dve.wait_ge(consts_in, 32)
                nc.vector.tensor_copy(keep["b16"][:], masks[:]).then_inc(masks_kept, 1)
                dve.wait_ge(z_done, 1)
                nc.vector.tensor_copy(zT[:], zbank[0:DST, 0:BF]).then_inc(z_copied, 1)
                for b in range(B):
                    dve.wait_ge(z_turned, b + 1)
                    nc.vector.tensor_copy(keep["zcat"][V:V + NFRAME, b, :],
                                          tbank[b % 2][0:NFRAME, 0:DST]).then_inc(z_kept, 1)

            @block.scalar
            def _(act):
                for n, (a, k) in enumerate(groups):
                    act.wait_ge(spectrum_done, n + 1)
                    if n >= 2:
                        act.wait_ge(powered, n - 1)
                    nc.scalar.activation(square[:, n % 2, 0:k, :],
                                         bank[n % 2][0:V, 0:k * W].rearrange("p (k w) -> p k w", w=W),
                                         ACT.Square).then_inc(squared, 1)
                act.wait_ge(powered, len(groups))
                nc.scalar.activation(mag[:], power[:], ACT.Sqrt).then_inc(mag_done, 1)

            @block.tensor
            def _(pe):
                pe.wait_ge(window_on, 1)
                for n, (a, k) in enumerate(groups):
                    pe.wait_ge(onehot_made, n + 1)
                    if n >= 2:
                        pe.wait_ge(squared, n - 1)
                    for i in range(k):
                        mm = nc.tensor.matmul(bank[n % 2][0:V, i * W:(i + 1) * W], onehot[:, n % 2, i, :],
                                              dftw[:], start=True, stop=True)
                    mm.then_inc(spectrum_done, 1)
                pe.wait_ge(mag_done, 1)
                pe.wait_ge(consts_in, 32)
                for f in range(NFREQ):
                    mm = nc.tensor.matmul(zbank[0:DST, 0:BF], pw_sb[:, f, :], mag[:, :, f],
                                          start=(f == 0), stop=(f == NFREQ - 1))
                mm.then_inc(z_done, 1)
                pe.wait_ge(z_copied, 1)
                for b in range(B):
                    if b >= 2:
                        pe.wait_ge(z_kept, b - 1)
                    nc.tensor.transpose(tbank[b % 2][0:NFRAME, 0:DST], zT[:, b * NFRAME:(b + 1) * NFRAME],
                                        keep["ident"][0:DST, 0:DST]).then_inc(z_turned, 1)


def attention(nc, scratch, keep, x_tok, emb, pb, wq, bq, wk, bk, wv, bv, wo, bo, wr, c_interp, c_rope):
    ctx = ExitStack()
    with ctx:
        def sb(name, shape, dt=F32):
            return ctx.enter_context(nc.sbuf_tensor(name, shape, dt))

        def sem(name):
            return ctx.enter_context(nc.semaphore(name))

        def psum(name, shape):
            return ctx.enter_context(nc.psum_tensor(name, shape, F32))

        ident = keep["ident"]
        identb, mask_q, mask_k = keep["b16"][:, 0, :], keep["b16"][:, 1, :], keep["b16"][:, 2, :]
        KE = V + NFRAME + 1
        e_lhs = sb("e_lhs", [KE, T])
        ids = e_lhs[0:V, :].bitcast(I32)
        e_rhs = sb("e_rhs", [KE, D])
        iota_p = keep["iota"][:, V:V + 1]
        rope = sb("rope", [P, 2, T])
        wq_sb, wk_sb, wv_sb, wo_sb = (sb(n, [P, 2, D]) for n in ("wq_sb", "wk_sb", "wv_sb", "wo_sb"))
        wr_sb = sb("wr_sb", [P, 2, NE])
        qk_bias = sb("qk_bias", [P, 2, 2])
        bv_sb, bo_sb = sb("bv_sb", [P, D]), sb("bo_sb", [P, D])
        h = sb("h", [P, NT, D])
        hp = sb("hp", [P, NT, D])
        xn = sb("xn", [P, NT, D])
        stats = sb("stats", [P, 2, NT, 6])
        mv = sb("mv", [P, 2, NT, 2])
        var, guess, newton = (sb(n, [P, 2, NT]) for n in ("var", "guess", "newton"))
        rstd = sb("rstd", [P, 2, 2, NT])
        half_bits = sb("half_bits", [P, 2, NT], I32)
        guess_bits = sb("guess_bits", [P, 2, NT], I32)
        xnT = sb("xnT", [P, 2, T])
        qk = sb("qk", [P, 2, 2, T])
        rot = sb("rot", [P, 2, 2, T // 2])
        turned = sb("turned", [P, 2, 2, T // 2])
        parts = sb("parts_sb", [P, 2, 3, 2, T // 2], BF16)
        qs = sb("qs", [P, 2, GH, T], BF16)
        ks = sb("ks", [P, 2, GH, T], BF16)
        vals = sb("vals", [P, NT, NH, VW])
        vnext = sb("vnext", [P, NT, NH, HD])
        probs = sb("probs", [P, 2, GH, T])
        mx = sb("mx", [P, NT, GH])
        mx2 = sb("mx2", [P, NT // 2, GH])
        mparts = sb("mparts", [P, 2, GH, NT], BF16)
        mrest = sb("mrest", [P, NT, GH])
        mT = sb("mT", [2 * GH * NT, P], BF16)
        sums = sb("sums", [P, 2, 512])
        rec = sb("rec", [P, 4, GH, 1])
        attn = sb("attn", [P, NT, D])
        ring = [psum(f"ring{i}", [P, 512]) for i in range(NB)]
        st = [psum(f"st{i}", [P, T]) for i in range(2)]
        pv = psum("pv", [P, 512])

        weights_in, ids_in, set_once, e_ready = sem("weights_in"), sem("ids_in"), sem("set_once"), sem("e_ready")
        ring_filled, ring_freed_act, ring_freed_dve = sem("ring_filled"), sem("ring_freed_act"), sem("ring_freed_dve")
        stats_done, aggr_done, rstd_done, normed = ([sem(f"{n}{i}") for i in range(2)] for n in
                                                    ("stats_done", "aggr_done", "rstd_done", "normed"))
        h_out, hp_in, hp_biased, h2_out, xn2_out = sem("h_out"), sem("hp_in"), sem("hp_biased"), sem("h2_out"), sem("xn2_out")
        rot_dve, rot_pool = sem("rot_dve"), sem("rot_pool")
        parts_out = [sem("q_parts_out"), sem("k_parts_out")]
        stack_in = sem("stack_in")
        st_done, exp_done, pv_done, pv_half, pv_freed = (sem("st_done"), sem("exp_done"), sem("pv_done"),
                                                         sem("pv_half"), sem("pv_freed"))
        max_joined, m_hi, m_diff, m_parts, m_rows = (
            sem("max_joined"), sem("m_hi"), sem("m_diff"), sem("m_parts"), sem("m_rows"))
        rec_done, vals_in = sem("rec_done"), sem("vals_in")

        ROT = 10
        LOADS = 12
        NTILES = NG * TILES_OF_GROUP
        N_W = 13
        block = ctx.enter_context(nc.Block())

        def wait_freed(eng, rg, use):
            act_reads, n = rg.freed(use)
            wait_for(eng, ring_freed_act if act_reads else ring_freed_dve, n)

        def take(pe, rg, use):
            n = rg.at[use]
            if n >= NB:
                wait_freed(pe, rg, rg.uses[n - NB])
            elif n == 0:
                wait_for(pe, ring_freed_act, rg.start[1])
                wait_for(pe, ring_freed_dve, rg.start[2])
            return ring[n % NB]

        def filled(eng, rg, use):
            eng.wait_ge(ring_filled, rg.filled(use))
            return ring[rg.at[use] % NB]

        def rotary(eng, ops, rg, b, i, c, buf, rot_sem, start, n):
            cols = slice(c * 512, (c + 1) * 512)
            x1, x2 = qk[:, i, 0, cols], qk[:, i, 1, cols]
            cos, sin = rope[:, 0, cols], rope[:, 1, cols]
            t1, t2, both = rot[:, buf, 0, :], rot[:, buf, 1, :], rot[:, buf]
            if n == 0:
                wait_freed(eng, rg, ("qk", 4 * i + 2 * c + 1))
            if n not in (1, 4):
                wait_for(eng, rot_sem, start + n)
            if n == 6:
                wait_for(eng, parts_out[i], 96 * (2 * b + c))
            eng.nop(nofuse=True)
            if n == 0:
                ins = ops.tensor_tensor(t1, x1, cos, ALU.mult)
            elif n == 1:
                ins = ops.tensor_tensor(t2, x2, sin, ALU.mult)
            elif n == 2:
                ins = ops.tensor_tensor(turned[:, buf, 0, :], t1, t2, ALU.subtract)
            elif n == 3:
                ins = ops.tensor_tensor(t1, x1, sin, ALU.mult)
            elif n == 4:
                ins = ops.tensor_tensor(t2, x2, cos, ALU.mult)
            elif n == 5:
                ins = ops.tensor_tensor(turned[:, buf, 1, :], t1, t2, ALU.add)
            elif n == 6:
                ins = ops.tensor_copy(parts[:, i, 0], turned[:, buf])
            elif n == 7:
                ins = ops.tensor_tensor(both, turned[:, buf], parts[:, i, 0], ALU.subtract)
            elif n == 8:
                ins = ops.tensor_copy(parts[:, i, 1], both)
            else:
                ins = ops.tensor_tensor(parts[:, i, 2], both, parts[:, i, 1], ALU.subtract)
            ins.then_inc(rot_sem, 1)

        DVE_ROT = [(0, 0), (0, 1), (1, 1)]

        def dve_rotary(dve, rg, b, turn, n):
            i, c = DVE_ROT[turn]
            rotary(dve, nc.vector, rg, b, i, c, 0, rot_dve, ROT * (3 * b + turn), n)

        @block.sync
        def _(sp):
            w_rows = [(w_sb[:], w) for w_sb, w in ((wq_sb, wq), (wk_sb, wk), (wv_sb, wv), (wo_sb, wo), (wr_sb, wr))]
            w_rows += [(qk_bias[:, 0, :], bq), (qk_bias[:, 1, :], bk), (rope[:], c_rope),
                       (bv_sb[:], bv.to_broadcast([P, D])), (bo_sb[:], bo.to_broadcast([P, D])),
                       (e_lhs[V:KE, :], c_interp), (e_rhs[0:V, 0:DEMB], emb),
                       (e_rhs[KE - 1:KE, DEMB:D], pb)]
            sp.wait_ge(set_once, 1)
            for dst, src in w_rows:
                sp.dma_start(dst, src).then_inc(weights_in, 16)

            def rows_of(name, b):
                return scratch[name][bass.ds(b * T, T), :].rearrange("(t p) d -> p t d", p=P)

            def load_ids(rg, b):
                wait_for(sp, ring_filled, rg.start[0])
                sp.nop(nofuse=True)
                sp.dma_start(ids, x_tok[bass.ds(b, 1), :].to_broadcast([V, T])).then_inc(ids_in, 16)

            def store_h(rg, b):
                wait_freed(sp, rg, ("emb", 3))
                sp.nop(nofuse=True)
                sp.dma_start(rows_of("h", b), h[:]).then_inc(h_out, 16)

            def store_parts(b, i, c):
                if (i, c) == (1, 0):
                    sp.wait_ge(rot_pool, ROT * (b + 1))
                else:
                    sp.wait_ge(rot_dve, ROT * (3 * b + DVE_ROT.index((i, c)) + 1))
                sp.nop(nofuse=True)
                for term in range(3):
                    for half in range(2):
                        dst = scratch["parts"][bass.ds(b, 1), i, term, :, half * HALF:(half + 1) * HALF,
                                               c * 512:(c + 1) * 512].rearrange("o h d t -> (o h) d t")
                        sp.dma_start(dst, parts[:, i, term, half, :]).then_inc(parts_out[i], 16)

            def stacks(b, g):
                if g == 0:
                    for i in range(2):
                        sp.wait_ge(parts_out[i], 96 * 2 * (b + 1))
                        sp.nop(nofuse=True)
                wait_for(sp, st_done, b * NTILES + (g - 1) * TILES_OF_GROUP)
                sp.nop(nofuse=True)
                for i, (buf, order) in enumerate(((qs, (0, 0, 1, 1, 0, 2)), (ks, (0, 1, 0, 1, 2, 0)))):
                    for k, term in enumerate(order):
                        src = scratch["parts"][bass.ds(b, 1), i, term, g * GH:(g + 1) * GH, :, :]
                        sp.dma_start(buf[k * HD:(k + 1) * HD, g % 2, :, :],
                                     src.rearrange("o h d t -> d (o h) t")).then_inc(stack_in, 16)

            def shift_rows(rg, g):
                wait_freed(sp, rg, ("mT", g))
                for s in range(2):
                    sp.dma_start(qs[STACK + s:STACK + s + 1, g % 2, :, :], mT[s * 32:(s + 1) * 32, :]).then_inc(m_rows, 16)

            def load_hp(b):
                wait_for(sp, h2_out, 16 * b)
                sp.nop(nofuse=True)
                sp.wait_ge(h_out, 16 * (b + 1))
                sp.nop(nofuse=True)
                sp.dma_start(hp[:], rows_of("h", b)).then_inc(hp_in, 16)

            def store_h2(rg, b):
                wait_freed(sp, rg, ("wo", 3))
                sp.nop(nofuse=True)
                sp.dma_start(rows_of("h2", b), hp[:]).then_inc(h2_out, 16)

            def store_xn2(b):
                sp.wait_ge(normed[1], NT * (b + 1))
                sp.nop(nofuse=True)
                sp.dma_start(rows_of("xn2", b), xn[:]).then_inc(xn2_out, 16)

            def body(b, rg, pre, post):
                stacks(b, 1)
                if pre:
                    load_ids(rg, b + 1)
                if post:
                    load_hp(b - 1)
                if pre:
                    store_h(rg, b + 1)
                shift_rows(rg, 1)
                if post:
                    store_h2(rg, b - 1)
                stacks(b, 2)
                if post:
                    store_xn2(b - 1)
                shift_rows(rg, 2)
                stacks(b, 3)
                if pre:
                    store_parts(b + 1, 0, 0)
                    store_parts(b + 1, 1, 0)
                    store_parts(b + 1, 0, 1)
                shift_rows(rg, 3)
                if pre:
                    store_parts(b + 1, 1, 1)
                    stacks(b + 1, 0)
                    shift_rows(rg, NG)

            rg = Ring("pro")
            load_ids(rg, 0)
            store_h(rg, 0)
            for i, c in ((0, 0), (1, 0), (0, 1), (1, 1)):
                store_parts(0, i, c)
            stacks(0, 0)
            shift_rows(rg, NG)
            body(0, Ring("first"), True, False)
            with sp.Fori(1, B - 1) as b:
                body(b, Ring("mid", b), True, True)
            body(B - 1, Ring("last", B - 1), False, True)
            load_hp(B - 1)
            store_h2(Ring("end"), B - 1)
            store_xn2(B - 1)
            sp.wait_ge(h2_out, 16 * B)
            sp.wait_ge(xn2_out, 16 * B)
            sp.wait_ge(h_out, 16 * B)
            sp.wait_ge(m_rows, 32 * NG * B)
            sp.wait_ge(stack_in, 16 * LOADS * NG * B)

        @block.gpsimd
        def _(pool):
            pool.wait_ge(weights_in, 16 * N_W)

            def copy_values(rg, b, g):
                if rg:
                    wait_freed(pool, rg, ("v", 3))
                wait_for(pool, pv_done, (b - 1) * STEPS + (g + 1) * NSTEP)
                pool.nop(nofuse=True)
                nc.gpsimd.tensor_copy(vals[:, :, g * GH:(g + 1) * GH, 0:HD],
                                      vnext[:, :, g * GH:(g + 1) * GH, :]).then_inc(vals_in, 1)

            def turn_k(rg, b):
                for n in range(ROT):
                    rotary(pool, nc.gpsimd, rg, b, 1, 0, 1, rot_pool, ROT * b, n)

            def add_bias(b):
                pool.wait_ge(hp_in, 16 * (b + 1))
                nc.gpsimd.tensor_tensor(hp[:], hp[:], bo_sb[:].unsqueeze(1).to_broadcast([P, NT, D]),
                                        ALU.add).then_inc(hp_biased, 1)

            def body(b, rg, pre, post):
                if post:
                    copy_values(None, b, 3)
                    add_bias(b - 1)
                if pre:
                    turn_k(rg, b + 1)
                    for g in range(3):
                        copy_values(rg, b + 1, g)

            pool.wait_ge(set_once, 4)
            turn_k(Ring("pro"), 0)
            for g in range(NG):
                copy_values(Ring("pro"), 0, g)
            body(0, Ring("first"), True, False)
            with pool.Fori(1, B - 1) as b:
                body(b, Ring("mid", b), True, True)
            body(B - 1, Ring("last", B - 1), False, True)
            add_bias(B - 1)

        @block.scalar
        def _(act):
            def evac(rg, use, b):
                name, k = use
                src = filled(act, rg, use)[:]
                if name == "emb":
                    if k == 0:
                        wait_for(act, h_out, 16 * b)
                        wait_for(act, stats_done[0], NT * b)
                        wait_for(act, normed[0], NT * b)
                    nc.scalar.activation(h[:, 2 * k:2 * k + 2, :].rearrange("p t d -> p (t d)"), src,
                                         ACT.Copy).then_inc(ring_freed_act, 1)
                elif name == "qk":
                    i, c, half = k // 4, k // 2 % 2, k % 2
                    nc.scalar.activation(qk[:, i, half, c * 512:(c + 1) * 512], src, ACT.Identity,
                                         bias=qk_bias[:, i, half:half + 1]).then_inc(ring_freed_act, 1)
                else:
                    nc.scalar.activation(xnT[:, :, 256 * k:256 * (k + 1)], src.rearrange("p (c t) -> p c t", c=2),
                                         ACT.Copy).then_inc(ring_freed_act, 1)

            def exps(b, s, k, done):
                t = s % NSTEP
                act.wait_ge(st_done, b * NTILES + done + 1)
                if k == 0:
                    wait_for(act, pv_done, b * STEPS + s - 1)
                dst = probs[:, s % 2, k, :] if t < NSTEP - 1 else probs[:, s % 2, 2 * k:2 * k + 2, 0:512]
                src = st[done % 2][:] if t < NSTEP - 1 else st[done % 2][:].rearrange("p (h q) -> p h q", h=2)
                nc.scalar.activation(dst, src, ACT.Exp, scale=SCALE).then_inc(exp_done, 1)

            def copy_sums(b, g, half):
                if g < 0:
                    b, g = b - 1, NG - 1
                if half == 0:
                    act.wait_ge(pv_half, b * NG + g + 1)
                else:
                    act.wait_ge(pv_done, b * STEPS + (g + 1) * NSTEP)
                wait_for(act, rec_done, 2 * NG * b + 2 * g + half - 1)
                nc.scalar.activation(sums[:, half, :], pv[:], ACT.Copy).then_inc(pv_freed, 1)

            def body(b, rg, pre, post):
                done = 0
                for s in range(STEPS):
                    for k in range(TILES_OF_STEP[s % NSTEP]):
                        exps(b, s, k, done)
                        done += 1
                        if k == 1:
                            for g, half in copied_in(s, post):
                                copy_sums(b, g, half)
                        for use in extra_uses(s, k, pre, post):
                            if by_act(use):
                                evac(rg, use, b + 1 if (s, k) in PRE_USES else b - 1)

            act.wait_ge(weights_in, 16 * N_W)
            rg = Ring("pro")
            for name in ("emb", "xT"):
                for k in range(4):
                    evac(rg, (name, k), 0)
            for k in QK_ORDER:
                evac(rg, ("qk", k), 0)
            body(0, Ring("first"), True, False)
            with act.Fori(1, B - 1) as b:
                body(b, Ring("mid", b), True, True)
            body(B - 1, Ring("last", B - 1), False, True)
            copy_sums(B, -1, 1)
            rg = Ring("end")
            for name in ("aT", "x2T"):
                for k in range(4):
                    evac(rg, (name, k), B - 1)

        @block.vector
        def _(dve):
            nc.vector.memset(e_rhs[:], 0.0).then_inc(set_once, 1)
            nc.vector.memset(ks[STACK:STACK + 32, :, :, :], -1.0).then_inc(set_once, 1)
            nc.vector.memset(vals[:], 0.0).then_inc(set_once, 1)
            dve.wait_ge(set_once, 3)
            nc.vector.memset(vals[:, :, :, HD:HD + 1], 1.0).then_inc(set_once, 1)
            dve.wait_ge(weights_in, 16 * N_W)

            def norm_stats(rg, b, f, tiles):
                for t in tiles:
                    wait_freed(dve, rg, (("emb", "wo")[f], t // 2))
                    nc.vector.bn_stats(stats[:, f, t, :], (h, hp)[f][:, t, :]).then_inc(stats_done[f], 1)

            def deviation(b, f):
                dve.wait_ge(stats_done[f], NT * (b + 1))
                wait_for(dve, normed[f], NT * b)
                dve.nop(nofuse=True)
                for t in range(NT):
                    nc.vector.bn_aggr(mv[:, f, t, :], stats[:, f, t, :]).then_inc(aggr_done[f], 1)
                dve.wait_ge(aggr_done[f], NT * (b + 1))
                n = 12 * b

                def step(ins):
                    ins.then_inc(rstd_done[f], 1)
                step(nc.vector.tensor_scalar(var[:, f], mv[:, f, :, 1], EPS, None, ALU.add))
                dve.wait_ge(rstd_done[f], n + 1)
                step(nc.vector.tensor_scalar(half_bits[:, f], var[:, f].bitcast(I32), 1, None, ALU.arith_shift_right))
                dve.wait_ge(rstd_done[f], n + 2)
                step(nc.vector.tensor_scalar(guess_bits[:, f], half_bits[:, f], -1.0, float(0x5F3759DF),
                                             ALU.mult, ALU.add))
                dve.wait_ge(rstd_done[f], n + 3)
                y = guess_bits[:, f].bitcast(F32)
                for r in range(3):
                    step(nc.vector.tensor_tensor(newton[:, f], y, y, ALU.mult))
                    dve.wait_ge(rstd_done[f], n + 3 * r + 4)
                    step(nc.vector.scalar_tensor_tensor(guess[:, f], newton[:, f], -0.5, var[:, f], ALU.mult, ALU.mult))
                    dve.wait_ge(rstd_done[f], n + 3 * r + 5)
                    step(nc.vector.scalar_tensor_tensor(rstd[:, f, r % 2], guess[:, f], 1.5, y, ALU.add, ALU.mult))
                    dve.wait_ge(rstd_done[f], n + 3 * r + 6)
                    y = rstd[:, f, r % 2]

            def normalise(rg, b, f, tiles):
                if tiles[0] == 0:
                    if f == 0:
                        wait_for(dve, xn2_out, 16 * (b - 1))
                    else:
                        wait_for(dve, ring_filled, rg.start[0])
                for t in tiles:
                    nc.vector.tensor_scalar(xn[:, t, :], (h, hp)[f][:, t, :], mv[:, f, t, 0:1], rstd[:, f, 0, t:t + 1],
                                            ALU.subtract, ALU.mult).then_inc(normed[f], 1)

            def embedding_operands(b):
                dve.wait_ge(ids_in, 16 * (b + 1))
                nc.vector.tensor_scalar(e_lhs[0:V, :], ids, iota_p[0:V], None, ALU.is_equal).then_inc(e_ready, 1)
                nc.vector.tensor_copy(e_rhs[V:V + NFRAME, DEMB:D],
                                      keep["zcat"][V:V + NFRAME, bass.ds(b, 1), :].rearrange("p b d -> p (b d)")
                                      ).then_inc(e_ready, 1)

            def maxima(rg, g, m):
                i, k0, w, heads, part = MAXB[m]
                src = filled(dve, rg, ("max", g, m))[:, 0:w * len(heads)].rearrange("p (h k) -> p h k", k=w)
                dst = mx[:, i, heads[0]:heads[-1] + 1] if part == 0 else mx2[:, i - 4, heads[0]:heads[-1] + 1]
                nc.vector.tensor_reduce(dst, src, AX.X, ALU.max).then_inc(ring_freed_dve, 1)

            def shift(rg, b, g):
                at = NG * b + g + 1
                wait_freed(dve, rg, ("max", g, len(MAXB) - 1))
                nc.vector.tensor_tensor(mx[:, 4:8, :], mx[:, 4:8, :], mx2[:], ALU.max).then_inc(max_joined, 1)
                dve.wait_ge(max_joined, at)
                nc.vector.tensor_copy(mparts[:, 0].rearrange("p h i -> p i h"), mx[:]).then_inc(m_hi, 1)
                dve.wait_ge(m_hi, at)
                nc.vector.tensor_tensor(mrest[:], mx[:], mparts[:, 0].rearrange("p h i -> p i h"),
                                        ALU.subtract).then_inc(m_diff, 1)
                dve.wait_ge(m_diff, at)
                nc.vector.tensor_copy(mparts[:, 1].rearrange("p h i -> p i h"), mrest[:]).then_inc(m_parts, 1)
                bank = filled(dve, rg, ("mT", g))
                wait_for(dve, m_rows, 32 * (NG * b + g))
                nc.vector.tensor_copy(mT[:], bank[0:64, 0:64].bitcast(BF16)).then_inc(ring_freed_dve, 1)

            def scale_half(rg, b, g, half):
                src = filled(dve, rg, ("turn", g, half))[:].rearrange("p (t h v) -> p t h v", t=4, h=GH)
                if g < 0:
                    b, g = b - 1, NG - 1
                n = rg.at[("turn", g, half)] if ("turn", g, half) in rg.at else rg.at[("turn", -1, 1)]
                wait_for(dve, ring_freed_dve, rg.start[2] + counts(rg.uses[:n])[2])
                nc.vector.reciprocal(rec[:], src[:, :, :, HD:HD + 1]).then_inc(rec_done, 1)
                dve.wait_ge(rec_done, 2 * NG * b + 2 * g + half + 1)
                dst = attn[:, 4 * half:4 * half + 4, g * GH * HD:(g + 1) * GH * HD]
                nc.vector.tensor_tensor(dst.rearrange("p t (h v) -> p t h v", h=GH), src[:, :, :, 0:HD],
                                        rec[:].to_broadcast([P, 4, GH, HD]), ALU.mult).then_inc(ring_freed_dve, 1)

            def read(rg, use, b):
                name, k = use
                bank = filled(dve, rg, use)
                if name == "v":
                    if k == 0:
                        wait_for(dve, vals_in, NG * b)
                    nc.vector.tensor_tensor(vnext[:, 2 * k:2 * k + 2], bank[:].rearrange("p (t h v) -> p t h v", t=2, h=NH),
                                            bv_sb[:].rearrange("p (h v) -> p h v", h=NH).unsqueeze(1)
                                            .to_broadcast([P, 2, NH, HD]), ALU.add).then_inc(ring_freed_dve, 1)
                elif name == "wo":
                    if k == 0:
                        dve.wait_ge(hp_biased, b + 1)
                    nc.vector.tensor_tensor(hp[:, 2 * k:2 * k + 2, :], bank[:].rearrange("p (t d) -> p t d", t=2),
                                            hp[:, 2 * k:2 * k + 2, :], ALU.add).then_inc(ring_freed_dve, 1)
                else:
                    nc.vector.tensor_copy(keep["logits"][:, bass.ds(b * NT, NT), :].rearrange("p t e -> p (t e)"),
                                          bank[:, 0:NT * NE]).then_inc(ring_freed_dve, 1)

            def between(rg, b, s, k, pre, post):
                if pre:
                    if (s, k) == (0, 3):
                        embedding_operands(b + 1)
                    if s == 2:
                        norm_stats(rg, b + 1, 0, (2 * k, 2 * k + 1))
                    if (s, k) == (3, 3):
                        deviation(b + 1, 0)
                    if (s, k) in ((7, 2), (7, 3)):
                        normalise(rg, b + 1, 0, range(4 * (k - 2), 4 * (k - 1)))
                    n = sum(TILES_OF_STEP[x % NSTEP] for x in range(10, s)) + k - 2
                    if s >= 10 and 0 <= n < 15:
                        for m in (2 * n, 2 * n + 1):
                            dve_rotary(dve, rg, b + 1, m // ROT, m % ROT)
                if post:
                    if s == 4:
                        norm_stats(rg, b - 1, 1, range(4 * k, 4 * k + 4))
                    if (s, k) == (5, 0):
                        deviation(b - 1, 1)
                    if (s, k) in ((5, 1), (5, 2)):
                        normalise(rg, b - 1, 1, range(4 * (k - 1), 4 * k))

            def body(b, rg, pre, post):
                for s in range(STEPS):
                    for k in range(TILES_OF_STEP[s % NSTEP]):
                        g, ms = max_range(s, k, pre)
                        for m in ms:
                            maxima(rg, g, m)
                        for use in extra_uses(s, k, pre, post):
                            if not by_act(use):
                                read(rg, use, b + 1 if (s, k) in PRE_USES else b - 1)
                        between(rg, b, s, k, pre, post)
                    if max_turned(s, pre) is not None:
                        shift(rg, b, max_turned(s, pre))
                    for g, half in turns_of(s, post):
                        scale_half(rg, b, g, half)

            rg = Ring("pro")
            embedding_operands(0)
            norm_stats(rg, 0, 0, range(NT))
            deviation(0, 0)
            normalise(rg, 0, 0, range(NT))
            for n in range(2 * ROT):
                dve_rotary(dve, rg, 0, n // ROT, n % ROT)
            for k in range(4):
                read(rg, ("v", k), 0)
            for n in range(2 * ROT, 3 * ROT):
                dve_rotary(dve, rg, 0, n // ROT, n % ROT)
            for m in range(len(MAXB)):
                maxima(rg, NG, m)
            shift(rg, -1, NG)
            body(0, Ring("first"), True, False)
            with dve.Fori(1, B - 1) as b:
                body(b, Ring("mid", b), True, True)
            body(B - 1, Ring("last", B - 1), False, True)
            rg = Ring("end")
            scale_half(rg, B, -1, 1)
            for k in range(4):
                read(rg, ("wo", k), B - 1)
            norm_stats(rg, B - 1, 1, range(NT))
            deviation(B - 1, 1)
            normalise(rg, B - 1, 1, range(NT))
            read(rg, ("logit", 0), B - 1)

        @block.tensor
        def _(pe):
            pe.wait_ge(weights_in, 16 * N_W)
            pe.wait_ge(set_once, 4)

            def turn_rows(bank, k, src):
                for c in range(2):
                    for u in range(2):
                        mm = nc.tensor.transpose(bank[:, (2 * c + u) * P:(2 * c + u + 1) * P],
                                                 src[:, 2 * k + u, c * P:(c + 1) * P], ident[:])
                return mm

            def rows_product(bank, k, w_sb):
                for u in range(2):
                    t = 2 * k + u
                    for c in range(2):
                        mm = nc.tensor.matmul(bank[:, u * D:(u + 1) * D], xnT[:, c, t * P:(t + 1) * P],
                                              w_sb[:, c, :], start=(c == 0), stop=(c == 1))
                return mm

            def extra(rg, use, b):
                name, k = use
                bank = take(pe, rg, use)
                if name == "emb":
                    if k == 0:
                        pe.wait_ge(e_ready, 2 * (b + 1))
                    for u in range(2):
                        t = 2 * k + u
                        mm = nc.tensor.matmul(bank[:, u * D:(u + 1) * D], e_lhs[:, t * P:(t + 1) * P], e_rhs[:],
                                              start=True, stop=True)
                elif name in ("xT", "x2T"):
                    pe.wait_ge(normed[0 if name == "xT" else 1], NT * b + 2 * k + 2)
                    mm = turn_rows(bank, k, xn)
                elif name == "aT":
                    if k == 0:
                        wait_freed(pe, rg, ("turn", -1, 1))
                    mm = turn_rows(bank, k, attn)
                elif name == "qk":
                    i, c, half = k // 4, k // 2 % 2, k % 2
                    if k == QK_ORDER[0]:
                        wait_freed(pe, rg, ("xT", 3))
                    for ch in range(2):
                        mm = nc.tensor.matmul(bank[:], (wq_sb, wk_sb)[i][:, ch, half * P:(half + 1) * P],
                                              xnT[:, ch, c * 512:(c + 1) * 512], start=(ch == 0), stop=(ch == 1))
                elif name == "v":
                    mm = rows_product(bank, k, wv_sb)
                elif name == "wo":
                    wait_freed(pe, rg, ("aT", k))
                    mm = rows_product(bank, k, wo_sb)
                else:
                    wait_freed(pe, rg, ("x2T", 3))
                    for t in range(NT):
                        for c in range(2):
                            mm = nc.tensor.matmul(bank[:, t * NE:(t + 1) * NE], xnT[:, c, t * P:(t + 1) * P],
                                                  wr_sb[:, c, :], start=(c == 0), stop=(c == 1))
                mm.then_inc(ring_filled, 1)

            def max_bank(rg, b, g, m):
                i, k0, w, heads, part = MAXB[m]
                bank = take(pe, rg, ("max", g, m))
                if m == 0:
                    pe.wait_ge(stack_in, 16 * LOADS * (NG * b + g + 1))
                diag = P * i if P * i >= k0 and P * (i + 1) <= k0 + w else None
                for n, h_ in enumerate(heads):
                    mm = nc.tensor.matmul(bank[:, n * w:(n + 1) * w], qs[0:STACK, g % 2, h_, P * i:P * (i + 1)],
                                          ks[0:STACK, g % 2, h_, k0:k0 + w], start=True, stop=(diag is None))
                    if diag is not None:
                        o = n * w + diag - k0
                        mm = nc.tensor.matmul(bank[:, o:o + P], identb, mask_q, start=False, stop=True)
                mm.then_inc(ring_filled, 1)

            def max_turn(rg, b, g):
                bank = take(pe, rg, ("mT", g))
                pe.wait_ge(m_parts, NG * b + g + 1)
                pe.nop(nofuse=True)
                nc.tensor.transpose(bank[0:64, 0:64].bitcast(BF16), mparts[:].rearrange("p s h i -> p (s h i)"),
                                    identb).then_inc(ring_filled, 1)

            def score_tile(b, s, k, done):
                g, t = divmod(s, NSTEP)
                if t == 0 and k == 0:
                    pe.wait_ge(m_rows, 32 * (NG * b + g + 1))
                wait_for(pe, exp_done, b * NTILES + done - 1)
                tile = st[done % 2]
                for h_ in ([k] if t < NSTEP - 1 else [2 * k, 2 * k + 1]):
                    o = 0 if t < NSTEP - 1 else 512 * (h_ % 2)
                    for (half, j, col) in HEAD_TILES[t]:
                        q0, w = piece_range(half, j)
                        diag = j // 4 == half
                        mm = nc.tensor.matmul(tile[:, o + col:o + col + w], ks[0:STACK + 2, g % 2, h_, P * j:P * (j + 1)],
                                              qs[0:STACK + 2, g % 2, h_, q0:q0 + w], start=True, stop=not diag)
                        if diag:
                            mm = nc.tensor.matmul(tile[:, o + col:o + col + P], identb, mask_k, start=False, stop=True)
                mm.then_inc(st_done, 1)

            def sum_pieces(s, half):
                g, t = divmod(s, NSTEP)
                for (hf, j, col) in PV_ORDER[t][half]:
                    q0, w = piece_range(hf, j)
                    q0 -= 512 * hf
                    first, last = (j == 0), (j == (2 if hf == 0 else 7))
                    for h_ in range(GH):
                        mm = nc.tensor.matmul(pv[32 * h_:32 * h_ + VW, q0:q0 + w],
                                              vals[:, j, g * GH + h_, :], probs[:, s % 2, h_, col:col + w],
                                              start=first, stop=last)
                return mm

            def sum_step(b, s, part):
                g, t = divmod(s, NSTEP)
                if part == 0:
                    pe.wait_ge(exp_done, b * NTILES + TILES_OF_GROUP * g + sum(TILES_OF_STEP[:t + 1]))
                    if t == 0:
                        pe.wait_ge(vals_in, NG * b + g + 1)
                        wait_for(pe, pv_freed, 2 * NG * b + 2 * g)
                    if PV_ORDER[t][0]:
                        sum_pieces(s, 0).then_inc(pv_half if t == 1 else pv_done, 1)
                elif PV_ORDER[t][1]:
                    if t == 1:
                        pe.wait_ge(pv_freed, 2 * NG * b + 2 * g + 1)
                    sum_pieces(s, 1).then_inc(pv_done, 1)

            def turn_half(rg, b, g, half):
                bank = take(pe, rg, ("turn", g, half))
                if g < 0:
                    b, g = b - 1, NG - 1
                pe.wait_ge(pv_freed, 2 * NG * b + 2 * g + half + 1)
                for t in range(4):
                    mm = nc.tensor.transpose(bank[:, t * P:(t + 1) * P], sums[:, half, t * P:(t + 1) * P], ident[:])
                mm.then_inc(ring_filled, 1)

            def body(b, rg, pre, post):
                done = 0
                for s in range(STEPS):
                    tiles = TILES_OF_STEP[s % NSTEP]
                    for k in range(tiles):
                        score_tile(b, s, k, done)
                        done += 1
                        g, ms = max_range(s, k, pre)
                        for m in ms:
                            max_bank(rg, b, g, m)
                        for use in extra_uses(s, k, pre, post):
                            extra(rg, use, b + 1 if (s, k) in PRE_USES else b - 1)
                        if s >= 1 or post:
                            at = (b, s - 1) if s else (b - 1, STEPS - 1)
                            if k == 1:
                                sum_step(*at, 0)
                            if k == (2 if tiles > 2 else 1):
                                sum_step(*at, 1)
                    if max_turned(s, pre) is not None:
                        max_turn(rg, b, max_turned(s, pre))
                    for g, half in turns_of(s, post):
                        turn_half(rg, b, g, half)

            rg = Ring("pro")
            for name in ("emb", "xT"):
                for k in range(4):
                    extra(rg, (name, k), 0)
            for k in QK_ORDER:
                extra(rg, ("qk", k), 0)
            for k in range(4):
                extra(rg, ("v", k), 0)
            for m in range(len(MAXB)):
                max_bank(rg, -1, NG, m)
            max_turn(rg, -1, NG)
            body(0, Ring("first"), True, False)
            with pe.Fori(1, B - 1) as b:
                body(b, Ring("mid", b), True, True)
            body(B - 1, Ring("last", B - 1), False, True)
            rg = Ring("end")
            for part in range(2):
                sum_step(B - 1, STEPS - 1, part)
            turn_half(rg, B, -1, 1)
            for name, n in (("aT", 4), ("wo", 4), ("x2T", 4), ("logit", 1)):
                for k in range(n):
                    extra(rg, (name, k), B - 1)


def experts(nc, scratch, keep, wg, wd, out):
    ctx = ExitStack()
    with ctx:
        def sb(name, shape, dt=F32):
            return ctx.enter_context(nc.sbuf_tensor(name, shape, dt))

        def sem(name):
            return ctx.enter_context(nc.semaphore(name))

        def psum(name):
            return ctx.enter_context(nc.psum_tensor(name, [P, 512], F32))

        N = NTILE
        logits = keep["logits"]
        route = {n: sb("r_" + n, [P, N, NE]) for n in
                 ("l", "g", "t", "eq", "sel", "pre", "pos", "ex", "ex2", "first", "second", "e")}
        one = {n: sb("o_" + n, [P, N]) for n in ("mx", "sum", "rs", "n0", "v2", "need", "va", "vb", "wden")}
        slot_f = sb("slot_f", [P, N, 2])
        slot = sb("slot", [P, N, 2], I32)
        weight = sb("weight", [P, N, 2])
        selb = sb("selb", [P, N, NE], BF16)
        spare = keep["iota"][:, V + 1:V + 2]
        ecap = keep["iota"][:, V + 2:V + 2 + NE]
        NC = NSLOT // P
        TG = 8
        slot_hl = sb("slot_hl", [P, 2, N, 2], I32)
        slot_hlf = sb("slot_hlf", [P, 2, N, 2])
        place_hot = sb("place_hot", [P, 2, TG, 2, P], BF16)
        tile_hot = sb("tile_hot", [P, 2, TG, 2, 3, NC], BF16)
        token_f = sb("token_f", [P, 2, NC])
        token = sb("token", [P, NC], I32)
        c_rows = keep["iota"][:, V + 2 + NE:V + 2 + NE + P]
        NX = 4
        idx = sb("idx", [P, NX, 2], I32)
        NXS = 5
        xidx = sb("xidx", [P, NXS, 2], I32)
        wg_sb = sb("wg_sb", [P, 2, HID])
        wd_sb = sb("wd_sb", [P, 2, 4, D])
        UN = 2
        NU = CAP // (UN * P)
        xs = sb("xs", [P, NXS, UN, D])
        xT = sb("xT", [P, 2, 2, UN * P])
        eneg = sb("eneg", [P, 2, 2, 512])
        hT = sb("hT", [P, 2, 4, UN * P])
        ys = sb("ys", [P, 2, UN * D])
        ya = sb("ya", [P, NX, D])
        yb = sb("yb", [P, NX, D])
        hh = sb("hh", [P, NX, D])
        oo = sb("oo", [P, NX, D])
        wcol = sb("wcol", [P, NX, 2])
        tb = [psum(f"tb{i}") for i in range(2)]
        hbk = [psum(f"hbk{i}") for i in range(4)]
        yb_ = [psum(f"ybk{i}") for i in range(2)]

        w_in, tri_done, route_step = sem("w_in"), sem("tri_done"), sem("route_step")
        exp_out = sem("exp_out")
        hot_made, hot_used = sem("hot_made"), sem("hot_used")
        idx_set = sem("idx_set")
        wd_in = [sem(f"wd_in{i}") for i in range(2)]
        xs_in = [sem(f"xs_in{i}") for i in range(NXS)]
        x_turned, xT_made, hid_done, e_done, r_done, h_made = (sem("x_turned"), sem("xT_made"), sem("hid_done"),
                                                              sem("e_done"), sem("r_done"), sem("h_made"))
        d_done = sem("d_done")
        y_done, y_copied = sem("y_done"), sem("y_copied")
        y_out = [sem(f"y_out{i}") for i in range(2)]
        gidx_set = sem("gidx_set")
        ya_in = [sem(f"ya_in{i}") for i in range(NX)]
        hh_in = [sem(f"hh_in{i}") for i in range(NX)]
        mixed, half_mixed, wcol_set = sem("mixed"), sem("half_mixed"), sem("wcol_set")
        o_out = [sem(f"o_out{i}") for i in range(NX)]

        count = [0]
        marks = {}
        block = ctx.enter_context(nc.Block())
        n_units = NE * NU

        def copy_out(act, pair, m):
            n = pair * (2 * NU) + m
            act.wait_ge(y_done, n + 1)
            wait_for(act, y_out[m % 2], 16 * (pair * NU + m // 2))
            nc.scalar.activation(ys[:, m % 2, :], yb_[m % 2][:], ACT.Copy).then_inc(y_copied, 1)

        def store_y(sp, pair, m):
            n = pair * (2 * NU) + m
            wait_for(sp, y_copied, n + 1)
            sp.dma_start(scratch["yslot"][bass.ds(n * UN * P, UN * P), :].rearrange("(t p) d -> p t d", p=P),
                         ys[:, m % 2, :].rearrange("p (t d) -> p t d", t=UN)).then_inc(y_out[m % 2], 16)

        @block.vector
        def _(dve):
            def step(ins):
                count[0] += 1
                ins.then_inc(route_step, 1)
                dve.wait_ge(route_step, count[0])

            def wide(a):
                return a[:].unsqueeze(2).to_broadcast([P, N, NE])
            v = nc.vector
            r, o = route, one
            dve.wait_ge(w_in, 16)
            step(v.tensor_reduce(o["mx"][:], logits[:], AX.X, ALU.max))
            step(v.tensor_tensor(r["l"][:], logits[:], wide(o["mx"]), ALU.subtract))
            step(v.tensor_scalar(r["l"][:], r["l"][:], -87.33654, None, ALU.max))
            marks["logits"] = count[0]
            step(v.tensor_scalar(r["eq"][:], r["l"][:], 0.0, None, ALU.is_equal))
            step(v.tensor_reduce(o["n0"][:], r["eq"][:], AX.X, ALU.add))
            step(v.scalar_tensor_tensor(r["t"][:], r["eq"][:], -1e4, r["l"][:], ALU.mult, ALU.add))
            step(v.tensor_reduce(o["v2"][:], r["t"][:], AX.X, ALU.max))
            step(v.tensor_scalar(o["n0"][:], o["n0"][:], 1.5, None, ALU.is_lt))
            step(v.tensor_tensor(o["v2"][:], o["v2"][:], o["n0"][:], ALU.mult))
            step(v.tensor_tensor(r["t"][:], r["l"][:], wide(o["v2"]), ALU.is_gt))
            step(v.tensor_reduce(o["need"][:], r["t"][:], AX.X, ALU.add))
            step(v.tensor_scalar(o["need"][:], o["need"][:], -1.0, 2.0, ALU.mult, ALU.add))
            step(v.tensor_tensor(r["eq"][:], r["l"][:], wide(o["v2"]), ALU.is_equal))

            def before(dst, src):
                step(v.memset(dst[:, :, 0:1], 0.0))
                for e in range(1, NE):
                    step(v.tensor_tensor(dst[:, :, e:e + 1], dst[:, :, e - 1:e], src[:, :, e - 1:e], ALU.add))
            before(r["pre"], r["eq"])
            step(v.tensor_tensor(r["pre"][:], r["pre"][:], wide(o["need"]), ALU.is_lt))
            step(v.tensor_tensor(r["eq"][:], r["eq"][:], r["pre"][:], ALU.mult))
            step(v.tensor_tensor(r["sel"][:], r["eq"][:], r["t"][:], ALU.add))
            step(v.tensor_copy(selb[:], r["sel"][:]))
            marks["chosen"] = count[0]
            before(r["pre"], r["sel"])
            step(v.tensor_scalar(r["first"][:], r["pre"][:], 0.5, None, ALU.is_lt))
            step(v.tensor_tensor(r["first"][:], r["first"][:], r["sel"][:], ALU.mult))
            step(v.tensor_tensor(r["second"][:], r["sel"][:], r["first"][:], ALU.subtract))
            dve.wait_ge(exp_out, 1)
            step(v.tensor_reduce(o["sum"][:], r["e"][:], AX.X, ALU.add))
            step(v.reciprocal(o["rs"][:], o["sum"][:]))
            step(v.tensor_tensor(r["g"][:], r["e"][:], wide(o["rs"]), ALU.mult))
            dve.wait_ge(tri_done, 2)
            step(v.memset(r["ex"][:, 0:1, :], 0.0))
            step(v.tensor_copy(r["ex"][:, 1:N, :], tb[1][:].rearrange("p (t e) -> p t e", e=NE)[:, 0:N - 1, :]))
            a, c = r["ex"], r["ex2"]
            reach = 1
            while reach < N:
                step(v.tensor_copy(c[:, 0:reach, :], a[:, 0:reach, :]))
                step(v.tensor_tensor(c[:, reach:N, :], a[:, reach:N, :], a[:, 0:N - reach, :], ALU.add))
                a, c = c, a
                reach *= 2
            step(v.scalar_tensor_tensor(r["pos"][:], tb[0][:].rearrange("p (t e) -> p t e", e=NE), -1.0, a[:],
                                        ALU.add, ALU.add))
            keep_ = r["eq"]
            step(v.tensor_scalar(keep_[:], r["pos"][:], CAP - 0.5, None, ALU.is_lt))
            step(v.tensor_tensor(r["pos"][:], r["pos"][:], ecap.unsqueeze(1).to_broadcast([P, N, NE]), ALU.add))
            for k, (name, valid) in enumerate((("first", "va"), ("second", "vb"))):
                step(v.tensor_tensor(r["t"][:], r[name][:], keep_[:], ALU.mult))
                step(v.tensor_reduce(o[valid][:], r["t"][:], AX.X, ALU.add))
                step(v.tensor_tensor(r["e"][:], r["t"][:], r["pos"][:], ALU.mult))
                step(v.tensor_reduce(slot_f[:, :, k], r["e"][:], AX.X, ALU.add))
                step(v.tensor_scalar(o[valid][:], o[valid][:], -1.0, 1.0, ALU.mult, ALU.add))
                step(v.tensor_scalar(o[valid][:], o[valid][:], spare, None, ALU.mult))
                step(v.tensor_tensor(slot_f[:, :, k], slot_f[:, :, k], o[valid][:], ALU.add))
                step(v.tensor_tensor(r["e"][:], r["t"][:], r["g"][:], ALU.mult))
                step(v.tensor_reduce(weight[:, :, k], r["e"][:], AX.X, ALU.add))
            step(v.tensor_copy(slot[:], slot_f[:]))
            step(v.tensor_tensor(o["wden"][:], weight[:, :, 0], weight[:, :, 1], ALU.add))
            step(v.tensor_scalar(o["wden"][:], o["wden"][:], 1e-6, None, ALU.add))
            step(v.reciprocal(o["wden"][:], o["wden"][:]))
            step(v.tensor_tensor(weight[:], weight[:], o["wden"][:].unsqueeze(2).to_broadcast([P, N, 2]), ALU.mult))
            marks["slots"] = count[0]

            step(v.tensor_scalar(slot_hl[:, 0], slot[:], 7, None, ALU.arith_shift_right))
            step(v.tensor_scalar(slot_hl[:, 1], slot[:], P - 1, None, ALU.bitwise_and))
            step(v.tensor_copy(slot_hlf[:], slot_hl[:]))
            for gr in range(N // TG):
                ts = slice(gr * TG, (gr + 1) * TG)
                if gr >= 2:
                    dve.wait_ge(hot_used, gr - 1)
                v.tensor_tensor(place_hot[:, gr % 2], slot_hlf[:, 1, ts, :].unsqueeze(3).to_broadcast([P, TG, 2, P]),
                                c_rows.unsqueeze(1).unsqueeze(1).to_broadcast([P, TG, 2, P]),
                                ALU.is_equal).then_inc(hot_made, 1)
                hot = tile_hot[:, gr % 2]
                step(v.tensor_tensor(hot[:, :, :, 0, :], slot_hlf[:, 0, ts, :].unsqueeze(3).to_broadcast([P, TG, 2, NC]),
                                     c_rows[:, 0:NC].unsqueeze(1).unsqueeze(1).to_broadcast([P, TG, 2, NC]),
                                     ALU.is_equal))
                v.tensor_scalar(hot[:, :, :, 1, :], hot[:, :, :, 0, :], keep["iota"][:, V:V + 1], None,
                                ALU.mult).then_inc(hot_made, 1)
                v.tensor_tensor(hot[:, :, :, 2, :], hot[:, :, :, 0, :],
                                c_rows[:, ts].unsqueeze(2).unsqueeze(3).to_broadcast([P, TG, 2, NC]),
                                ALU.mult).then_inc(hot_made, 1)
            dve.wait_ge(hot_used, N // TG)
            sums = hbk[0][:, 0:2 * NC].rearrange("p (k c) -> p k c", k=2)
            step(v.tensor_scalar(token_f[:, 1, :], sums[:, 1, :], float(P), None, ALU.mult))
            step(v.tensor_tensor(token_f[:, 0, :], sums[:, 0, :], token_f[:, 1, :], ALU.add))
            step(v.tensor_copy(token[:], token_f[:, 0, :]))
            marks["tokens"] = count[0]

            def expert_pair(pair):
                for m in range(2 * NU):
                    n = pair * (2 * NU) + m
                    wait_for(dve, x_turned, n + 1)
                    if m >= 2:
                        wait_for(dve, hid_done, 2 * n - 2)
                    v.tensor_copy(xT[:, m % 2].rearrange("p c t -> p (c t)"), tb[m % 2][:]).then_inc(xT_made, 1)
                    for f in range(2):
                        e_, d_ = eneg[:, f, 0, :], eneg[:, f, 1, :]
                        dve.wait_ge(e_done, 2 * n + f + 1)
                        wait_for(dve, h_made, 2 * n + f - 1) if m else wait_for(dve, h_made, 2 * n)
                        v.tensor_scalar(d_, e_, 1.0, None, ALU.add).then_inc(d_done, 1)
                        dve.wait_ge(d_done, 2 * n + f + 1)
                        v.reciprocal(d_, d_).then_inc(r_done, 1)
                        wait_for(dve, r_done, 2 * n + f + 1)
                        if m >= 2:
                            wait_for(dve, y_done, n - 1)
                        v.tensor_tensor(hT[:, m % 2, 2 * f:2 * f + 2, :].rearrange("p f t -> p (f t)"),
                                        hbk[2 * (m % 2) + f][:], d_, ALU.mult).then_inc(h_made, 1)

            expert_pair(0)
            with dve.Fori(1, NE // 2) as pair:
                expert_pair(pair)

            def tile_group(q):
                for i in range(NX):
                    n = q * NX + i
                    dve.wait_ge(ya_in[i], 32 * (q + 1))
                    dve.wait_ge(hh_in[i], 16 * (q + 1))
                    wait_for(dve, o_out[i], 16 * q)
                    v.tensor_copy(wcol[:, i, :], weight[:, bass.ds(n, 1), :].rearrange("p t k -> p (t k)")
                                  ).then_inc(wcol_set, 1)
                    dve.wait_ge(wcol_set, n + 1)
                    v.scalar_tensor_tensor(hh[:, i, :], ya[:, i, :], wcol[:, i, 0:1], hh[:, i, :],
                                           ALU.mult, ALU.add).then_inc(half_mixed, 1)
                    dve.wait_ge(half_mixed, n + 1)
                    v.scalar_tensor_tensor(oo[:, i, :], yb[:, i, :], wcol[:, i, 1:2], hh[:, i, :],
                                           ALU.mult, ALU.add).then_inc(mixed, 1)

            tile_group(0)
            with dve.Fori(1, N // NX) as q:
                tile_group(q)

        @block.scalar
        def _(act):
            act.wait_ge(route_step, marks["logits"])
            nc.scalar.activation(route["e"][:], route["l"][:], ACT.Exp).then_inc(exp_out, 1)
            def expert_pair(pair):
                for m in range(2 * NU):
                    n = pair * (2 * NU) + m
                    for f in range(2):
                        act.wait_ge(hid_done, 2 * n + f + 1)
                        wait_for(act, r_done, 2 * n + f - 1) if m else wait_for(act, r_done, 2 * n)
                        nc.scalar.activation(eneg[:, f, 0, :], hbk[2 * (m % 2) + f][:], ACT.Exp,
                                             scale=-1.0).then_inc(e_done, 1)
                    if m >= 1:
                        copy_out(act, pair, m - 1)
                copy_out(act, pair, 2 * NU - 1)

            expert_pair(0)
            with act.Fori(1, NE // 2) as pair:
                expert_pair(pair)

        @block.tensor
        def _(pe):
            pe.wait_ge(route_step, marks["chosen"])
            for k in range(2):
                nc.tensor.matmul(tb[k][:], keep["b16"][:, 3 + k, :], selb[:].rearrange("p t e -> p (t e)"),
                                 start=True, stop=True).then_inc(tri_done, 1)
            pe.wait_ge(w_in, 16)
            for gr in range(N // TG):
                pe.wait_ge(hot_made, 3 * (gr + 1))
                for t in range(TG):
                    for k in range(2):
                        mm = nc.tensor.matmul(hbk[0][:, 0:2 * NC], place_hot[:, gr % 2, t, k, :],
                                              tile_hot[:, gr % 2, t, k, 1:3, :].rearrange("p a c -> p (a c)"),
                                              start=(gr == 0 and t == 0 and k == 0),
                                              stop=(gr == N // TG - 1 and t == TG - 1 and k == 1))
                mm.then_inc(hot_used, 1)
            pe.wait_ge(route_step, marks["tokens"])

            def out_rows(pair, m):
                n = pair * (2 * NU) + m
                wait_for(pe, h_made, 2 * n + 2)
                if m % NU == 0:
                    pe.wait_ge(wd_in[m // NU], 16 * (pair + 1))
                wait_for(pe, y_copied, n - 1) if m >= 2 else wait_for(pe, y_copied, pair * (2 * NU))
                for t in range(UN):
                    for f in range(4):
                        mm = nc.tensor.matmul(yb_[m % 2][:, t * D:(t + 1) * D], hT[:, m % 2, f, t * P:(t + 1) * P],
                                              wd_sb[:, m // NU, f, :], start=(f == 0), stop=(f == 3))
                mm.then_inc(y_done, 1)

            def expert_pair(pair):
                for m in range(2 * NU):
                    n = pair * (2 * NU) + m
                    pe.wait_ge(xs_in[m % NXS], 32 * (pair * 2 + m // NXS + 1))
                    wait_for(pe, xT_made, n - 1) if m >= 2 else wait_for(pe, xT_made, pair * (2 * NU))
                    for c in range(2):
                        for t in range(UN):
                            mm = nc.tensor.transpose(tb[m % 2][:, (c * UN + t) * P:(c * UN + t + 1) * P],
                                                     xs[:, m % NXS, t, c * P:(c + 1) * P], keep["ident"][:])
                    mm.then_inc(x_turned, 1)
                    pe.wait_ge(xT_made, n + 1)
                    wait_for(pe, h_made, 2 * n - 2) if m >= 2 else wait_for(pe, h_made, pair * (4 * NU))
                    for f in range(4):
                        for c in range(2):
                            mm = nc.tensor.matmul(hbk[2 * (m % 2) + f // 2][:, (f % 2) * 256:(f % 2) * 256 + 256],
                                                  wg_sb[:, c, f * P:(f + 1) * P], xT[:, m % 2, c, :],
                                                  start=(c == 0), stop=(c == 1))
                        if f % 2:
                            mm.then_inc(hid_done, 1)
                    if m >= 1:
                        out_rows(pair, m - 1)
                out_rows(pair, 2 * NU - 1)

            expert_pair(0)
            with pe.Fori(1, NE // 2) as pair:
                expert_pair(pair)

        @block.sync
        def _(sp):
            sp.dma_start(wg_sb[:], wg).then_inc(w_in, 16)
            def expert_pair(pair):
                for m in range(2 * NU):
                    n = pair * (2 * NU) + m
                    if m % NU == 0:
                        e = m // NU
                        wait_for(sp, y_done, pair * (2 * NU))
                        sp.dma_start(wd_sb[:, e], wd[bass.ds(pair * 2 + e, 1)].rearrange("o p f d -> (o p) f d")
                                     ).then_inc(wd_in[e], 16)
                    if m >= 3:
                        store_y(sp, pair, m - 3)
                for m in range(2 * NU - 3, 2 * NU):
                    store_y(sp, pair, m)

            expert_pair(0)
            with sp.Fori(1, NE // 2) as pair:
                expert_pair(pair)
            for i in range(2):
                sp.wait_ge(y_out[i], 16 * (n_units // 2))
            def tile_group(q):
                for i in range(NX):
                    n = q * NX + i
                    wait_for(sp, mixed, q * NX)
                    sp.dma_start(hh[:, i, :], scratch["h2"][bass.ds(n * P, P), :]).then_inc(hh_in[i], 16)
                for i in range(NX):
                    n = q * NX + i
                    sp.wait_ge(mixed, n + 1)
                    sp.dma_start(out[bass.ds(n * P, P), :], oo[:, i, :]).then_inc(o_out[i], 16)

            tile_group(0)
            with sp.Fori(1, N // NX) as q:
                tile_group(q)
            for i in range(NX):
                sp.wait_ge(o_out[i], 16 * (N // NX))

        @block.gpsimd
        def _(pool):
            pool.wait_ge(route_step, marks["tokens"])
            def expert_pair(pair):
                for m in range(2 * NU):
                    n = pair * (2 * NU) + m
                    wait_for(pool, x_turned, n - NXS + 1) if m >= NXS else wait_for(pool, x_turned, pair * (2 * NU))
                    pool.nop(nofuse=True)
                    nc.gpsimd.tensor_copy(xidx[:, m % NXS, :], token[:, bass.ds(n * UN, UN)]).then_inc(idx_set, 1)
                    pool.wait_ge(idx_set, n + 1)
                    pool.nop(nofuse=True)
                    for t in range(UN):
                        nc.gpsimd.indirect_dma_start(
                            xs[:, m % NXS, t, :], None, scratch["xn2"],
                            bass.IndirectOffsetOnAxis(xidx[:, m % NXS, t:t + 1].bitcast(U32), 0)
                            ).then_inc(xs_in[m % NXS], 16)

            expert_pair(0)
            with pool.Fori(1, NE // 2) as pair:
                expert_pair(pair)
            for i in range(2):
                pool.wait_ge(y_out[i], 16 * (n_units // 2))
            def tile_group(q):
                for i in range(NX):
                    n = q * NX + i
                    wait_for(pool, ya_in[i], 32 * q)
                    pool.nop(nofuse=True)
                    nc.gpsimd.tensor_copy(idx[:, i, :], slot[:, bass.ds(n, 1), :].rearrange("p t k -> p (t k)")
                                          ).then_inc(gidx_set, 1)
                for i in range(NX):
                    n = q * NX + i
                    pool.wait_ge(gidx_set, n + 1)
                    wait_for(pool, mixed, q * NX)
                    pool.nop(nofuse=True)
                    for k, dst in enumerate((ya, yb)):
                        nc.gpsimd.indirect_dma_start(
                            dst[:, i, :], None, scratch["yslot"],
                            bass.IndirectOffsetOnAxis(idx[:, i, k:k + 1].bitcast(U32), 0)).then_inc(ya_in[i], 16)

            tile_group(0)
            with pool.Fori(1, N // NX) as q:
                tile_group(q)


def constants(np):
    f32 = np.float32
    n, f = np.arange(NFFT)[:, None], np.arange(NFREQ)[None, :]
    angle = 2.0 * np.pi * ((n * f) % NFFT) / NFFT
    dft = np.concatenate([np.cos(angle), -np.sin(angle)], 1).astype(f32)
    coord = np.clip((np.arange(T, dtype=f32) + f32(0.5)) * f32(NFRAME / T) - f32(0.5), f32(0), f32(NFRAME - 1))
    i0 = np.floor(coord).astype(np.int32)
    i1 = np.minimum(i0 + 1, NFRAME - 1)
    w = (coord - i0).astype(f32)
    interp = np.zeros((NFRAME + 1, T), f32)
    interp[i0, np.arange(T)] += f32(1) - w
    interp[i1, np.arange(T)] += w
    interp[NFRAME] = 1
    theta = f32(10000.0) ** (-np.arange(0, HD, 2, dtype=f32) / f32(HD))
    freqs = (np.arange(T, dtype=f32)[:, None] * theta[None, :]).T.astype(np.float64)
    rope = np.stack([np.tile(np.cos(freqs), (NH, 1)), np.tile(np.sin(freqs), (NH, 1))], 1).astype(f32)
    ident = np.eye(P, dtype=f32)
    row, col = np.arange(P)[:, None], np.arange(P)[None, :]
    b16 = np.stack([ident, np.where(col <= row, 0, -1e30), np.where(col >= row, 0, -1e30),
                    (row <= col) * 1.0, np.ones((P, P))], 1).astype(f32)
    iota = np.zeros((P, V + 2 + NE + P), f32)
    iota[:, 0:V] = np.arange(V)
    iota[:, V] = np.arange(P)
    iota[:, V + 1] = NSLOT + np.arange(P)
    iota[:, V + 2:V + 2 + NE] = np.arange(NE) * CAP
    iota[:, V + 2 + NE:] = np.arange(P)
    return dict(c_dft=dft, c_interp=interp, c_rope=rope, c_ident=ident, c_mask=b16, c_iota=iota)


def kernel(**inputs):
    import numpy as np
    import concourse.bacc as bacc
    from concourse.bass_utils import run_bass_kernel_spmd

    i = {k: np.asarray(v) for k, v in inputs.items()}
    x = i["x"]
    c = np.ascontiguousarray
    padded = np.pad(x, ((0, 0), (NFFT // 2, NFFT // 2)), mode="reflect")
    frames = np.stack([padded[:, NFFT * t:NFFT * (t + 1)] for t in range(NFRAME)], 1)

    def cols(w):
        return c(w.T.reshape(2, P, -1).transpose(1, 0, 2))

    order = np.concatenate([np.arange(0, D, 2), np.arange(1, D, 2)])
    arrays = dict(
        x_frames=c(frames.reshape(BF, NFFT).T), x_tok=c(x), emb=c(i["L0_tok_emb_table"]),
        pw=c(i["L0_tok_proj_w"].reshape(DST, NFREQ, V).transpose(2, 1, 0)),
        pb=c(i["L0_tok_proj_b"][None]), window=c(i["L0_tok_window"][:, None]),
        wq=cols(i["L0_attn_Wq"][order]), bq=c(i["L0_attn_bq"][order].reshape(2, P).T),
        wk=cols(i["L0_attn_Wk"][order]), bk=c(i["L0_attn_bk"][order].reshape(2, P).T),
        wv=cols(i["L0_attn_Wv"]), bv=c(i["L0_attn_bv"][None]),
        wo=cols(i["L0_attn_Wo"]), bo=c(i["L0_attn_bo"][None]),
        wr=cols(i["L0_ffn_w_router"]), wg=cols(i["L0_ffn_w_gate"]),
        wd=c(i["L0_ffn_w_down"].transpose(0, 2, 1).reshape(NE, 4, P, D).transpose(0, 2, 1, 3)),
        **constants(np))
    nc = bacc.Bacc("TRN2", target_bir_lowering=False, num_devices=1)
    ins = [nc.dram_tensor(k, a.shape, mybir.dt.from_np(a.dtype), kind="ExternalInput").ap() for k, a in arrays.items()]
    out = nc.dram_tensor("out", (NTOK, D), F32, kind="ExternalOutput").ap()
    build(nc, ins, out)
    r = run_bass_kernel_spmd(nc, [arrays], core_ids=[0])
    return r.results[0]["out"].reshape(B, T, D)
```

```python
import concourse.bass as bass
from concourse import mybir
from contextlib import ExitStack

F32 = mybir.dt.float32
BF16 = mybir.dt.bfloat16
I32 = mybir.dt.int32
U32 = mybir.dt.uint32
ALU = mybir.AluOpType
ACT = mybir.ActivationFunctionType
AX = mybir.AxisListType

B, T, V, D = 8, 1024, 64, 256
P = 128
NT = T // P
NFFT, NFRAME, NFREQ = 64, 17, 33
DEMB = 179
DST = D - DEMB
BF = B * NFRAME
NH, HD, HALF = 16, 16, 8
GH, NG = 4, 4
NE, HID, CAP = 8, 512, 1280
NTOK = B * T
NTILE = NTOK // P
NSLOT = NE * CAP
SCALE = HD ** -0.5
EPS = 1e-5
STACK = 6 * HD
VW = 32


def piece_range(half, j):
    start = max(512 * half, P * j)
    return start, 512 * (half + 1) - start


HEAD_TILES = [
    [(0, 0, 0), (0, 1, 512), (0, 3, 896)],
    [(0, 2, 0), (1, 6, 256), (1, 0, 512)],
    [(1, 1, 0), (1, 2, 512)],
    [(1, 3, 0), (1, 4, 512)],
    [(1, 5, 0), (1, 7, 384)],
]
PV_ORDER = [
    [[(0, 0, 0), (0, 1, 512), (0, 3, 896)], []],
    [[(0, 2, 0)], [(1, 0, 512), (1, 6, 256)]],
    [[], [(1, 1, 0), (1, 2, 512)]],
    [[], [(1, 3, 0), (1, 4, 512)]],
    [[], [(1, 5, 0), (1, 7, 384)]],
]
NSTEP = len(HEAD_TILES)
STEPS = NG * NSTEP
TILES_OF_STEP = [4, 4, 4, 4, 2]
TILES_OF_GROUP = sum(TILES_OF_STEP)


def max_banks():
    out = []
    for i in range(NT):
        w = min(512, P * (i + 1))
        per = min(GH, 512 // w)
        for h in range(0, GH, per):
            out.append((i, 0, w, list(range(h, h + per)), 0))
    for i in range(4, NT):
        w = P * (i + 1) - 512
        per = min(GH, 512 // w)
        for h in range(0, GH, per):
            out.append((i, 512, w, list(range(h, h + per)), 1))
    return out


MAXB = max_banks()


MAX_FROM, MAX_TILES = 3, 13


def max_quota(tile_no):
    if tile_no < MAX_FROM:
        return 0
    return min(len(MAXB), -(-(tile_no + 1 - MAX_FROM) * len(MAXB) // MAX_TILES))


POST_USES = {(2, k): [("aT", k)] for k in range(4)} | {(3, k): [("wo", k)] for k in range(4)} \
    | {(11, k): [("x2T", k)] for k in range(4)} | {(12, 0): [("logit", 0)]}
QK_ORDER = (4, 5, 0, 1, 6, 7, 2, 3)
PRE_USES = {(1, k): [("emb", k)] for k in range(4)} | {(6, k): [("xT", k)] for k in range(4)} \
    | {(7 + k // 4, k % 4): [("qk", QK_ORDER[k])] for k in range(8)} \
    | {(9, k): [("v", 2 * k), ("v", 2 * k + 1)] for k in range(2)}
ROTARY = dict(zip([(s, k) for s in range(8, 14) for k in range(TILES_OF_STEP[s % NSTEP])],
                  [1, 1, 1, 1, 1, 2, 1, 1, 1, 0, 1, 1, 1, 1, 1, 1, 1, 1, 1, 1, 0, 0]))


STORES = {(10, 1): (1, 0), (11, 0): (0, 0), (13, 0): (0, 1), (14, 0): (1, 1)}


def extra_uses(s, k, pre, post):
    return (PRE_USES.get((s, k), []) if pre else []) + (POST_USES.get((s, k), []) if post else [])


def max_range(s, k, pre):
    g, t = divmod(s, NSTEP)
    if g + 1 == NG and not pre:
        return 0, range(0)
    n = sum(TILES_OF_STEP[:t]) + k
    return g + 1, range(max_quota(n - 1) if n else 0, max_quota(n))


def max_turned(s, k, pre):
    g, t = divmod(s, NSTEP)
    return g + 1 if (t, k) == (NSTEP - 1, 1) and (g + 1 < NG or pre) else None


def turns_of(s, post):
    g, t = divmod(s, NSTEP)
    out = []
    if t == 3 and s < STEPS:
        out.append((g, 0))
    if t == 1 and (g >= 1 or post):
        out.append((g - 1, 1))
    return out


def copied_in(s, post):
    return turns_of(s + 1, post)


def body_uses(pre, post):
    r = []
    for s in range(STEPS):
        for k in range(TILES_OF_STEP[s % NSTEP]):
            g, ms = max_range(s, k, pre)
            r += [("max", g, m) for m in ms]
            if max_turned(s, k, pre) is not None:
                r.append(("mT", max_turned(s, k, pre)))
            r += extra_uses(s, k, pre, post)
        r += [("turn", g, half) for g, half in turns_of(s, post)]
    return r


SEGMENTS = {
    "pro": [("emb", k) for k in range(4)] + [("xT", k) for k in range(4)] + [("qk", k) for k in QK_ORDER]
    + [("v", k) for k in range(4)] + [("max", NG, m) for m in range(len(MAXB))] + [("mT", NG)],
    "first": body_uses(True, False),
    "mid": body_uses(True, True),
    "last": body_uses(False, True),
    "end": [("turn", -1, 1)] + [("aT", k) for k in range(4)] + [("wo", k) for k in range(4)]
    + [("x2T", k) for k in range(4)] + [("logit", 0)],
}
ACT_USES = ("emb", "xT", "qk", "aT", "x2T")
NB = 3


def by_act(u):
    return u[0] in ACT_USES


def counts(uses):
    a = sum(by_act(u) for u in uses)
    return len(uses), a, len(uses) - a


class Ring:

    def __init__(self, segment, b=0):
        self.uses = SEGMENTS[segment]
        self.at = {u: n for n, u in enumerate(self.uses)}
        pro, first, mid, last = (counts(SEGMENTS[x]) for x in ("pro", "first", "mid", "last"))
        if segment == "pro":
            self.start = (0, 0, 0)
        elif segment == "first":
            self.start = pro
        elif segment == "end":
            self.start = tuple(p + f + (B - 2) * m + e for p, f, m, e in zip(pro, first, mid, last))
        else:
            self.start = tuple(b * m + (p + f - m) for p, f, m in zip(pro, first, mid))

    def filled(self, use):
        return self.start[0] + self.at[use] + 1

    def freed(self, use):
        _, a, v = counts(self.uses[:self.at[use] + 1])
        return (True, self.start[1] + a) if by_act(use) else (False, self.start[2] + v)


def build(nc, ins, out):
    (x_frames, x_tok, emb, pw, pb, window, wq, bq, wk, bk, wv, bv, wo, bo, wr, wg, wd,
     c_dft, c_interp, c_rope, c_ident, c_mask, c_iota) = ins
    top = ExitStack()
    with top:
        def dram(name, shape, dt):
            return nc.dram_tensor(name, shape, dt, kind="Internal").ap()

        scratch = {
            "parts": dram("parts", [B, 2, 3, HD, NH, T], BF16),
            "h": dram("h_rows", [NTOK, D], F32),
            "h2": dram("h2", [NTOK, D], F32),
            "xn2": dram("xn2", [NTOK, D], F32),
            "yslot": dram("yslot", [NSLOT + P, D], F32),
        }
        keep = {}
        for name, shape, dt in (("zcat", [P, B, DST], F32), ("logits", [P, NTILE, NE], F32),
                                ("ident", [P, P], F32), ("b16", [P, 5, P], BF16),
                                ("iota", [P, V + 2 + NE + P], F32)):
            keep[name] = top.enter_context(nc.sbuf_tensor(name, shape, dt))
        features(nc, scratch, keep, x_frames, pw, window, c_dft, c_ident, c_mask, c_iota)
        attention(nc, scratch, keep, x_tok, emb, pb, wq, bq, wk, bk, wv, bv, wo, bo, wr, c_interp, c_rope)
        experts(nc, scratch, keep, wg, wd, out)


def wait_for(eng, sem, value):
    if not isinstance(value, int) or value > 0:
        eng.wait_ge(sem, value)


def features(nc, scratch, keep, x_frames, pw, window, c_dft, c_ident, c_mask, c_iota):
    ctx = ExitStack()
    with ctx:
        def sb(name, shape, dt=F32):
            return ctx.enter_context(nc.sbuf_tensor(name, shape, dt))

        def sem(name):
            return ctx.enter_context(nc.semaphore(name))

        PER = 7
        groups = [(a, min(PER, BF - a)) for a in range(0, BF, PER)]
        W = 2 * NFREQ
        xf_i = sb("xf_i", [NFFT, BF], I32)
        xf = sb("xf", [NFFT, BF])
        iota = keep["iota"][:, 0:V]
        win = sb("win", [NFFT, 1])
        dft = sb("dft", [NFFT, W])
        dftw = sb("dftw", [NFFT, W])
        onehot = sb("onehot", [NFFT, 2, PER, V])
        square = sb("square", [V, 2, PER, W])
        power = sb("power", [V, BF, NFREQ])
        mag = sb("mag", [V, BF, NFREQ])
        pw_sb = sb("pw_sb", [V, NFREQ, DST])
        zT = sb("zT", [DST, BF])
        zero = sb("zero", [P, D])
        masks = sb("masks", [P, 5, P])
        bank = [ctx.enter_context(nc.psum_tensor(f"f_bank{i}", [P, 512], F32)) for i in range(2)]
        zbank = ctx.enter_context(nc.psum_tensor("zbank", [P, 512], F32))
        tbank = [ctx.enter_context(nc.psum_tensor(f"tbank{i}", [P, 512], F32)) for i in range(2)]
        loaded, consts_in, masks_kept = sem("loaded"), sem("consts_in"), sem("masks_kept")
        zero_set, zero_out = sem("zero_set"), sem("zero_out")
        ids_float, window_on = sem("ids_float"), sem("window_on")
        onehot_made, spectrum_done = sem("onehot_made"), sem("spectrum_done")
        squared, powered, mag_done = sem("squared"), sem("powered"), sem("mag_done")
        z_done, z_copied, z_turned, z_kept = sem("z_done"), sem("z_copied"), sem("z_turned"), sem("z_kept")

        with nc.Block() as block:
            @block.sync
            def _(sp):
                for dst, src in ((xf_i[:], x_frames), (keep["iota"][:], c_iota), (win[:], window),
                                 (dft[:], c_dft), (keep["ident"][:], c_ident)):
                    sp.dma_start(dst, src).then_inc(loaded, 16)
                sp.dma_start(masks[:], c_mask).then_inc(consts_in, 16)
                sp.dma_start(pw_sb[:], pw).then_inc(consts_in, 16)
                sp.wait_ge(zero_set, 1)
                sp.dma_start(scratch["yslot"][NSLOT:NSLOT + P, :], zero[:]).then_inc(zero_out, 16)
                sp.wait_ge(zero_out, 16)
                sp.wait_ge(consts_in, 32)

            @block.vector
            def _(dve):
                nc.vector.memset(zero[:], 0.0).then_inc(zero_set, 1)
                dve.wait_ge(loaded, 80)
                nc.vector.tensor_copy(xf[:], xf_i[:]).then_inc(ids_float, 1)
                nc.vector.tensor_scalar(dftw[:], dft[:], win[:, 0:1], None, ALU.mult).then_inc(window_on, 1)
                dve.wait_ge(ids_float, 1)
                for n in range(len(groups) + 1):
                    if n < len(groups):
                        a, k = groups[n]
                        if n >= 2:
                            dve.wait_ge(spectrum_done, n - 1)
                        nc.vector.tensor_tensor(
                            onehot[:, n % 2, 0:k, :],
                            xf[:, a:a + k].unsqueeze(2).to_broadcast([NFFT, k, V]),
                            iota[0:NFFT].unsqueeze(1).to_broadcast([NFFT, k, V]),
                            ALU.is_equal).then_inc(onehot_made, 1)
                    if n >= 1:
                        a, k = groups[n - 1]
                        dve.wait_ge(squared, n)
                        nc.vector.tensor_tensor(power[:, a:a + k, :], square[:, (n - 1) % 2, 0:k, 0:NFREQ],
                                                square[:, (n - 1) % 2, 0:k, NFREQ:W], ALU.add).then_inc(powered, 1)
                dve.wait_ge(consts_in, 32)
                nc.vector.tensor_copy(keep["b16"][:], masks[:]).then_inc(masks_kept, 1)
                dve.wait_ge(z_done, 1)
                nc.vector.tensor_copy(zT[:], zbank[0:DST, 0:BF]).then_inc(z_copied, 1)
                for b in range(B):
                    dve.wait_ge(z_turned, b + 1)
                    nc.vector.tensor_copy(keep["zcat"][V:V + NFRAME, b, :],
                                          tbank[b % 2][0:NFRAME, 0:DST]).then_inc(z_kept, 1)

            @block.scalar
            def _(act):
                for n, (a, k) in enumerate(groups):
                    act.wait_ge(spectrum_done, n + 1)
                    if n >= 2:
                        act.wait_ge(powered, n - 1)
                    nc.scalar.activation(square[:, n % 2, 0:k, :],
                                         bank[n % 2][0:V, 0:k * W].rearrange("p (k w) -> p k w", w=W),
                                         ACT.Square).then_inc(squared, 1)
                act.wait_ge(powered, len(groups))
                nc.scalar.activation(mag[:], power[:], ACT.Sqrt).then_inc(mag_done, 1)

            @block.tensor
            def _(pe):
                pe.wait_ge(window_on, 1)
                for n, (a, k) in enumerate(groups):
                    pe.wait_ge(onehot_made, n + 1)
                    if n >= 2:
                        pe.wait_ge(squared, n - 1)
                    for i in range(k):
                        mm = nc.tensor.matmul(bank[n % 2][0:V, i * W:(i + 1) * W], onehot[:, n % 2, i, :],
                                              dftw[:], start=True, stop=True)
                    mm.then_inc(spectrum_done, 1)
                pe.wait_ge(mag_done, 1)
                pe.wait_ge(consts_in, 32)
                for f in range(NFREQ):
                    mm = nc.tensor.matmul(zbank[0:DST, 0:BF], pw_sb[:, f, :], mag[:, :, f],
                                          start=(f == 0), stop=(f == NFREQ - 1))
                mm.then_inc(z_done, 1)
                pe.wait_ge(z_copied, 1)
                for b in range(B):
                    if b >= 2:
                        pe.wait_ge(z_kept, b - 1)
                    nc.tensor.transpose(tbank[b % 2][0:NFRAME, 0:DST], zT[:, b * NFRAME:(b + 1) * NFRAME],
                                        keep["ident"][0:DST, 0:DST]).then_inc(z_turned, 1)


def attention(nc, scratch, keep, x_tok, emb, pb, wq, bq, wk, bk, wv, bv, wo, bo, wr, c_interp, c_rope):
    ctx = ExitStack()
    with ctx:
        def sb(name, shape, dt=F32):
            return ctx.enter_context(nc.sbuf_tensor(name, shape, dt))

        def sem(name):
            return ctx.enter_context(nc.semaphore(name))

        def psum(name, shape):
            return ctx.enter_context(nc.psum_tensor(name, shape, F32))

        ident = keep["ident"]
        identb, mask_q, mask_k = keep["b16"][:, 0, :], keep["b16"][:, 1, :], keep["b16"][:, 2, :]
        KE = V + NFRAME + 1
        e_lhs = sb("e_lhs", [KE, T])
        ids = e_lhs[0:V, :].bitcast(I32)
        e_rhs = sb("e_rhs", [KE, D])
        iota_p = keep["iota"][:, V:V + 1]
        rope = sb("rope", [P, 2, T])
        wq_sb, wk_sb, wv_sb, wo_sb = (sb(n, [P, 2, D]) for n in ("wq_sb", "wk_sb", "wv_sb", "wo_sb"))
        wr_sb = sb("wr_sb", [P, 2, NE])
        qk_bias = sb("qk_bias", [P, 2, 2])
        bv_sb, bo_sb = sb("bv_sb", [P, D]), sb("bo_sb", [P, D])
        h = sb("h", [P, NT, D])
        hp = sb("hp", [P, NT, D])
        xn = sb("xn", [P, NT, D])
        stats = sb("stats", [P, 2, NT, 6])
        mv = sb("mv", [P, 2, NT, 2])
        var, guess, newton = (sb(n, [P, 2, NT]) for n in ("var", "guess", "newton"))
        rstd = sb("rstd", [P, 2, 2, NT])
        half_bits = sb("half_bits", [P, 2, NT], I32)
        guess_bits = sb("guess_bits", [P, 2, NT], I32)
        xnT = sb("xnT", [P, 2, T])
        qk = sb("qk", [P, 2, 2, T])
        rot = sb("rot", [P, 2, 2, T // 2])
        turned = sb("turned", [P, 2, 2, T // 2])
        parts = sb("parts_sb", [P, 2, 3, 2, T // 2], BF16)
        qs = sb("qs", [P, 2, GH, T], BF16)
        ks = sb("ks", [P, 2, GH, T], BF16)
        vals = sb("vals", [P, NT, NH, VW])
        vnext = sb("vnext", [P, NT, NH, HD])
        probs = sb("probs", [P, 2, GH, T])
        mx = sb("mx", [P, NT, GH])
        mx2 = sb("mx2", [P, NT // 2, GH])
        mparts = sb("mparts", [P, 2, GH, NT], BF16)
        mrest = sb("mrest", [P, NT, GH])
        mT = sb("mT", [2 * GH * NT, P], BF16)
        sums = sb("sums", [P, 2, 512])
        rec = sb("rec", [P, 4, GH, 1])
        attn = sb("attn", [P, NT, D])
        ring = [psum(f"ring{i}", [P, 512]) for i in range(NB)]
        st = [psum(f"st{i}", [P, T]) for i in range(2)]
        pv = psum("pv", [P, 512])

        emb_in, values_set = sem("emb_in"), sem("values_set")
        weights_in, ids_in, set_once, e_ready = sem("weights_in"), sem("ids_in"), sem("set_once"), sem("e_ready")
        ring_filled, ring_freed_act, ring_freed_dve = sem("ring_filled"), sem("ring_freed_act"), sem("ring_freed_dve")
        stats_done, aggr_done, rstd_done, normed = ([sem(f"{n}{i}") for i in range(2)] for n in
                                                    ("stats_done", "aggr_done", "rstd_done", "normed"))
        h_out, hp_in, hp_biased, h2_out, xn2_out = sem("h_out"), sem("hp_in"), sem("hp_biased"), sem("h2_out"), sem("xn2_out")
        rot_dve, rot_pool = sem("rot_dve"), sem("rot_pool")
        parts_out = [sem("q_parts_out"), sem("k_parts_out")]
        stack_in = sem("stack_in")
        st_done, exp_done, pv_done, pv_half, pv_freed = (sem("st_done"), sem("exp_done"), sem("pv_done"),
                                                         sem("pv_half"), sem("pv_freed"))
        max_joined, m_hi, m_diff, m_parts, m_rows = (
            sem("max_joined"), sem("m_hi"), sem("m_diff"), sem("m_parts"), sem("m_rows"))
        rec_done, vals_in = sem("rec_done"), sem("vals_in")

        ROT = 10
        LOADS = 6
        NTILES = NG * TILES_OF_GROUP
        N_W = 10
        block = ctx.enter_context(nc.Block())

        def wait_freed(eng, rg, use):
            act_reads, n = rg.freed(use)
            wait_for(eng, ring_freed_act if act_reads else ring_freed_dve, n)

        def take(pe, rg, use):
            n = rg.at[use]
            if n >= NB:
                wait_freed(pe, rg, rg.uses[n - NB])
            elif n == 0:
                wait_for(pe, ring_freed_act, rg.start[1])
                wait_for(pe, ring_freed_dve, rg.start[2])
            return ring[n % NB]

        def filled(eng, rg, use):
            eng.wait_ge(ring_filled, rg.filled(use))
            return ring[rg.at[use] % NB]

        def rotary(eng, ops, rg, b, i, c, buf, rot_sem, start, n):
            cols = slice(c * 512, (c + 1) * 512)
            x1, x2 = qk[:, i, 0, cols], qk[:, i, 1, cols]
            cos, sin = rope[:, 0, cols], rope[:, 1, cols]
            t1, t2, both = rot[:, buf, 0, :], rot[:, buf, 1, :], rot[:, buf]
            if n == 0:
                wait_freed(eng, rg, ("qk", 4 * i + 2 * c + 1))
            if n not in (1, 4):
                wait_for(eng, rot_sem, start + n)
            if n == 6:
                wait_for(eng, parts_out[i], 16 * (2 * b + c))
            eng.nop(nofuse=True)
            if n == 0:
                ins = ops.tensor_tensor(t1, x1, cos, ALU.mult)
            elif n == 1:
                ins = ops.tensor_tensor(t2, x2, sin, ALU.mult)
            elif n == 2:
                ins = ops.tensor_tensor(turned[:, buf, 0, :], t1, t2, ALU.subtract)
            elif n == 3:
                ins = ops.tensor_tensor(t1, x1, sin, ALU.mult)
            elif n == 4:
                ins = ops.tensor_tensor(t2, x2, cos, ALU.mult)
            elif n == 5:
                ins = ops.tensor_tensor(turned[:, buf, 1, :], t1, t2, ALU.add)
            elif n == 6:
                ins = ops.tensor_copy(parts[:, i, 0], turned[:, buf])
            elif n == 7:
                ins = ops.tensor_tensor(both, turned[:, buf], parts[:, i, 0], ALU.subtract)
            elif n == 8:
                ins = ops.tensor_copy(parts[:, i, 1], both)
            else:
                ins = ops.tensor_tensor(parts[:, i, 2], both, parts[:, i, 1], ALU.subtract)
            ins.then_inc(rot_sem, 1)

        DVE_ROT, FIRST_ROT = [(0, 0), (1, 1)], [(0, 0), (0, 1), (1, 1)]

        def turn_start(b, i, c):
            if isinstance(b, int) and b == 0:
                return (rot_pool, 0) if (i, c) == (1, 0) else (rot_dve, ROT * FIRST_ROT.index((i, c)))
            if (i, c) in ((1, 0), (0, 1)):
                return rot_pool, ROT * (2 * b - 1 + (i == 0))
            return rot_dve, ROT * (2 * b + 1 + i)

        def dve_rotary(dve, rg, b, turn, n):
            i, c = (FIRST_ROT if isinstance(b, int) and b == 0 else DVE_ROT)[turn]
            rotary(dve, nc.vector, rg, b, i, c, 0, *turn_start(b, i, c), n)

        def store_parts(eng, b, i, c):
            rot_sem, start = turn_start(b, i, c)
            eng.wait_ge(rot_sem, start + ROT)
            eng.nop(nofuse=True)
            dst = scratch["parts"][bass.ds(b, 1), i, :, :, :, c * 512:(c + 1) * 512]
            eng.dma_start(dst.rearrange("o s (f d) h t -> (d h) (o s f) t", f=2),
                          parts[:, i].rearrange("p s f t -> p (s f) t")).then_inc(parts_out[i], 16)

        @block.sync
        def _(sp):
            w_rows = [(w_sb[:], w) for w_sb, w in ((wq_sb, wq), (wk_sb, wk), (wv_sb, wv), (wo_sb, wo), (wr_sb, wr))]
            w_rows += [(qk_bias[:, 0, :], bq), (qk_bias[:, 1, :], bk), (rope[:], c_rope),
                       (bv_sb[:], bv.to_broadcast([P, D])), (bo_sb[:], bo.to_broadcast([P, D]))]

            def rows_of(name, b):
                return scratch[name][bass.ds(b * T, T), :].rearrange("(t p) d -> p t d", p=P)

            def load_ids(rg, b):
                wait_for(sp, ring_filled, rg.start[0])
                sp.nop(nofuse=True)
                sp.dma_start(ids, x_tok[bass.ds(b, 1), :].to_broadcast([V, T])).then_inc(ids_in, 16)

            def store_h(rg, b):
                wait_freed(sp, rg, ("emb", 3))
                sp.nop(nofuse=True)
                sp.dma_start(rows_of("h", b), h[:]).then_inc(h_out, 16)

            def stacks(b, g):
                if g == 0:
                    for i in range(2):
                        sp.wait_ge(parts_out[i], 16 * 2 * (b + 1))
                        sp.nop(nofuse=True)
                wait_for(sp, st_done, b * NTILES + (g - 1) * TILES_OF_GROUP)
                sp.nop(nofuse=True)
                for row, term, n in ((0, 0, 3), (3, 1, 2), (5, 2, 1)):
                    for i, buf in enumerate((qs, ks)):
                        terms = (slice(0, n), slice(term, term + 1))[i]
                        src = scratch["parts"][bass.ds(b, 1), i, terms, :, g * GH:(g + 1) * GH, :]
                        src = src.rearrange("o s d h t -> (o s) d h t")
                        if i == 1:
                            src = src.to_broadcast([n, HD, GH, T])
                        sp.dma_start(buf[row * HD:(row + n) * HD, g % 2, :, :], src).then_inc(stack_in, 16)

            def shift_rows(rg, g):
                wait_freed(sp, rg, ("mT", g))
                sp.dma_start(qs[STACK:STACK + 2, g % 2, :, :], mT[:]).then_inc(m_rows, 16)

            def load_hp(b):
                wait_for(sp, h2_out, 16 * b)
                sp.nop(nofuse=True)
                sp.wait_ge(h_out, 16 * (b + 1))
                sp.nop(nofuse=True)
                sp.dma_start(hp[:], rows_of("h", b)).then_inc(hp_in, 16)

            def store_h2(rg, b):
                wait_freed(sp, rg, ("wo", 3))
                sp.nop(nofuse=True)
                sp.dma_start(rows_of("h2", b), hp[:]).then_inc(h2_out, 16)

            def store_xn2(b):
                sp.wait_ge(normed[1], NT * (b + 1))
                sp.nop(nofuse=True)
                sp.dma_start(rows_of("xn2", b), xn[:]).then_inc(xn2_out, 16)

            def body(b, rg, pre, post):
                stacks(b, 1)
                if pre:
                    load_ids(rg, b + 1)
                if post:
                    load_hp(b - 1)
                if pre:
                    store_h(rg, b + 1)
                shift_rows(rg, 1)
                stacks(b, 2)
                if post:
                    store_h2(rg, b - 1)
                shift_rows(rg, 2)
                stacks(b, 3)
                if post:
                    store_xn2(b - 1)
                shift_rows(rg, 3)
                if pre:
                    stacks(b + 1, 0)
                    shift_rows(rg, NG)

            rg = Ring("pro")
            load_ids(rg, 0)
            sp.dma_start(e_lhs[V:KE, :], c_interp).then_inc(emb_in, 16)
            sp.wait_ge(set_once, 1)
            sp.dma_start(e_rhs[0:V, 0:DEMB], emb).then_inc(emb_in, 16)
            sp.dma_start(e_rhs[KE - 1:KE, DEMB:D], pb).then_inc(emb_in, 16)
            for dst, src in w_rows:
                sp.dma_start(dst, src).then_inc(weights_in, 16)
            store_h(rg, 0)
            for i, c in ((0, 0), (0, 1), (1, 0), (1, 1)):
                store_parts(sp, 0, i, c)
            stacks(0, 0)
            shift_rows(rg, NG)
            body(0, Ring("first"), True, False)
            body(1, Ring("mid", 1), True, True)
            with sp.Fori(2, B - 1) as b:
                body(b, Ring("mid", b), True, True)
            body(B - 1, Ring("last", B - 1), False, True)
            load_hp(B - 1)
            store_h2(Ring("end"), B - 1)
            store_xn2(B - 1)
            sp.wait_ge(h2_out, 16 * B)
            sp.wait_ge(xn2_out, 16 * B)
            sp.wait_ge(h_out, 16 * B)
            sp.wait_ge(m_rows, 16 * NG * B)
            sp.wait_ge(stack_in, 16 * LOADS * NG * B)

        @block.gpsimd
        def _(pool):
            nc.gpsimd.memset(ks[STACK:STACK + 32, :, :, :], -1.0).then_inc(values_set, 1)
            pool.wait_ge(values_set, 1)
            nc.gpsimd.memset(vals[:], 0.0).then_inc(values_set, 1)
            pool.wait_ge(values_set, 2)
            nc.gpsimd.memset(vals[:, :, :, HD:HD + 1], 1.0).then_inc(values_set, 1)
            pool.wait_ge(weights_in, 16 * N_W)

            def copy_values(rg, b, g):
                if rg:
                    wait_freed(pool, rg, ("v", 3))
                wait_for(pool, pv_done, (b - 1) * STEPS + (g + 1) * NSTEP)
                pool.nop(nofuse=True)
                nc.gpsimd.tensor_copy(vals[:, :, g * GH:(g + 1) * GH, 0:HD],
                                      vnext[:, :, g * GH:(g + 1) * GH, :]).then_inc(vals_in, 1)

            def turn(rg, b, i, c):
                for n in range(ROT):
                    rotary(pool, nc.gpsimd, rg, b, i, c, 1, *turn_start(b, i, c), n)

            def add_bias(b):
                pool.wait_ge(hp_in, 16 * (b + 1))
                nc.gpsimd.tensor_tensor(hp[:], hp[:], bo_sb[:].unsqueeze(1).to_broadcast([P, NT, D]),
                                        ALU.add).then_inc(hp_biased, 1)

            def body(b, rg, pre, post):
                if post:
                    copy_values(None, b, 3)
                    add_bias(b - 1)
                if pre:
                    turn(rg, b + 1, 1, 0)
                    copy_values(rg, b + 1, 0)
                    turn(rg, b + 1, 0, 1)
                    for g in (1, 2):
                        copy_values(rg, b + 1, g)

            pool.wait_ge(values_set, 3)
            turn(Ring("pro"), 0, 1, 0)
            for g in range(NG):
                copy_values(Ring("pro"), 0, g)
            body(0, Ring("first"), True, False)
            body(1, Ring("mid", 1), True, True)
            with pool.Fori(2, B - 1) as b:
                body(b, Ring("mid", b), True, True)
            body(B - 1, Ring("last", B - 1), False, True)
            add_bias(B - 1)

        @block.scalar
        def _(act):
            def evac(rg, use, b):
                name, k = use
                src = filled(act, rg, use)[:]
                if name == "emb":
                    if k == 0:
                        wait_for(act, h_out, 16 * b)
                        wait_for(act, stats_done[0], NT * b)
                        wait_for(act, normed[0], NT * b)
                    nc.scalar.activation(h[:, 2 * k:2 * k + 2, :].rearrange("p t d -> p (t d)"), src,
                                         ACT.Copy).then_inc(ring_freed_act, 1)
                elif name == "qk":
                    i, c, half = k // 4, k // 2 % 2, k % 2
                    nc.scalar.activation(qk[:, i, half, c * 512:(c + 1) * 512], src, ACT.Identity,
                                         bias=qk_bias[:, i, half:half + 1]).then_inc(ring_freed_act, 1)
                else:
                    nc.scalar.activation(xnT[:, :, 256 * k:256 * (k + 1)], src.rearrange("p (c t) -> p c t", c=2),
                                         ACT.Copy).then_inc(ring_freed_act, 1)

            def exps(b, s, k, done):
                t = s % NSTEP
                act.wait_ge(st_done, b * NTILES + done + 1)
                if k == 0:
                    wait_for(act, pv_done, b * STEPS + s - 1)
                dst = probs[:, s % 2, k, :] if t < NSTEP - 1 else probs[:, s % 2, 2 * k:2 * k + 2, 0:512]
                src = st[done % 2][:] if t < NSTEP - 1 else st[done % 2][:].rearrange("p (h q) -> p h q", h=2)
                nc.scalar.activation(dst, src, ACT.Exp, scale=SCALE).then_inc(exp_done, 1)

            def copy_sums(b, g, half):
                if g < 0:
                    b, g = b - 1, NG - 1
                if half == 0:
                    act.wait_ge(pv_half, b * NG + g + 1)
                else:
                    act.wait_ge(pv_done, b * STEPS + (g + 1) * NSTEP)
                wait_for(act, rec_done, 2 * NG * b + 2 * g + half - 1)
                nc.scalar.activation(sums[:, half, :], pv[:], ACT.Copy).then_inc(pv_freed, 1)

            def body(b, rg, pre, post):
                done = 0
                for s in range(STEPS):
                    for k in range(TILES_OF_STEP[s % NSTEP]):
                        exps(b, s, k, done)
                        done += 1
                        if k == 1:
                            for g, half in copied_in(s, post):
                                copy_sums(b, g, half)
                        if pre and (s, k) in STORES:
                            store_parts(act, b + 1, *STORES[s, k])
                        for use in extra_uses(s, k, pre, post):
                            if by_act(use):
                                evac(rg, use, b + 1 if (s, k) in PRE_USES else b - 1)

            rg = Ring("pro")
            for name in ("emb", "xT"):
                for k in range(4):
                    evac(rg, (name, k), 0)
            act.wait_ge(weights_in, 16 * N_W)
            for k in QK_ORDER:
                evac(rg, ("qk", k), 0)
            body(0, Ring("first"), True, False)
            body(1, Ring("mid", 1), True, True)
            with act.Fori(2, B - 1) as b:
                body(b, Ring("mid", b), True, True)
            body(B - 1, Ring("last", B - 1), False, True)
            copy_sums(B, -1, 1)
            rg = Ring("end")
            for name in ("aT", "x2T"):
                for k in range(4):
                    evac(rg, (name, k), B - 1)

        @block.vector
        def _(dve):
            nc.vector.memset(e_rhs[:], 0.0).then_inc(set_once, 1)
            dve.wait_ge(set_once, 1)

            def norm_stats(rg, b, f, tiles):
                for t in tiles:
                    wait_freed(dve, rg, (("emb", "wo")[f], t // 2))
                    nc.vector.bn_stats(stats[:, f, t, :], (h, hp)[f][:, t, :]).then_inc(stats_done[f], 1)

            def deviation(b, f):
                dve.wait_ge(stats_done[f], NT * (b + 1))
                wait_for(dve, normed[f], NT * b)
                dve.nop(nofuse=True)
                for t in range(NT):
                    nc.vector.bn_aggr(mv[:, f, t, :], stats[:, f, t, :]).then_inc(aggr_done[f], 1)
                dve.wait_ge(aggr_done[f], NT * (b + 1))
                n = 12 * b

                def step(ins):
                    ins.then_inc(rstd_done[f], 1)
                step(nc.vector.tensor_scalar(var[:, f], mv[:, f, :, 1], EPS, None, ALU.add))
                dve.wait_ge(rstd_done[f], n + 1)
                step(nc.vector.tensor_scalar(half_bits[:, f], var[:, f].bitcast(I32), 1, None, ALU.arith_shift_right))
                dve.wait_ge(rstd_done[f], n + 2)
                step(nc.vector.tensor_scalar(guess_bits[:, f], half_bits[:, f], -1.0, float(0x5F3759DF),
                                             ALU.mult, ALU.add))
                dve.wait_ge(rstd_done[f], n + 3)
                y = guess_bits[:, f].bitcast(F32)
                for r in range(3):
                    step(nc.vector.tensor_tensor(newton[:, f], y, y, ALU.mult))
                    dve.wait_ge(rstd_done[f], n + 3 * r + 4)
                    step(nc.vector.scalar_tensor_tensor(guess[:, f], newton[:, f], -0.5, var[:, f], ALU.mult, ALU.mult))
                    dve.wait_ge(rstd_done[f], n + 3 * r + 5)
                    step(nc.vector.scalar_tensor_tensor(rstd[:, f, r % 2], guess[:, f], 1.5, y, ALU.add, ALU.mult))
                    dve.wait_ge(rstd_done[f], n + 3 * r + 6)
                    y = rstd[:, f, r % 2]

            def normalise(rg, b, f, tiles):
                if tiles[0] == 0:
                    wait_for(dve, xn2_out, 16 * (b - 2 if f == 0 else b))
                    wait_for(dve, ring_filled, rg.filled(("xT", 3)) if f and ("xT", 3) in rg.at else rg.start[0])
                    dve.nop(nofuse=True)
                for t in tiles:
                    nc.vector.tensor_scalar(xn[:, t, :], (h, hp)[f][:, t, :], mv[:, f, t, 0:1], rstd[:, f, 0, t:t + 1],
                                            ALU.subtract, ALU.mult).then_inc(normed[f], 1)

            def embedding_operands(b):
                dve.wait_ge(ids_in, 16 * (b + 1))
                nc.vector.tensor_scalar(e_lhs[0:V, :], ids, iota_p[0:V], None, ALU.is_equal).then_inc(e_ready, 1)
                nc.vector.tensor_copy(e_rhs[V:V + NFRAME, DEMB:D],
                                      keep["zcat"][V:V + NFRAME, bass.ds(b, 1), :].rearrange("p b d -> p (b d)")
                                      ).then_inc(e_ready, 1)

            def maxima(rg, g, m):
                i, k0, w, heads, part = MAXB[m]
                src = filled(dve, rg, ("max", g, m))[:, 0:w * len(heads)].rearrange("p (h k) -> p h k", k=w)
                dst = mx[:, i, heads[0]:heads[-1] + 1] if part == 0 else mx2[:, i - 4, heads[0]:heads[-1] + 1]
                nc.vector.tensor_reduce(dst, src, AX.X, ALU.max).then_inc(ring_freed_dve, 1)

            def shift(rg, b, g):
                at = NG * b + g + 1
                wait_freed(dve, rg, ("max", g, len(MAXB) - 1))
                nc.vector.tensor_tensor(mx[:, 4:8, :], mx[:, 4:8, :], mx2[:], ALU.max).then_inc(max_joined, 1)
                dve.wait_ge(max_joined, at)
                nc.vector.tensor_copy(mparts[:, 0].rearrange("p h i -> p i h"), mx[:]).then_inc(m_hi, 1)
                dve.wait_ge(m_hi, at)
                nc.vector.tensor_tensor(mrest[:], mx[:], mparts[:, 0].rearrange("p h i -> p i h"),
                                        ALU.subtract).then_inc(m_diff, 1)
                dve.wait_ge(m_diff, at)
                nc.vector.tensor_copy(mparts[:, 1].rearrange("p h i -> p i h"), mrest[:]).then_inc(m_parts, 1)
                bank = filled(dve, rg, ("mT", g))
                wait_for(dve, m_rows, 16 * (NG * b + g))
                nc.vector.tensor_copy(mT[:], bank[0:64, 0:64].bitcast(BF16)).then_inc(ring_freed_dve, 1)

            def scale_half(rg, b, g, half):
                src = filled(dve, rg, ("turn", g, half))[:].rearrange("p (t h v) -> p t h v", t=4, h=GH)
                if g < 0:
                    b, g = b - 1, NG - 1
                n = rg.at[("turn", g, half)] if ("turn", g, half) in rg.at else rg.at[("turn", -1, 1)]
                wait_for(dve, ring_freed_dve, rg.start[2] + counts(rg.uses[:n])[2])
                nc.vector.reciprocal(rec[:], src[:, :, :, HD:HD + 1]).then_inc(rec_done, 1)
                dve.wait_ge(rec_done, 2 * NG * b + 2 * g + half + 1)
                dst = attn[:, 4 * half:4 * half + 4, g * GH * HD:(g + 1) * GH * HD]
                nc.vector.tensor_tensor(dst.rearrange("p t (h v) -> p t h v", h=GH), src[:, :, :, 0:HD],
                                        rec[:].to_broadcast([P, 4, GH, HD]), ALU.mult).then_inc(ring_freed_dve, 1)

            def read(rg, use, b):
                name, k = use
                bank = filled(dve, rg, use)
                if name == "v":
                    if k == 0:
                        wait_for(dve, vals_in, NG * b)
                    nc.vector.tensor_tensor(vnext[:, 2 * k:2 * k + 2], bank[:].rearrange("p (t h v) -> p t h v", t=2, h=NH),
                                            bv_sb[:].rearrange("p (h v) -> p h v", h=NH).unsqueeze(1)
                                            .to_broadcast([P, 2, NH, HD]), ALU.add).then_inc(ring_freed_dve, 1)
                elif name == "wo":
                    if k == 0:
                        dve.wait_ge(hp_biased, b + 1)
                    nc.vector.tensor_tensor(hp[:, 2 * k:2 * k + 2, :], bank[:].rearrange("p (t d) -> p t d", t=2),
                                            hp[:, 2 * k:2 * k + 2, :], ALU.add).then_inc(ring_freed_dve, 1)
                else:
                    nc.vector.tensor_copy(keep["logits"][:, bass.ds(b * NT, NT), :].rearrange("p t e -> p (t e)"),
                                          bank[:, 0:NT * NE]).then_inc(ring_freed_dve, 1)

            def between(rg, b, s, k, pre, post):
                if pre:
                    if (s, k) == (0, 3):
                        embedding_operands(b + 1)
                    if s == 2:
                        norm_stats(rg, b + 1, 0, (2 * k, 2 * k + 1))
                    if (s, k) == (4, 1):
                        deviation(b + 1, 0)
                    if s == 5:
                        normalise(rg, b + 1, 0, (2 * k, 2 * k + 1))
                    n = sum(ROTARY[t] for t in ROTARY if t < (s, k))
                    for m in range(n, n + ROTARY.get((s, k), 0)):
                        dve_rotary(dve, rg, b + 1, m // ROT, m % ROT)
                if post:
                    if s == 4:
                        norm_stats(rg, b - 1, 1, range(4 * k, 4 * k + 4))
                    if (s, k) == (5, 1):
                        deviation(b - 1, 1)
                    if s == 10:
                        normalise(rg, b - 1, 1, (2 * k, 2 * k + 1))

            def body(b, rg, pre, post):
                for s in range(STEPS):
                    for k in range(TILES_OF_STEP[s % NSTEP]):
                        g, ms = max_range(s, k, pre)
                        for m in ms:
                            maxima(rg, g, m)
                        if max_turned(s, k, pre) is not None:
                            shift(rg, b, max_turned(s, k, pre))
                        for use in extra_uses(s, k, pre, post):
                            if not by_act(use):
                                read(rg, use, b + 1 if (s, k) in PRE_USES else b - 1)
                        between(rg, b, s, k, pre, post)
                    for g, half in turns_of(s, post):
                        scale_half(rg, b, g, half)

            rg = Ring("pro")
            embedding_operands(0)
            norm_stats(rg, 0, 0, range(NT))
            deviation(0, 0)
            normalise(rg, 0, 0, range(NT))
            dve.wait_ge(weights_in, 16 * N_W)
            for n in range(ROT):
                dve_rotary(dve, rg, 0, 0, n)
            for k in range(4):
                read(rg, ("v", k), 0)
            for n in range(ROT, 3 * ROT):
                dve_rotary(dve, rg, 0, n // ROT, n % ROT)
            for m in range(len(MAXB)):
                maxima(rg, NG, m)
            shift(rg, -1, NG)
            body(0, Ring("first"), True, False)
            body(1, Ring("mid", 1), True, True)
            with dve.Fori(2, B - 1) as b:
                body(b, Ring("mid", b), True, True)
            body(B - 1, Ring("last", B - 1), False, True)
            rg = Ring("end")
            scale_half(rg, B, -1, 1)
            for k in range(4):
                read(rg, ("wo", k), B - 1)
            norm_stats(rg, B - 1, 1, range(NT))
            deviation(B - 1, 1)
            normalise(rg, B - 1, 1, range(NT))
            read(rg, ("logit", 0), B - 1)

        @block.tensor
        def _(pe):
            pe.wait_ge(emb_in, 48)
            pe.wait_ge(set_once, 1)

            def turn_rows(bank, k, src):
                for c in range(2):
                    for u in range(2):
                        mm = nc.tensor.transpose(bank[:, (2 * c + u) * P:(2 * c + u + 1) * P],
                                                 src[:, 2 * k + u, c * P:(c + 1) * P], ident[:])
                return mm

            def rows_product(bank, k, w_sb):
                for u in range(2):
                    t = 2 * k + u
                    for c in range(2):
                        mm = nc.tensor.matmul(bank[:, u * D:(u + 1) * D], xnT[:, c, t * P:(t + 1) * P],
                                              w_sb[:, c, :], start=(c == 0), stop=(c == 1))
                return mm

            def extra(rg, use, b):
                name, k = use
                bank = take(pe, rg, use)
                if name == "emb":
                    if k == 0:
                        pe.wait_ge(e_ready, 2 * (b + 1))
                    for u in range(2):
                        t = 2 * k + u
                        mm = nc.tensor.matmul(bank[:, u * D:(u + 1) * D], e_lhs[:, t * P:(t + 1) * P], e_rhs[:],
                                              start=True, stop=True)
                elif name in ("xT", "x2T"):
                    pe.wait_ge(normed[0 if name == "xT" else 1], NT * b + 2 * k + 2)
                    mm = turn_rows(bank, k, xn)
                elif name == "aT":
                    if k == 0:
                        wait_freed(pe, rg, ("turn", -1, 1))
                    mm = turn_rows(bank, k, attn)
                elif name == "qk":
                    i, c, half = k // 4, k // 2 % 2, k % 2
                    if k == QK_ORDER[0]:
                        wait_freed(pe, rg, ("xT", 3))
                    for ch in range(2):
                        mm = nc.tensor.matmul(bank[:], (wq_sb, wk_sb)[i][:, ch, half * P:(half + 1) * P],
                                              xnT[:, ch, c * 512:(c + 1) * 512], start=(ch == 0), stop=(ch == 1))
                elif name == "v":
                    mm = rows_product(bank, k, wv_sb)
                elif name == "wo":
                    wait_freed(pe, rg, ("aT", k))
                    mm = rows_product(bank, k, wo_sb)
                else:
                    wait_freed(pe, rg, ("x2T", 3))
                    for t in range(NT):
                        for c in range(2):
                            mm = nc.tensor.matmul(bank[:, t * NE:(t + 1) * NE], xnT[:, c, t * P:(t + 1) * P],
                                                  wr_sb[:, c, :], start=(c == 0), stop=(c == 1))
                mm.then_inc(ring_filled, 1)

            def max_bank(rg, b, g, m):
                i, k0, w, heads, part = MAXB[m]
                bank = take(pe, rg, ("max", g, m))
                if m == 0:
                    pe.wait_ge(stack_in, 16 * LOADS * (NG * b + g + 1))
                diag = P * i if P * i >= k0 and P * (i + 1) <= k0 + w else None
                for n, h_ in enumerate(heads):
                    mm = nc.tensor.matmul(bank[:, n * w:(n + 1) * w], qs[0:STACK, g % 2, h_, P * i:P * (i + 1)],
                                          ks[0:STACK, g % 2, h_, k0:k0 + w], start=True, stop=(diag is None))
                    if diag is not None:
                        o = n * w + diag - k0
                        mm = nc.tensor.matmul(bank[:, o:o + P], identb, mask_q, start=False, stop=True)
                mm.then_inc(ring_filled, 1)

            def max_turn(rg, b, g):
                bank = take(pe, rg, ("mT", g))
                pe.wait_ge(m_parts, NG * b + g + 1)
                pe.nop(nofuse=True)
                nc.tensor.transpose(bank[0:64, 0:64].bitcast(BF16), mparts[:].rearrange("p s h i -> p (s h i)"),
                                    identb).then_inc(ring_filled, 1)

            def score_tile(b, s, k, done):
                g, t = divmod(s, NSTEP)
                if t == 0 and k == 0:
                    pe.wait_ge(m_rows, 16 * (NG * b + g + 1))
                wait_for(pe, exp_done, b * NTILES + done - 1)
                tile = st[done % 2]
                for h_ in ([k] if t < NSTEP - 1 else [2 * k, 2 * k + 1]):
                    o = 0 if t < NSTEP - 1 else 512 * (h_ % 2)
                    for (half, j, col) in HEAD_TILES[t]:
                        q0, w = piece_range(half, j)
                        diag = j // 4 == half
                        mm = nc.tensor.matmul(tile[:, o + col:o + col + w], ks[0:STACK + 2, g % 2, h_, P * j:P * (j + 1)],
                                              qs[0:STACK + 2, g % 2, h_, q0:q0 + w], start=True, stop=not diag)
                        if diag:
                            mm = nc.tensor.matmul(tile[:, o + col:o + col + P], identb, mask_k, start=False, stop=True)
                mm.then_inc(st_done, 1)

            def sum_pieces(s, half):
                g, t = divmod(s, NSTEP)
                for (hf, j, col) in PV_ORDER[t][half]:
                    q0, w = piece_range(hf, j)
                    q0 -= 512 * hf
                    first, last = (j == 0), (j == (2 if hf == 0 else 7))
                    for h_ in range(GH):
                        mm = nc.tensor.matmul(pv[32 * h_:32 * h_ + VW, q0:q0 + w],
                                              vals[:, j, g * GH + h_, :], probs[:, s % 2, h_, col:col + w],
                                              start=first, stop=last)
                return mm

            def sum_step(b, s, part):
                g, t = divmod(s, NSTEP)
                if part == 0:
                    pe.wait_ge(exp_done, b * NTILES + TILES_OF_GROUP * g + sum(TILES_OF_STEP[:t + 1]))
                    if t == 0:
                        pe.wait_ge(vals_in, NG * b + g + 1)
                        wait_for(pe, pv_freed, 2 * NG * b + 2 * g)
                    if PV_ORDER[t][0]:
                        sum_pieces(s, 0).then_inc(pv_half if t == 1 else pv_done, 1)
                elif PV_ORDER[t][1]:
                    if t == 1:
                        pe.wait_ge(pv_freed, 2 * NG * b + 2 * g + 1)
                    sum_pieces(s, 1).then_inc(pv_done, 1)

            def turn_half(rg, b, g, half):
                bank = take(pe, rg, ("turn", g, half))
                if g < 0:
                    b, g = b - 1, NG - 1
                pe.wait_ge(pv_freed, 2 * NG * b + 2 * g + half + 1)
                for t in range(4):
                    mm = nc.tensor.transpose(bank[:, t * P:(t + 1) * P], sums[:, half, t * P:(t + 1) * P], ident[:])
                mm.then_inc(ring_filled, 1)

            def body(b, rg, pre, post):
                done = 0
                for s in range(STEPS):
                    tiles = TILES_OF_STEP[s % NSTEP]
                    for k in range(tiles):
                        score_tile(b, s, k, done)
                        done += 1
                        g, ms = max_range(s, k, pre)
                        for m in ms[:2]:
                            max_bank(rg, b, g, m)
                        if max_turned(s, k, pre) is not None:
                            max_turn(rg, b, max_turned(s, k, pre))
                        extras = [(use, b + 1 if (s, k) in PRE_USES else b - 1) for use in extra_uses(s, k, pre, post)]
                        if tiles == 2:
                            for use, seq in extras:
                                extra(rg, use, seq)
                        if s >= 1 or post:
                            at = (b, s - 1) if s else (b - 1, STEPS - 1)
                            if k == 1:
                                sum_step(*at, 0)
                            if k == (2 if tiles > 2 else 1):
                                sum_step(*at, 1)
                        for m in ms[2:]:
                            max_bank(rg, b, g, m)
                        if tiles > 2:
                            for use, seq in extras:
                                extra(rg, use, seq)
                    for g, half in turns_of(s, post):
                        turn_half(rg, b, g, half)

            rg = Ring("pro")
            for name in ("emb", "xT"):
                for k in range(4):
                    extra(rg, (name, k), 0)
            pe.wait_ge(weights_in, 16 * N_W)
            for k in QK_ORDER:
                extra(rg, ("qk", k), 0)
            for k in range(4):
                extra(rg, ("v", k), 0)
            pe.wait_ge(values_set, 3)
            for m in range(len(MAXB)):
                max_bank(rg, -1, NG, m)
            max_turn(rg, -1, NG)
            body(0, Ring("first"), True, False)
            body(1, Ring("mid", 1), True, True)
            with pe.Fori(2, B - 1) as b:
                body(b, Ring("mid", b), True, True)
            body(B - 1, Ring("last", B - 1), False, True)
            rg = Ring("end")
            for part in range(2):
                sum_step(B - 1, STEPS - 1, part)
            turn_half(rg, B, -1, 1)
            for name, n in (("aT", 4), ("wo", 4), ("x2T", 4), ("logit", 1)):
                for k in range(n):
                    extra(rg, (name, k), B - 1)


def experts(nc, scratch, keep, wg, wd, out):
    ctx = ExitStack()
    with ctx:
        def sb(name, shape, dt=F32):
            return ctx.enter_context(nc.sbuf_tensor(name, shape, dt))

        def sem(name):
            return ctx.enter_context(nc.semaphore(name))

        def psum(name):
            return ctx.enter_context(nc.psum_tensor(name, [P, 512], F32))

        N = NTILE
        logits = keep["logits"]
        route = {n: sb("r_" + n, [P, N, NE]) for n in
                 ("l", "g", "t", "eq", "sel", "pre", "pos", "ex", "ex2", "first", "second", "e")}
        one = {n: sb("o_" + n, [P, N]) for n in ("mx", "sum", "rs", "n0", "v2", "need", "va", "vb", "wden")}
        slot_f = sb("slot_f", [P, N, 2])
        slot = sb("slot", [P, N, 2], I32)
        weight = sb("weight", [P, N, 2])
        selb = sb("selb", [P, N, NE], BF16)
        spare = keep["iota"][:, V + 1:V + 2]
        ecap = keep["iota"][:, V + 2:V + 2 + NE]
        NC = NSLOT // P
        TG = 8
        slot_hl = sb("slot_hl", [P, 2, N, 2], I32)
        slot_hlf = sb("slot_hlf", [P, 2, N, 2], BF16)
        rows_b = sb("rows_b", [P, P], BF16)
        place_hot = sb("place_hot", [P, 2, TG, 2, P], BF16)
        tile_hot = sb("tile_hot", [P, 2, TG, 2, 3, NC], BF16)
        token_f = sb("token_f", [P, 2, NC])
        token = sb("token", [P, NC], I32)
        c_rows = keep["iota"][:, V + 2 + NE:V + 2 + NE + P]
        NX = 8
        idx = sb("idx", [P, NX, 2], I32)
        NXS = 5
        xidx = sb("xidx", [P, NXS, 2], I32)
        wg_sb = sb("wg_sb", [P, 2, HID])
        wd_sb = sb("wd_sb", [P, 2, 4, D])
        UN = 2
        NU = CAP // (UN * P)
        xs = sb("xs", [P, NXS, UN, D])
        xT = sb("xT", [P, 2, 2, UN * P])
        hT = sb("hT", [P, 2, 4, UN * P])
        ys = sb("ys", [P, 2, UN * D])
        ya = sb("ya", [P, NX, D])
        yb = sb("yb", [P, NX, D])
        hh = sb("hh", [P, NX, D])
        oo = sb("oo", [P, NX, D])
        wcol = sb("wcol", [P, NX, 2])
        tb = [psum(f"tb{i}") for i in range(2)]
        hbk = [psum(f"hbk{i}") for i in range(4)]
        yb_ = [psum(f"ybk{i}") for i in range(2)]

        w_in, tri_done, route_step = sem("w_in"), sem("tri_done"), sem("route_step")
        exp_out = sem("exp_out")
        tile_made, hot_made, hot_used = sem("tile_made"), sem("hot_made"), sem("hot_used")
        rows_made, tiles_made = sem("rows_made"), sem("tiles_made")
        idx_set = sem("idx_set")
        wd_in = [sem(f"wd_in{i}") for i in range(2)]
        xs_in = [sem(f"xs_in{i}") for i in range(NXS)]
        x_turned, xT_made, hid_done, h_made = sem("x_turned"), sem("xT_made"), sem("hid_done"), sem("h_made")
        y_done, y_copied = sem("y_done"), sem("y_copied")
        y_out = [sem(f"y_out{i}") for i in range(2)]
        gidx_set = sem("gidx_set")
        ya_in = [sem(f"ya_in{i}") for i in range(NX)]
        hh_in = [sem(f"hh_in{i}") for i in range(NX)]
        mixed, half_mixed, wcol_set = sem("mixed"), sem("half_mixed"), sem("wcol_set")
        o_out = [sem(f"o_out{i}") for i in range(NX)]

        count = [0]
        marks = {}
        block = ctx.enter_context(nc.Block())
        n_units = NE * NU

        def store_y(sp, pair, m):
            n = pair * (2 * NU) + m
            wait_for(sp, y_copied, n + 1)
            sp.dma_start(scratch["yslot"][bass.ds(n * UN * P, UN * P), :].rearrange("(t p) d -> p t d", p=P),
                         ys[:, m % 2, :].rearrange("p (t d) -> p t d", t=UN)).then_inc(y_out[m % 2], 16)

        @block.vector
        def _(dve):
            def step(ins):
                count[0] += 1
                ins.then_inc(route_step, 1)
                dve.wait_ge(route_step, count[0])

            def wide(a):
                return a[:].unsqueeze(2).to_broadcast([P, N, NE])
            v = nc.vector
            r, o = route, one
            dve.wait_ge(w_in, 16)
            step(v.tensor_reduce(o["mx"][:], logits[:], AX.X, ALU.max))
            step(v.tensor_tensor(r["l"][:], logits[:], wide(o["mx"]), ALU.subtract))
            step(v.tensor_scalar(r["l"][:], r["l"][:], -87.33654, None, ALU.max))
            marks["logits"] = count[0]
            step(v.tensor_scalar(r["eq"][:], r["l"][:], 0.0, None, ALU.is_equal))
            step(v.tensor_reduce(o["n0"][:], r["eq"][:], AX.X, ALU.add))
            step(v.scalar_tensor_tensor(r["t"][:], r["eq"][:], -1e4, r["l"][:], ALU.mult, ALU.add))
            step(v.tensor_reduce(o["v2"][:], r["t"][:], AX.X, ALU.max))
            step(v.tensor_scalar(o["n0"][:], o["n0"][:], 1.5, None, ALU.is_lt))
            step(v.tensor_tensor(o["v2"][:], o["v2"][:], o["n0"][:], ALU.mult))
            step(v.tensor_tensor(r["t"][:], r["l"][:], wide(o["v2"]), ALU.is_gt))
            step(v.tensor_reduce(o["need"][:], r["t"][:], AX.X, ALU.add))
            step(v.tensor_scalar(o["need"][:], o["need"][:], -1.0, 2.0, ALU.mult, ALU.add))
            step(v.tensor_tensor(r["eq"][:], r["l"][:], wide(o["v2"]), ALU.is_equal))

            def before(dst, src):
                step(v.memset(dst[:, :, 0:1], 0.0))
                for e in range(1, NE):
                    step(v.tensor_tensor(dst[:, :, e:e + 1], dst[:, :, e - 1:e], src[:, :, e - 1:e], ALU.add))
            before(r["pre"], r["eq"])
            step(v.tensor_tensor(r["pre"][:], r["pre"][:], wide(o["need"]), ALU.is_lt))
            step(v.tensor_tensor(r["eq"][:], r["eq"][:], r["pre"][:], ALU.mult))
            step(v.tensor_tensor(r["sel"][:], r["eq"][:], r["t"][:], ALU.add))
            step(v.tensor_copy(selb[:], r["sel"][:]))
            marks["chosen"] = count[0]
            before(r["pre"], r["sel"])
            step(v.tensor_scalar(r["first"][:], r["pre"][:], 0.5, None, ALU.is_lt))
            step(v.tensor_tensor(r["first"][:], r["first"][:], r["sel"][:], ALU.mult))
            step(v.tensor_tensor(r["second"][:], r["sel"][:], r["first"][:], ALU.subtract))
            dve.wait_ge(exp_out, 1)
            step(v.tensor_reduce(o["sum"][:], r["e"][:], AX.X, ALU.add))
            step(v.reciprocal(o["rs"][:], o["sum"][:]))
            step(v.tensor_tensor(r["g"][:], r["e"][:], wide(o["rs"]), ALU.mult))
            dve.wait_ge(tri_done, 2)
            step(v.memset(r["ex"][:, 0:1, :], 0.0))
            step(v.tensor_copy(r["ex"][:, 1:N, :], tb[1][:].rearrange("p (t e) -> p t e", e=NE)[:, 0:N - 1, :]))
            a, c = r["ex"], r["ex2"]
            reach = 1
            while reach < N:
                step(v.tensor_copy(c[:, 0:reach, :], a[:, 0:reach, :]))
                step(v.tensor_tensor(c[:, reach:N, :], a[:, reach:N, :], a[:, 0:N - reach, :], ALU.add))
                a, c = c, a
                reach *= 2
            step(v.scalar_tensor_tensor(r["pos"][:], tb[0][:].rearrange("p (t e) -> p t e", e=NE), -1.0, a[:],
                                        ALU.add, ALU.add))
            keep_ = r["eq"]
            step(v.tensor_scalar(keep_[:], r["pos"][:], CAP - 0.5, None, ALU.is_lt))
            step(v.tensor_tensor(r["pos"][:], r["pos"][:], ecap.unsqueeze(1).to_broadcast([P, N, NE]), ALU.add))
            for k, (name, valid) in enumerate((("first", "va"), ("second", "vb"))):
                step(v.tensor_tensor(r["t"][:], r[name][:], keep_[:], ALU.mult))
                step(v.tensor_reduce(o[valid][:], r["t"][:], AX.X, ALU.add))
                step(v.tensor_tensor(r["e"][:], r["t"][:], r["pos"][:], ALU.mult))
                step(v.tensor_reduce(slot_f[:, :, k], r["e"][:], AX.X, ALU.add))
                step(v.tensor_scalar(o[valid][:], o[valid][:], -1.0, 1.0, ALU.mult, ALU.add))
                step(v.tensor_scalar(o[valid][:], o[valid][:], spare, None, ALU.mult))
                step(v.tensor_tensor(slot_f[:, :, k], slot_f[:, :, k], o[valid][:], ALU.add))
                step(v.tensor_tensor(r["e"][:], r["t"][:], r["g"][:], ALU.mult))
                step(v.tensor_reduce(weight[:, :, k], r["e"][:], AX.X, ALU.add))
            step(v.tensor_copy(slot[:], slot_f[:]))
            step(v.tensor_tensor(o["wden"][:], weight[:, :, 0], weight[:, :, 1], ALU.add))
            step(v.tensor_scalar(o["wden"][:], o["wden"][:], 1e-6, None, ALU.add))
            step(v.reciprocal(o["wden"][:], o["wden"][:]))
            step(v.tensor_tensor(weight[:], weight[:], o["wden"][:].unsqueeze(2).to_broadcast([P, N, 2]), ALU.mult))
            marks["slots"] = count[0]

            step(v.tensor_scalar(slot_hl[:, 0], slot[:], 7, None, ALU.arith_shift_right))
            step(v.tensor_scalar(slot_hl[:, 1], slot[:], P - 1, None, ALU.bitwise_and))
            step(v.tensor_copy(slot_hlf[:], slot_hl[:]))
            step(v.tensor_copy(rows_b[:], c_rows))
            for gr in range(N // TG):
                ts = slice(gr * TG, (gr + 1) * TG)
                if gr >= 2:
                    dve.wait_ge(hot_used, gr - 1)
                v.tensor_tensor(place_hot[:, gr % 2], slot_hlf[:, 1, ts, :].unsqueeze(3).to_broadcast([P, TG, 2, P]),
                                rows_b[:].unsqueeze(1).unsqueeze(1).to_broadcast([P, TG, 2, P]),
                                ALU.is_equal).then_inc(hot_made, 1)
                hot = tile_hot[:, gr % 2]
                v.tensor_tensor(hot[:, :, :, 0, :], slot_hlf[:, 0, ts, :].unsqueeze(3).to_broadcast([P, TG, 2, NC]),
                                rows_b[:, 0:NC].unsqueeze(1).unsqueeze(1).to_broadcast([P, TG, 2, NC]),
                                ALU.is_equal).then_inc(tile_made, 1)
            dve.wait_ge(hot_used, N // TG)
            sums = hbk[0][:, 0:2 * NC].rearrange("p (k c) -> p k c", k=2)
            step(v.tensor_scalar(token_f[:, 1, :], sums[:, 1, :], float(P), None, ALU.mult))
            step(v.tensor_tensor(token_f[:, 0, :], sums[:, 0, :], token_f[:, 1, :], ALU.add))
            step(v.tensor_copy(token[:], token_f[:, 0, :]))
            marks["tokens"] = count[0]

            def copy_out(pair, m):
                n = pair * (2 * NU) + m
                dve.wait_ge(y_done, n + 1)
                wait_for(dve, y_out[m % 2], 16 * (pair * NU + m // 2))
                v.tensor_copy(ys[:, m % 2, :], yb_[m % 2][:]).then_inc(y_copied, 1)

            def expert_pair(pair):
                for m in range(2 * NU):
                    n = pair * (2 * NU) + m
                    wait_for(dve, x_turned, n + 1)
                    if m >= 2:
                        wait_for(dve, hid_done, 2 * n - 2)
                    v.tensor_copy(xT[:, m % 2].rearrange("p c t -> p (c t)"), tb[m % 2][:]).then_inc(xT_made, 1)
                    if m >= 2:
                        copy_out(pair, m - 2)
                copy_out(pair, 2 * NU - 2)
                copy_out(pair, 2 * NU - 1)

            expert_pair(0)
            with dve.Fori(1, NE // 2) as pair:
                expert_pair(pair)

            def tile_group(q):
                for i in range(NX):
                    n = q * NX + i
                    dve.wait_ge(ya_in[i], 32 * (q + 1))
                    dve.wait_ge(hh_in[i], 16 * (q + 1))
                    wait_for(dve, o_out[i], 16 * q)
                    v.tensor_copy(wcol[:, i, :], weight[:, bass.ds(n, 1), :].rearrange("p t k -> p (t k)")
                                  ).then_inc(wcol_set, 1)
                    dve.wait_ge(wcol_set, n + 1)
                    v.scalar_tensor_tensor(hh[:, i, :], ya[:, i, :], wcol[:, i, 0:1], hh[:, i, :],
                                           ALU.mult, ALU.add).then_inc(half_mixed, 1)
                    dve.wait_ge(half_mixed, n + 1)
                    v.scalar_tensor_tensor(oo[:, i, :], yb[:, i, :], wcol[:, i, 1:2], hh[:, i, :],
                                           ALU.mult, ALU.add).then_inc(mixed, 1)

            tile_group(0)
            with dve.Fori(1, N // NX) as q:
                tile_group(q)

        @block.scalar
        def _(act):
            act.wait_ge(route_step, marks["logits"])
            nc.scalar.activation(route["e"][:], route["l"][:], ACT.Exp).then_inc(exp_out, 1)
            for gr in range(N // TG):
                hot = tile_hot[:, gr % 2]
                act.wait_ge(tile_made, gr + 1)
                nc.scalar.activation(hot[:, :, :, 1, :], hot[:, :, :, 0, :], ACT.Copy,
                                     scale=keep["iota"][:, V:V + 1]).then_inc(rows_made, 1)
            def expert_pair(pair):
                for m in range(2 * NU):
                    n = pair * (2 * NU) + m
                    for f in range(2):
                        act.wait_ge(hid_done, 2 * n + f + 1)
                        if m >= 2:
                            act.wait_ge(y_done, n - 1)
                        nc.scalar.activation(hT[:, m % 2, 2 * f:2 * f + 2, :].rearrange("p f t -> p (f t)"),
                                             hbk[2 * (m % 2) + f][:], ACT.Silu).then_inc(h_made, 1)

            expert_pair(0)
            with act.Fori(1, NE // 2) as pair:
                expert_pair(pair)

            def tile_group(q):
                for i in range(NX):
                    n = q * NX + i
                    act.wait_ge(mixed, n + 1)
                    act.nop(nofuse=True)
                    act.dma_start(out[bass.ds(n * P, P), :], oo[:, i, :]).then_inc(o_out[i], 16)

            tile_group(0)
            with act.Fori(1, N // NX) as q:
                tile_group(q)

        @block.tensor
        def _(pe):
            pe.wait_ge(route_step, marks["chosen"])
            for k in range(2):
                nc.tensor.matmul(tb[k][:], keep["b16"][:, 3 + k, :], selb[:].rearrange("p t e -> p (t e)"),
                                 start=True, stop=True).then_inc(tri_done, 1)
            pe.wait_ge(w_in, 16)
            for gr in range(N // TG):
                pe.wait_ge(hot_made, gr + 1)
                pe.wait_ge(rows_made, gr + 1)
                pe.wait_ge(tiles_made, gr + 1)
                for t in range(TG):
                    for k in range(2):
                        mm = nc.tensor.matmul(hbk[0][:, 0:2 * NC], place_hot[:, gr % 2, t, k, :],
                                              tile_hot[:, gr % 2, t, k, 1:3, :].rearrange("p a c -> p (a c)"),
                                              start=(gr == 0 and t == 0 and k == 0),
                                              stop=(gr == N // TG - 1 and t == TG - 1 and k == 1))
                mm.then_inc(hot_used, 1)
            pe.wait_ge(route_step, marks["tokens"])

            def out_rows(pair, m):
                n = pair * (2 * NU) + m
                wait_for(pe, h_made, 2 * n + 2)
                if m % NU == 0:
                    pe.wait_ge(wd_in[m // NU], 16 * (pair + 1))
                wait_for(pe, y_copied, n - 1 if m >= 2 else pair * (2 * NU))
                for t in range(UN):
                    for f in range(4):
                        mm = nc.tensor.matmul(yb_[m % 2][:, t * D:(t + 1) * D], hT[:, m % 2, f, t * P:(t + 1) * P],
                                              wd_sb[:, m // NU, f, :], start=(f == 0), stop=(f == 3))
                mm.then_inc(y_done, 1)

            def turn_unit(pair, m):
                n = pair * (2 * NU) + m
                pe.wait_ge(xs_in[m % NXS], 32 * (pair * 2 + m // NXS + 1))
                wait_for(pe, xT_made, n - 1 if m >= 2 else pair * (2 * NU))
                for c in range(2):
                    for t in range(UN):
                        mm = nc.tensor.transpose(tb[m % 2][:, (c * UN + t) * P:(c * UN + t + 1) * P],
                                                 xs[:, m % NXS, t, c * P:(c + 1) * P], keep["ident"][:])
                mm.then_inc(x_turned, 1)

            def expert_pair(pair):
                turn_unit(pair, 0)
                for m in range(2 * NU):
                    n = pair * (2 * NU) + m
                    if m + 1 < 2 * NU:
                        turn_unit(pair, m + 1)
                    pe.wait_ge(xT_made, n + 1)
                    wait_for(pe, h_made, 2 * n - 2 if m >= 2 else pair * (4 * NU))
                    for f in range(4):
                        for c in range(2):
                            mm = nc.tensor.matmul(hbk[2 * (m % 2) + f // 2][:, (f % 2) * 256:(f % 2) * 256 + 256],
                                                  wg_sb[:, c, f * P:(f + 1) * P], xT[:, m % 2, c, :],
                                                  start=(c == 0), stop=(c == 1))
                        if f % 2:
                            mm.then_inc(hid_done, 1)
                    if m >= 1:
                        out_rows(pair, m - 1)
                out_rows(pair, 2 * NU - 1)

            expert_pair(0)
            with pe.Fori(1, NE // 2) as pair:
                expert_pair(pair)

        @block.sync
        def _(sp):
            sp.dma_start(wg_sb[:], wg).then_inc(w_in, 16)
            def expert_pair(pair):
                for m in range(2 * NU):
                    n = pair * (2 * NU) + m
                    if m % NU == 0:
                        e = m // NU
                        wait_for(sp, y_done, pair * (2 * NU))
                        sp.dma_start(wd_sb[:, e], wd[bass.ds(pair * 2 + e, 1)].rearrange("o p f d -> (o p) f d")
                                     ).then_inc(wd_in[e], 16)
                    if m >= 3:
                        store_y(sp, pair, m - 3)
                for m in range(2 * NU - 3, 2 * NU):
                    store_y(sp, pair, m)

            expert_pair(0)
            with sp.Fori(1, NE // 2) as pair:
                expert_pair(pair)
            for i in range(2):
                sp.wait_ge(y_out[i], 16 * (n_units // 2))
            def tile_group(q):
                for i in range(NX):
                    n = q * NX + i
                    wait_for(sp, mixed, n - NX + 1)
                    sp.nop(nofuse=True)
                    sp.dma_start(hh[:, i, :], scratch["h2"][bass.ds(n * P, P), :]).then_inc(hh_in[i], 16)

            tile_group(0)
            with sp.Fori(1, N // NX) as q:
                tile_group(q)
            for i in range(NX):
                sp.wait_ge(o_out[i], 16 * (N // NX))

        @block.gpsimd
        def _(pool):
            for gr in range(N // TG):
                hot = tile_hot[:, gr % 2]
                pool.wait_ge(tile_made, gr + 1)
                nc.gpsimd.tensor_tensor(hot[:, :, :, 2, :], hot[:, :, :, 0, :],
                                        c_rows[:, gr * TG:(gr + 1) * TG].unsqueeze(2).unsqueeze(3)
                                        .to_broadcast([P, TG, 2, NC]), ALU.mult).then_inc(tiles_made, 1)
            pool.wait_ge(route_step, marks["tokens"])
            def expert_pair(pair):
                for m in range(2 * NU):
                    n = pair * (2 * NU) + m
                    wait_for(pool, x_turned, n - NXS + 1 if m >= NXS else pair * (2 * NU))
                    pool.nop(nofuse=True)
                    nc.gpsimd.tensor_copy(xidx[:, m % NXS, :], token[:, bass.ds(n * UN, UN)]).then_inc(idx_set, 1)
                    pool.wait_ge(idx_set, n + 1)
                    pool.nop(nofuse=True)
                    for t in range(UN):
                        nc.gpsimd.indirect_dma_start(
                            xs[:, m % NXS, t, :], None, scratch["xn2"],
                            bass.IndirectOffsetOnAxis(xidx[:, m % NXS, t:t + 1].bitcast(U32), 0)
                            ).then_inc(xs_in[m % NXS], 16)

            expert_pair(0)
            with pool.Fori(1, NE // 2) as pair:
                expert_pair(pair)
            for i in range(2):
                pool.wait_ge(y_out[i], 16 * (n_units // 2))
            def tile_group(q):
                for i in range(NX):
                    n = q * NX + i
                    wait_for(pool, ya_in[i], 32 * q)
                    pool.nop(nofuse=True)
                    nc.gpsimd.tensor_copy(idx[:, i, :], slot[:, bass.ds(n, 1), :].rearrange("p t k -> p (t k)")
                                          ).then_inc(gidx_set, 1)
                for i in range(NX):
                    n = q * NX + i
                    pool.wait_ge(gidx_set, n + 1)
                    wait_for(pool, mixed, n - NX + 1)
                    pool.nop(nofuse=True)
                    for k, dst in enumerate((ya, yb)):
                        nc.gpsimd.indirect_dma_start(
                            dst[:, i, :], None, scratch["yslot"],
                            bass.IndirectOffsetOnAxis(idx[:, i, k:k + 1].bitcast(U32), 0)).then_inc(ya_in[i], 16)

            tile_group(0)
            with pool.Fori(1, N // NX) as q:
                tile_group(q)


def constants(np):
    f32 = np.float32
    n, f = np.arange(NFFT)[:, None], np.arange(NFREQ)[None, :]
    angle = 2.0 * np.pi * ((n * f) % NFFT) / NFFT
    dft = np.concatenate([np.cos(angle), -np.sin(angle)], 1).astype(f32)
    coord = np.clip((np.arange(T, dtype=f32) + f32(0.5)) * f32(NFRAME / T) - f32(0.5), f32(0), f32(NFRAME - 1))
    i0 = np.floor(coord).astype(np.int32)
    i1 = np.minimum(i0 + 1, NFRAME - 1)
    w = (coord - i0).astype(f32)
    interp = np.zeros((NFRAME + 1, T), f32)
    interp[i0, np.arange(T)] += f32(1) - w
    interp[i1, np.arange(T)] += w
    interp[NFRAME] = 1
    theta = f32(10000.0) ** (-np.arange(0, HD, 2, dtype=f32) / f32(HD))
    freqs = (np.arange(T, dtype=f32)[:, None] * theta[None, :]).T.astype(np.float64)
    rope = np.stack([np.repeat(np.cos(freqs), NH, 0), np.repeat(np.sin(freqs), NH, 0)], 1).astype(f32)
    ident = np.eye(P, dtype=f32)
    row, col = np.arange(P)[:, None], np.arange(P)[None, :]
    b16 = np.stack([ident, np.where(col <= row, 0, -1e30), np.where(col >= row, 0, -1e30),
                    (row <= col) * 1.0, np.ones((P, P))], 1).astype(f32)
    iota = np.zeros((P, V + 2 + NE + P), f32)
    iota[:, 0:V] = np.arange(V)
    iota[:, V] = np.arange(P)
    iota[:, V + 1] = NSLOT + np.arange(P)
    iota[:, V + 2:V + 2 + NE] = np.arange(NE) * CAP
    iota[:, V + 2 + NE:] = np.arange(P)
    return dict(c_dft=dft, c_interp=interp, c_rope=rope, c_ident=ident, c_mask=b16, c_iota=iota)


def kernel(**inputs):
    import numpy as np
    import concourse.bacc as bacc
    from concourse.bass_utils import run_bass_kernel_spmd

    i = {k: np.asarray(v) for k, v in inputs.items()}
    x = i["x"]
    c = np.ascontiguousarray
    padded = np.pad(x, ((0, 0), (NFFT // 2, NFFT // 2)), mode="reflect")
    frames = np.stack([padded[:, NFFT * t:NFFT * (t + 1)] for t in range(NFRAME)], 1)

    def cols(w):
        return c(w.T.reshape(2, P, -1).transpose(1, 0, 2))

    order = np.arange(D).reshape(NH, HALF, 2).transpose(2, 1, 0).reshape(-1)
    arrays = dict(
        x_frames=c(frames.reshape(BF, NFFT).T), x_tok=c(x), emb=c(i["L0_tok_emb_table"]),
        pw=c(i["L0_tok_proj_w"].reshape(DST, NFREQ, V).transpose(2, 1, 0)),
        pb=c(i["L0_tok_proj_b"][None]), window=c(i["L0_tok_window"][:, None]),
        wq=cols(i["L0_attn_Wq"][order]), bq=c(i["L0_attn_bq"][order].reshape(2, P).T),
        wk=cols(i["L0_attn_Wk"][order]), bk=c(i["L0_attn_bk"][order].reshape(2, P).T),
        wv=cols(i["L0_attn_Wv"]), bv=c(i["L0_attn_bv"][None]),
        wo=cols(i["L0_attn_Wo"]), bo=c(i["L0_attn_bo"][None]),
        wr=cols(i["L0_ffn_w_router"]), wg=cols(i["L0_ffn_w_gate"]),
        wd=c(i["L0_ffn_w_down"].transpose(0, 2, 1).reshape(NE, 4, P, D).transpose(0, 2, 1, 3)),
        **constants(np))
    nc = bacc.Bacc("TRN2", target_bir_lowering=False, num_devices=1)
    ins = [nc.dram_tensor(k, a.shape, mybir.dt.from_np(a.dtype), kind="ExternalInput").ap() for k, a in arrays.items()]
    out = nc.dram_tensor("out", (NTOK, D), F32, kind="ExternalOutput").ap()
    build(nc, ins, out)
    r = run_bass_kernel_spmd(nc, [arrays], core_ids=[0])
    return r.results[0]["out"].reshape(B, T, D)
```
